# Optimizing a Trainium2 kernel written in Bass

```python
import numpy as np
import jax
import jax.numpy as jnp

def _softmax(x, axis=-1):
    return jax.nn.softmax(x, axis=axis)

def _gelu(x):
    return jax.nn.gelu(x, approximate=True)

def _silu(x):
    return jax.nn.silu(x)

def _sigmoid(x):
    return jax.nn.sigmoid(x)

def _layernorm(x, axis=-1, eps=1e-05):
    m = jnp.mean(x, axis=axis, keepdims=True)
    v = jnp.var(x, axis=axis, keepdims=True)
    return (x - m) / jnp.sqrt(v + eps)

def _scatter_add(tgt, idx, src, axis=0):
    return tgt.at[idx].add(src)

def _segment_sum(src, seg, n):
    return jax.ops.segment_sum(src, seg, n)
kernel_name = 'mk_adj_ffn_d2_adj_r2_2a5f46'

def setup_inputs(seed: int=0):
    np.random.seed(seed)
    _w = jnp.asarray

    def _rec_inputs():
        import jax
        import jax.numpy as jnp
        _gk = jax.random.key(seed)
        x = -0.0002928 + 1 * jax.random.normal(jax.random.fold_in(_gk, 1), (2048, 256), jnp.float32)
        _a = jax.random.bernoulli(jax.random.fold_in(_gk, 2), 0.00390625, (2048, 2048))
        _a = jnp.logical_or(_a, jnp.swapaxes(_a, -1, -2))
        _a = jnp.logical_or(_a, jnp.eye(2048, dtype=bool))
        adj = _a.astype(jnp.int32)
        return (x, adj)
    x, adj = _rec_inputs()

    def _L0_gnn_setup():
        import jax, jax.numpy as jnp
        import numpy as np
        EPS = 1e-08
        key = jax.random.key(seed)
        k1, k2, k3 = jax.random.split(key, 3)
        N, IN_DIM, OUT_DIM = (4096, 256, 256)
        h = jax.random.normal(k1, (N, IN_DIM), dtype=jnp.float32)
        adj = jax.random.randint(k2, (N, N), 0, 2, dtype=jnp.int32)
        W = jax.random.normal(k3, (OUT_DIM, IN_DIM), dtype=jnp.float32) * (1.0 / np.sqrt(IN_DIM))
        return {'h': h, 'adj': adj, 'W': W}
    _L0_gnn_all = _L0_gnn_setup()
    _L0_gnn_in = {k: v for k, v in _L0_gnn_all.items() if k in ('W',)}
    del _L0_gnn_all

    def _L0_ffn_setup():
        import jax, jax.numpy as jnp
        import numpy as np
        H = 256
        FF = 4 * H
        E = 8
        K = 2
        B, S = (4, 2048)
        key = jax.random.key(seed)
        ks = jax.random.split(key, 4)
        s = 0.02
        return {'x': jax.random.normal(ks[0], (B, S, H), dtype=jnp.float32), 'Wg': jax.random.normal(ks[1], (H, E), dtype=jnp.float32) * s, 'bg': jnp.zeros((E,), dtype=jnp.float32), 'W1': jax.random.normal(ks[2], (E, H, FF), dtype=jnp.float32) * s, 'b1': jnp.zeros((E, FF), dtype=jnp.float32), 'W2': jax.random.normal(ks[3], (E, FF, H), dtype=jnp.float32) * s, 'b2': jnp.zeros((E, H), dtype=jnp.float32)}
    _L0_ffn_all = _L0_ffn_setup()
    _L0_ffn_in = {k: v for k, v in _L0_ffn_all.items() if k in ('Wg', 'bg', 'W1', 'b1', 'W2', 'b2')}
    del _L0_ffn_all

    def _L1_gnn_setup():
        import jax, jax.numpy as jnp
        import numpy as np
        key = jax.random.key(seed)
        kX, kA, k1, k2, k3, k4 = jax.random.split(key, 6)
        N, Cin, Cout = (4096, 256, 256)
        X = jax.random.normal(kX, (N, Cin), dtype=jnp.float32)
        A = jax.random.randint(kA, (N, N), 0, 2, dtype=jnp.int32)
        bound = 1.0 / np.sqrt(Cin)
        W_nb = jax.random.uniform(k1, (Cout, Cin), jnp.float32, -bound, bound)
        b_nb = jax.random.uniform(k2, (Cout,), jnp.float32, -bound, bound)
        W_line = jax.random.uniform(k3, (Cout, Cin), jnp.float32, -bound, bound)
        b_line = jax.random.uniform(k4, (Cout,), jnp.float32, -bound, bound)
        return {'X': X, 'A': A, 'W_nb': W_nb, 'b_nb': b_nb, 'W_line': W_line, 'b_line': b_line, 'neibor_num': 64}
    _L1_gnn_all = _L1_gnn_setup()
    _L1_gnn_in = {k: v for k, v in _L1_gnn_all.items() if k in ('W_nb', 'b_nb', 'W_line', 'b_line')}
    del _L1_gnn_all

    def _L1_ffn_setup():
        import jax, jax.numpy as jnp
        import numpy as np
        EPS = 1.1920929e-07
        NUM_HEADS = 8
        UP_HEAD = 64
        ROPE_HEAD = 32
        TOP_K = 4
        HIDDEN = 256
        INTER = 128
        DQ = 128
        DKV = 128
        N_EXPERTS = 16
        B, S = (2, 1024)

        def _rmsnorm(x, w):
            return x * jax.lax.rsqrt(jnp.mean(x * x, axis=-1, keepdims=True) + EPS) * w

        def _rope(x):
            D = x.shape[-1]
            s = x.shape[-2]
            inv_freq = 1.0 / 10000.0 ** (jnp.arange(0, D, 2, dtype=jnp.float32) / D)
            freqs = jnp.outer(jnp.arange(s, dtype=jnp.float32), inv_freq)
            emb = jnp.concatenate([freqs, freqs], axis=-1)
            cos, sin = (jnp.cos(emb), jnp.sin(emb))
            x1, x2 = (x[..., :D // 2], x[..., D // 2:])
            rot = jnp.concatenate([-x2, x1], axis=-1)
            return x * cos + rot * sin

        def _swiglu(x, wg, wu, wd):
            return jax.nn.silu(x @ wg) * (x @ wu) @ wd
        key = jax.random.key(seed)
        ks = jax.random.split(key, 18)
        sd = 0.02
        inp = {'hidden_states': jax.random.normal(ks[0], (B, S, HIDDEN), jnp.float32), 'w_in_norm': jnp.ones((HIDDEN,), jnp.float32), 'w_dq': sd * jax.random.normal(ks[1], (HIDDEN, DQ), jnp.float32), 'w_qnorm': jnp.ones((DQ,), jnp.float32), 'w_uq': sd * jax.random.normal(ks[2], (DQ, NUM_HEADS * (UP_HEAD + ROPE_HEAD)), jnp.float32), 'w_dkv': sd * jax.random.normal(ks[3], (HIDDEN, DKV + ROPE_HEAD), jnp.float32), 'w_kvnorm': jnp.ones((DKV,), jnp.float32), 'w_ukv': sd * jax.random.normal(ks[4], (DKV, NUM_HEADS * UP_HEAD * 2), jnp.float32), 'w_o': sd * jax.random.normal(ks[5], (NUM_HEADS * UP_HEAD, HIDDEN), jnp.float32), 'w_post_norm': jnp.ones((HIDDEN,), jnp.float32), 'w_gate': sd * jax.random.normal(ks[6], (HIDDEN, N_EXPERTS), jnp.float32), 'sh_wg': sd * jax.random.normal(ks[7], (HIDDEN, INTER), jnp.float32), 'sh_wu': sd * jax.random.normal(ks[8], (HIDDEN, INTER), jnp.float32), 'sh_wd': sd * jax.random.normal(ks[9], (INTER, HIDDEN), jnp.float32), 'r_wg': sd * jax.random.normal(ks[10], (N_EXPERTS, HIDDEN, INTER), jnp.float32), 'r_wu': sd * jax.random.normal(ks[11], (N_EXPERTS, HIDDEN, INTER), jnp.float32), 'r_wd': sd * jax.random.normal(ks[12], (N_EXPERTS, INTER, HIDDEN), jnp.float32)}
        return inp
    _L1_ffn_all = _L1_ffn_setup()
    _L1_ffn_in = {k: v for k, v in _L1_ffn_all.items() if k in ('w_in_norm', 'w_dq', 'w_qnorm', 'w_uq', 'w_dkv', 'w_kvnorm', 'w_ukv', 'w_o', 'w_post_norm', 'w_gate', 'sh_wg', 'sh_wu', 'sh_wd', 'r_wg', 'r_wu', 'r_wd')}
    del _L1_ffn_all
    return {'x': x, 'adj': adj, 'L0_gnn_W': _L0_gnn_in['W'], 'L0_ffn_Wg': _L0_ffn_in['Wg'], 'L0_ffn_bg': _L0_ffn_in['bg'], 'L0_ffn_W1': _L0_ffn_in['W1'], 'L0_ffn_b1': _L0_ffn_in['b1'], 'L0_ffn_W2': _L0_ffn_in['W2'], 'L0_ffn_b2': _L0_ffn_in['b2'], 'L1_gnn_W_nb': _L1_gnn_in['W_nb'], 'L1_gnn_b_nb': _L1_gnn_in['b_nb'], 'L1_gnn_W_line': _L1_gnn_in['W_line'], 'L1_gnn_b_line': _L1_gnn_in['b_line'], 'L1_ffn_w_in_norm': _L1_ffn_in['w_in_norm'], 'L1_ffn_w_dq': _L1_ffn_in['w_dq'], 'L1_ffn_w_qnorm': _L1_ffn_in['w_qnorm'], 'L1_ffn_w_uq': _L1_ffn_in['w_uq'], 'L1_ffn_w_dkv': _L1_ffn_in['w_dkv'], 'L1_ffn_w_kvnorm': _L1_ffn_in['w_kvnorm'], 'L1_ffn_w_ukv': _L1_ffn_in['w_ukv'], 'L1_ffn_w_o': _L1_ffn_in['w_o'], 'L1_ffn_w_post_norm': _L1_ffn_in['w_post_norm'], 'L1_ffn_w_gate': _L1_ffn_in['w_gate'], 'L1_ffn_sh_wg': _L1_ffn_in['sh_wg'], 'L1_ffn_sh_wu': _L1_ffn_in['sh_wu'], 'L1_ffn_sh_wd': _L1_ffn_in['sh_wd'], 'L1_ffn_r_wg': _L1_ffn_in['r_wg'], 'L1_ffn_r_wu': _L1_ffn_in['r_wu'], 'L1_ffn_r_wd': _L1_ffn_in['r_wd']}

def reference(x, adj, L0_gnn_W, L0_ffn_Wg, L0_ffn_bg, L0_ffn_W1, L0_ffn_b1, L0_ffn_W2, L0_ffn_b2, L1_gnn_W_nb, L1_gnn_b_nb, L1_gnn_W_line, L1_gnn_b_line, L1_ffn_w_in_norm, L1_ffn_w_dq, L1_ffn_w_qnorm, L1_ffn_w_uq, L1_ffn_w_dkv, L1_ffn_w_kvnorm, L1_ffn_w_ukv, L1_ffn_w_o, L1_ffn_w_post_norm, L1_ffn_w_gate, L1_ffn_sh_wg, L1_ffn_sh_wu, L1_ffn_sh_wd, L1_ffn_r_wg, L1_ffn_r_wu, L1_ffn_r_wd):
    import jax
    import jax.numpy as jnp

    def _L0_gnn_ref(h, adj, W):
        import jax, jax.numpy as jnp
        import numpy as np
        EPS = 1e-08
        Wh = h @ W.T
        N = Wh.shape[0]
        norms = jnp.linalg.norm(Wh, axis=1, keepdims=True)
        sim = Wh @ Wh.T / (norms * norms.T + EPS)
        mask = (adj > 0) | jnp.eye(N, dtype=bool)
        sim_masked = jnp.where(mask, sim, -jnp.inf)
        alpha = jax.nn.softmax(sim_masked, axis=1)
        return alpha @ Wh

    def _L0_ffn_ref(x, Wg, bg, W1, b1, W2, b2):
        import jax, jax.numpy as jnp
        import numpy as np
        H = 256
        FF = 4 * H
        E = 8
        K = 2
        B, S = (4, 2048)
        logits = x @ Wg + bg
        w, idx = jax.lax.top_k(logits, K)
        w = jax.nn.softmax(w, axis=-1)
        h = jax.nn.silu(jnp.einsum('bsh,ehf->ebsf', x, W1) + b1[:, None, None, :])
        y = jnp.einsum('ebsf,efh->ebsh', h, W2) + b2[:, None, None, :]
        comb = jnp.einsum('bske,bsk->ebs', jax.nn.one_hot(idx, E, dtype=x.dtype), w)
        return jnp.einsum('ebsh,ebs->bsh', y, comb)

    def _L1_gnn_ref(X, A, W_nb, b_nb, W_line, b_line, neibor_num):
        import jax, jax.numpy as jnp
        import numpy as np
        Ab = A > 0
        keep = Ab & (jnp.cumsum(Ab.astype(jnp.int32), axis=1) <= neibor_num)
        cnt = keep.sum(axis=1, keepdims=True).astype(X.dtype)
        nb_sum = keep.astype(X.dtype) @ X
        nb_mean = nb_sum / jnp.maximum(cnt, 1.0)
        xj = jax.nn.leaky_relu(nb_mean @ W_nb.T + b_nb)
        xi = jax.nn.leaky_relu(X @ W_line.T + b_line)
        return xi + jnp.where(cnt > 0, xj, jnp.zeros((), X.dtype))

    def _L1_ffn_ref(hidden_states, w_in_norm, w_dq, w_qnorm, w_uq, w_dkv, w_kvnorm, w_ukv, w_o, w_post_norm, w_gate, sh_wg, sh_wu, sh_wd, r_wg, r_wu, r_wd):
        import jax, jax.numpy as jnp
        import numpy as np
        EPS = 1.1920929e-07
        NUM_HEADS = 8
        UP_HEAD = 64
        ROPE_HEAD = 32
        TOP_K = 4
        HIDDEN = 256
        INTER = 128
        DQ = 128
        DKV = 128
        N_EXPERTS = 16
        B, S = (2, 1024)

        def _rmsnorm(x, w):
            return x * jax.lax.rsqrt(jnp.mean(x * x, axis=-1, keepdims=True) + EPS) * w

        def _rope(x):
            D = x.shape[-1]
            s = x.shape[-2]
            inv_freq = 1.0 / 10000.0 ** (jnp.arange(0, D, 2, dtype=jnp.float32) / D)
            freqs = jnp.outer(jnp.arange(s, dtype=jnp.float32), inv_freq)
            emb = jnp.concatenate([freqs, freqs], axis=-1)
            cos, sin = (jnp.cos(emb), jnp.sin(emb))
            x1, x2 = (x[..., :D // 2], x[..., D // 2:])
            rot = jnp.concatenate([-x2, x1], axis=-1)
            return x * cos + rot * sin

        def _swiglu(x, wg, wu, wd):
            return jax.nn.silu(x @ wg) * (x @ wu) @ wd
        b, s, h = hidden_states.shape
        residual = hidden_states
        x = _rmsnorm(hidden_states, w_in_norm)
        c_q = x @ w_dq
        qcr = _rmsnorm(c_q, w_qnorm) @ w_uq
        qcr = qcr.reshape(b, s, NUM_HEADS, UP_HEAD + ROPE_HEAD).transpose(0, 2, 1, 3)
        q_c, q_r = (qcr[..., :UP_HEAD], qcr[..., UP_HEAD:])
        ckv_kr = x @ w_dkv
        c_kv, k_r = (ckv_kr[..., :DKV], ckv_kr[..., DKV:])
        k_r = k_r[:, None, :, :]
        kv = (_rmsnorm(c_kv, w_kvnorm) @ w_ukv).reshape(b, s, NUM_HEADS, 2 * UP_HEAD).transpose(0, 2, 1, 3)
        k_c, v = (kv[..., :UP_HEAD], kv[..., UP_HEAD:])
        q = jnp.concatenate([q_c, _rope(q_r)], axis=-1)
        k = jnp.concatenate([k_c, jnp.broadcast_to(_rope(k_r), (b, NUM_HEADS, s, ROPE_HEAD))], axis=-1)
        scale = 1.0 / jnp.sqrt(jnp.float32(UP_HEAD + ROPE_HEAD))
        attn = jax.nn.softmax(jnp.einsum('bhqd,bhkd->bhqk', q, k) * scale, axis=-1)
        o = jnp.einsum('bhqk,bhkd->bhqd', attn, v).transpose(0, 2, 1, 3).reshape(b, s, NUM_HEADS * UP_HEAD)
        x = o @ w_o + residual
        residual = x
        x = _rmsnorm(x, w_post_norm)
        x2 = x.reshape(-1, h)
        shared = _swiglu(x2, sh_wg, sh_wu, sh_wd)
        scores = jax.nn.sigmoid(x2 @ w_gate)
        tw, ti = jax.lax.top_k(scores, TOP_K)
        tw = tw / jnp.sum(tw, axis=-1, keepdims=True)
        combine = jnp.sum(jax.nn.one_hot(ti, N_EXPERTS, dtype=x2.dtype) * tw[..., None], axis=1)
        g = jnp.einsum('th,ehi->tei', x2, r_wg)
        u = jnp.einsum('th,ehi->tei', x2, r_wu)
        y = jnp.einsum('tei,eih->teh', jax.nn.silu(g) * u, r_wd)
        routed = jnp.einsum('teh,te->th', y, combine)
        return (shared + routed).reshape(b, s, h) + residual
    x = x + _L0_gnn_ref(_layernorm(x, axis=-1), adj, L0_gnn_W)
    x = x + _L0_ffn_ref(_layernorm(x, axis=-1)[None], L0_ffn_Wg, L0_ffn_bg, L0_ffn_W1, L0_ffn_b1, L0_ffn_W2, L0_ffn_b2)[0]
    x = x + _L1_gnn_ref(_layernorm(x, axis=-1), adj, L1_gnn_W_nb, L1_gnn_b_nb, L1_gnn_W_line, L1_gnn_b_line, 64)
    x = x + _L1_ffn_ref(_layernorm(x, axis=-1)[None], L1_ffn_w_in_norm, L1_ffn_w_dq, L1_ffn_w_qnorm, L1_ffn_w_uq, L1_ffn_w_dkv, L1_ffn_w_kvnorm, L1_ffn_w_ukv, L1_ffn_w_o, L1_ffn_w_post_norm, L1_ffn_w_gate, L1_ffn_sh_wg, L1_ffn_sh_wu, L1_ffn_sh_wd, L1_ffn_r_wg, L1_ffn_r_wu, L1_ffn_r_wd)[0]
    return x

_drawn_inputs = setup_inputs


def setup_inputs(seed=0):
    import zlib

    import numpy as np

    out = dict(_drawn_inputs(seed))
    spreads = {'L0_ffn_bg': (0.0, 0.1),
     'L0_ffn_b1': (0.0, 0.326),
     'L0_ffn_b2': (0.0, 0.1),
     'L1_ffn_w_in_norm': (1.0, 0.6),
     'L1_ffn_w_qnorm': (1.0, 0.6),
     'L1_ffn_w_kvnorm': (1.0, 0.6),
     'L1_ffn_w_post_norm': (1.0, 0.6)}
    factors = {'L1_gnn_b_nb': 2.762,
     'L1_ffn_w_dq': 8.0,
     'L1_ffn_w_uq': 8.0,
     'L1_ffn_w_dkv': 8.0,
     'L1_ffn_w_ukv': 8.0,
     'L1_ffn_w_o': 8.0,
     'L1_ffn_w_gate': 8.0,
     'L1_ffn_sh_wg': 8.0,
     'L1_ffn_sh_wu': 8.0,
     'L1_ffn_sh_wd': 8.0,
     'L1_ffn_r_wg': 8.0,
     'L1_ffn_r_wu': 8.0,
     'L1_ffn_r_wd': 8.0}
    for name, (base, spread) in spreads.items():
        noise = np.random.default_rng([zlib.crc32(name.encode()), seed]).standard_normal(out[name].shape)
        drawn = base * np.exp(spread * noise) if base else spread * noise
        out[name] = jnp.asarray(drawn.astype(out[name].dtype))
    for name, factor in factors.items():
        out[name] = (out[name] * factor).astype(out[name].dtype)
    return out
```

```python
import concourse.bass as bass
from concourse import mybir
from contextlib import ExitStack

F32 = mybir.dt.float32
F16 = mybir.dt.float16
I32 = mybir.dt.int32
ALU = mybir.AluOpType
ACT = mybir.ActivationFunctionType
AXF = mybir.AxisListType.X
ds = bass.ds

P = 128
N = 2048
D = 256
T = N // P
KD = D // P
G = 4
GN = N // G
TG = GN // P
WS = 64.0
UNWS = 1.0 / WS
LN_EPS = 1e-5
RMS_EPS = 1.1920929e-07
SIM_EPS = 1e-8
NEIGHBORS = 64
L0_E, L0_F, L0_K = 8, 1024, 2
FC = L0_F // P
L1_E, L1_I, L1_K = 16, 128, 4
HEADS, UP, ROPE = 8, 64, 32
QK = UP + ROPE
HH = 4
DQ = DKV = 128
ATT_SCALE = 1.0 / float(QK) ** 0.5
BIG = 1.0e30


class Scope:

    used = []

    def __init__(self, nc, ctx, prefix):
        self.nc, self.ctx, self.prefix = nc, ctx, prefix

    def sb(self, name, shape, dt=F32):
        return self.ctx.enter_context(self.nc.sbuf_tensor(self.prefix + name, shape, dt))

    def ps(self, name, shape, dt=F32):
        return self.ctx.enter_context(self.nc.psum_tensor(self.prefix + name, shape, dt))

    def sem(self, name):
        handle = self.nc.alloc_semaphore(self.prefix + name)
        Scope.used.append(handle)
        return handle


def recycle_semaphores(nc):
    nc.clear_and_free_semaphores(Scope.used)
    nc.all_engine_barrier()
    Scope.used.clear()


class Chain:

    def __init__(self, eng, sem):
        self.eng, self.sem, self.n = eng, sem, 0

    def __call__(self, ins):
        ins.then_inc(self.sem, 1)
        self.n += 1
        self.eng.wait_ge(self.sem, self.n)


def each(eng, n, step, body):
    for i in range(step):
        body(i, i)
    if n > step:
        with eng.Fori(1, n // step) as j:
            for p in range(step):
                body(j * step + p, p)


def past(i, n):
    return not isinstance(i, int) or i >= n


def make_identities(nc, ident, ident16, ones):
    with ExitStack() as ctx:
        s = Scope(nc, ctx, "id_")
        cleared, done = s.sem("cleared"), s.sem("done")
        block = ctx.enter_context(nc.Block())

        @block.gpsimd
        def _(pool):
            pool.memset(ident[:, :], 0.0).then_inc(cleared, 1)
            pool.wait_ge(cleared, 1)
            pool.affine_select(out=ident[:, :], in_=ident[:, :], compare_op=ALU.not_equal, fill=1.0, base=0,
                               pattern=[[-1, P]], channel_multiplier=1).then_inc(done, 1)

        @block.vector
        def _(dve):
            dve.memset(ones[:, :], 1.0)
            dve.wait_ge(done, 1)
            dve.tensor_copy(ident16[:, :], ident[:, :])


def split_weights(nc, prefix, items):
    with ExitStack() as ctx:
        s = Scope(nc, ctx, prefix)
        raw = [s.sb(f"raw{i}", list(src.shape)) for i, (src, *_) in enumerate(items)]
        scale = [s.sb(f"scale{i}", list(sc.shape)) if sc is not None else None for i, (_, sc, _, _) in enumerate(items)]
        loaded = [s.sem(f"loaded{i}") for i in range(len(items))]
        scaled, hi_done, lo_done = s.sem("scaled"), s.sem("hi"), s.sem("lo")
        block = ctx.enter_context(nc.Block())

        @block.sync
        def _(sp):
            for i, (src, sc, _, _) in enumerate(items):
                sp.dma_start(raw[i][:, :, :], src).then_inc(loaded[i], 16)
                if sc is not None:
                    with nc.allow_non_contiguous_dma(reason="a short column of norm weights"):
                        sp.dma_start(scale[i][:, :], sc).then_inc(loaded[i], 16)

        @block.scalar
        def _(act):
            for i, (src, sc, hi, _) in enumerate(items):
                act.wait_ge(scaled, i + 1)
                act.activation(hi, raw[i][:, :, :], ACT.Copy, scale=WS).then_inc(hi_done, 1)

        @block.vector
        def _(dve):
            steps = s_steps = 0
            for i, (src, sc, hi, lo) in enumerate(items):
                dve.wait_ge(loaded[i], 16 if sc is None else 32)
                if sc is not None:
                    for k in range(src.shape[1]):
                        last = dve.tensor_scalar(raw[i][:, k, :], raw[i][:, k, :], scale[i][:, k:k + 1], None, ALU.mult)
                    last.then_inc(scaled, 1)
                else:
                    dve.engine_nop().then_inc(scaled, 1)
            for i, (src, sc, hi, lo) in enumerate(items):
                dve.wait_ge(scaled, i + 1)
                dve.wait_ge(hi_done, i + 1)
                dve.scalar_tensor_tensor(lo, raw[i][:, :, :], WS, hi, ALU.mult, ALU.subtract).then_inc(lo_done, 1)


def split_transposed_weights(nc, prefix, ident, items):
    with ExitStack() as ctx:
        s = Scope(nc, ctx, prefix)
        raw = [s.sb(f"raw{i}", [P, KD, D]) for i in range(len(items))]
        flipped = [s.ps(f"flipped{i}", [P, KD, D]) for i in range(len(items))]
        loaded = [s.sem(f"loaded{i}") for i in range(len(items))]
        turned, hi_done = s.sem("turned"), s.sem("hi")
        block = ctx.enter_context(nc.Block())

        @block.sync
        def _(sp):
            for i, (src, _, _) in enumerate(items):
                sp.dma_start(raw[i][:, :, :], src.rearrange("(o p) i -> p o i", p=P)).then_inc(loaded[i], 16)

        @block.tensor
        def _(pe):
            for i in range(len(items)):
                pe.wait_ge(loaded[i], 16)
                for o in range(KD):
                    for k in range(KD):
                        last = pe.transpose(flipped[i][:, k, o * P:(o + 1) * P], raw[i][:, o, k * P:(k + 1) * P], ident[:, :])
                last.then_inc(turned, 1)

        @block.scalar
        def _(act):
            for i, (_, hi, _) in enumerate(items):
                act.wait_ge(turned, i + 1)
                act.activation(hi, flipped[i][:, :, :], ACT.Copy, scale=WS).then_inc(hi_done, 1)

        @block.vector
        def _(dve):
            for i, (_, hi, lo) in enumerate(items):
                dve.wait_ge(hi_done, i + 1)
                dve.scalar_tensor_tensor(lo, flipped[i][:, :, :], WS, hi, ALU.mult, ALU.subtract)


def normalize_and_turn(nc, prefix, ident, src, width, kind, xT_hi, xT_lo, tok=None, tok_hi=None, tok_lo=None):
    chunks, NB = width // P, 4
    with ExitStack() as ctx:
        s = Scope(nc, ctx, prefix)
        stats = s.sb("stats", [P, T, 6])
        dif, mean, second, var = (s.sb(n, [P, T]) for n in ("dif", "mean", "second", "var"))
        std, rstd = s.sb("std", [P, T]), s.sb("rstd", [P, T])
        stage = [s.sb(f"stage{i}", [P, width]) for i in range(NB)]
        turned = [s.ps(f"turned{i}", [P, 512]) for i in range(NB)]
        stat_done, steps, var_done, std_done = s.sem("stat"), s.sem("steps"), s.sem("var"), s.sem("std")
        staged, flipped, hi_done, lo_done = s.sem("staged"), s.sem("flipped"), s.sem("hi"), s.sem("lo")
        copied, tok_hi_done = s.sem("copied"), s.sem("tok_hi")
        block = ctx.enter_context(nc.Block())
        keeps = tok is not None or tok_hi is not None

        @block.vector
        def _(dve):
            if tok_hi is not None:
                dve.memset(tok_hi[:, :, width:width + 1], 1.0)
            if kind:
                with dve.Fori(0, T) as t:
                    dve.bn_stats(stats[:, ds(t, 1), :], src[:, ds(t, 1), :]).then_inc(stat_done, 1)
                dve.wait_ge(stat_done, T)
                link = Chain(dve, steps)
                me, mo = stats[:, :, 1], stats[:, :, 4]
                link(dve.tensor_tensor(dif[:, :], me, mo, ALU.subtract))
                link(dve.tensor_tensor(mean[:, :], me, mo, ALU.add))
                link(dve.tensor_scalar(mean[:, :], mean[:, :], 0.5, None, ALU.mult))
                link(dve.tensor_tensor(second[:, :], stats[:, :, 2], stats[:, :, 5], ALU.add))
                link(dve.tensor_tensor(dif[:, :], dif[:, :], dif[:, :], ALU.mult))
                link(dve.tensor_scalar(second[:, :], second[:, :], 1.0 / width, LN_EPS if kind == "layer" else RMS_EPS,
                                       ALU.mult, ALU.add))
                link(dve.scalar_tensor_tensor(var[:, :], dif[:, :], 0.25, second[:, :], ALU.mult, ALU.add))
                if kind == "rms":
                    link(dve.tensor_tensor(dif[:, :], mean[:, :], mean[:, :], ALU.mult))
                    link(dve.tensor_tensor(var[:, :], var[:, :], dif[:, :], ALU.add))
                dve.engine_nop().then_inc(var_done, 1)
                dve.wait_ge(std_done, 1)
                link(dve.reciprocal(rstd[:, :], std[:, :]))
            if xT_hi is None:
                with dve.Fori(0, T) as t:
                    dve.tensor_scalar(tok[:, ds(t, 1), :], src[:, ds(t, 1), :], mean[:, ds(t, 1)], rstd[:, ds(t, 1)],
                                      ALU.subtract, ALU.mult)
                return

            def finish(t, p):
                dve.wait_ge(hi_done, t + 1)
                dve.tensor_tensor(xT_lo[:, :, ds(t * P, P)], turned[p][:, 0:width].rearrange("p (k n) -> p k n", k=chunks),
                                  xT_hi[:, :, ds(t * P, P)], ALU.subtract).then_inc(lo_done, 1)
                if tok_lo is not None:
                    dve.wait_ge(tok_hi_done, t + 1)
                    dve.tensor_tensor(tok_lo[:, ds(t, 1), 0:width], stage[p][:, :].unsqueeze(1),
                                      tok_hi[:, ds(t, 1), 0:width], ALU.subtract)

            def step(t, p):
                if past(t, NB):
                    dve.wait_ge(flipped, t - NB + 1)
                    if keeps:
                        dve.wait_ge(copied, t - NB + 1)
                out = stage[p][:, :].unsqueeze(1)
                if kind == "layer":
                    ins = dve.tensor_scalar(out, src[:, ds(t, 1), :], mean[:, ds(t, 1)], rstd[:, ds(t, 1)],
                                            ALU.subtract, ALU.mult)
                elif kind == "rms":
                    ins = dve.tensor_scalar(out, src[:, ds(t, 1), :], rstd[:, ds(t, 1)], None, ALU.mult)
                else:
                    ins = dve.tensor_copy(out, src[:, ds(t, 1), :])
                ins.then_inc(staged, 1)
                if past(t, 1):
                    finish(t - 1, (p - 1) % NB)

            each(dve, T, NB, step)
            finish(T - 1, (T - 1) % NB)

        @block.tensor
        def _(pe):
            if xT_hi is None:
                return

            def step(t, p):
                pe.wait_ge(staged, t + 1)
                if past(t, NB):
                    pe.wait_ge(lo_done, t - NB + 1)
                for k in range(chunks):
                    last = pe.transpose(turned[p][:, k * P:(k + 1) * P], stage[p][:, k * P:(k + 1) * P], ident[:, :])
                last.then_inc(flipped, 1)

            each(pe, T, NB, step)

        @block.scalar
        def _(act):
            if kind:
                act.wait_ge(var_done, 1)
                act.activation(std[:, :], var[:, :], ACT.Sqrt).then_inc(std_done, 1)
            if xT_hi is None:
                return

            def step(t, p):
                if keeps:
                    act.wait_ge(staged, t + 1)
                    if tok_hi is not None:
                        ins = act.activation(tok_hi[:, ds(t, 1), 0:width], stage[p][:, :].unsqueeze(1), ACT.Copy)
                        ins.then_inc(tok_hi_done, 1)
                    if tok is not None:
                        ins = act.activation(tok[:, ds(t, 1), 0:width], stage[p][:, :].unsqueeze(1), ACT.Copy)
                    else:
                        ins = act.nop()
                    ins.then_inc(copied, 1)
                act.wait_ge(flipped, t + 1)
                act.activation(xT_hi[:, :, ds(t * P, P)], turned[p][:, 0:width].rearrange("p (k n) -> p k n", k=chunks),
                               ACT.Copy).then_inc(hi_done, 1)

            each(act, T, NB, step)


def matmul3(pe, out, a_hi, a_lo, b_hi, b_lo, first, last):
    pe.matmul(out, lhsT=a_hi, rhs=b_hi, start=first, stop=False)
    pe.matmul(out, lhsT=a_hi, rhs=b_lo, start=False, stop=False)
    return pe.matmul(out, lhsT=a_lo, rhs=b_hi, start=False, stop=last)


def transpose_adjacency(nc, adj, ident16, adjT, diag):
    NB, RB = 2, 3
    with ExitStack() as ctx:
        s = Scope(nc, ctx, "adj_")
        raw = [s.sb(f"raw{i}", [P, N], I32) for i in range(RB)]
        mask = [s.sb(f"mask{i}", [P, N], F16) for i in range(NB)]
        flipped = [s.ps(f"flipped{i}", [P, T, P], F16) for i in range(NB)]
        loaded = [s.sem(f"loaded{i}") for i in range(RB)]
        masked, turned, act_out, dve_out, kept = (s.sem(n) for n in ("masked", "turned", "act_out", "dve_out", "kept"))
        half = T // 2
        block = ctx.enter_context(nc.Block())

        @block.sync
        def _(sp):
            for t in range(T):
                if t >= RB:
                    sp.wait_ge(masked, t - RB + 1)
                sp.dma_start(raw[t % RB][:, :], adj[t * P:(t + 1) * P, :]).then_inc(loaded[t % RB], 16)

        @block.vector
        def _(dve):
            def out(t, p):
                dve.wait_ge(turned, t + 1)
                dve.tensor_copy(adjT[:, half:T, ds(t * P, P)], flipped[p][:, half:T, :]).then_inc(dve_out, 1)

            for t in range(T):
                dve.wait_ge(loaded[t % RB], 16 * (t // RB + 1))
                if t >= NB:
                    dve.wait_ge(turned, t - NB + 1)
                dve.tensor_scalar(mask[t % NB][:, :], raw[t % RB][:, :], 0, None, ALU.is_gt).then_inc(masked, 1)
                if t >= 1:
                    out(t - 1, (t - 1) % NB)
            out(T - 1, (T - 1) % NB)
            dve.wait_ge(act_out, T)
            dve.wait_ge(dve_out, T)
            with dve.Fori(0, T) as c:
                dve.tensor_copy(diag[:, ds(c, 1), :], adjT[:, ds(c, 1), ds(c * P, P)]).then_inc(kept, 1)
            dve.wait_ge(kept, T)
            with dve.Fori(0, T) as c:
                dve.tensor_tensor(adjT[:, ds(c, 1), ds(c * P, P)], diag[:, ds(c, 1), :], ident16[:, :].unsqueeze(1), ALU.max)

        @block.tensor
        def _(pe):
            def step(t, p):
                pe.wait_ge(masked, t + 1)
                if past(t, NB):
                    pe.wait_ge(act_out, t - NB + 1)
                    pe.wait_ge(dve_out, t - NB + 1)
                for c in range(T):
                    last = pe.transpose(flipped[p][:, c, :], mask[p][:, c * P:(c + 1) * P], ident16[:, :])
                last.then_inc(turned, 1)

            each(pe, T, NB, step)

        @block.scalar
        def _(act):
            def step(t, p):
                act.wait_ge(turned, t + 1)
                act.activation(adjT[:, 0:half, ds(t * P, P)], flipped[p][:, 0:half, :], ACT.Copy).then_inc(act_out, 1)

            each(act, T, NB, step)


def project_gnn(nc, hT, WT, wh_hi, wh_lo, whT_hi, whT_lo, norm_row, norm_col, ones):
    NB = 2
    with ExitStack() as ctx:
        s = Scope(nc, ctx, "wh_")
        junk = [s.sb(f"junk{i}", [P, D]) for i in range(NB)]
        squares = s.sb("squares", [P, T])
        sqT = [[s.sb(f"sqT{b}{d}", [P, GN]) for d in range(KD)] for b in range(2)]
        prod = [s.ps(f"prod{i}", [P, 512]) for i in range(NB)]
        prodT = [s.ps(f"prodT{i}", [P, GN]) for i in range(KD)]
        sums = s.ps("sums", [P, GN])
        made, sq_done, hi_done, lo_done = (s.sem(n) for n in ("made", "sq", "hi", "lo"))
        madeT, sqT_done, hiT_done, loT_done, sums_done, sums_out = (
            s.sem(n) for n in ("madeT", "sqT", "hiT", "loT", "sums", "sums_out"))
        (hT_hi, hT_lo), (WT_hi, WT_lo) = hT, WT
        block = ctx.enter_context(nc.Block())

        @block.tensor
        def _(pe):
            def tile(t, p):
                if past(t, NB):
                    pe.wait_ge(lo_done, t - NB + 1)
                for k in range(KD):
                    last = matmul3(pe, prod[p][:, 0:D], hT_hi[:, k, ds(t * P, P)], hT_lo[:, k, ds(t * P, P)],
                                   WT_hi[:, k, :], WT_lo[:, k, :], k == 0, k == KD - 1)
                last.then_inc(made, 1)

            each(pe, T, NB, tile)
            for g in range(G):
                for d in range(KD):
                    if g:
                        pe.wait_ge(loT_done, KD * (g - 1) + d + 1)
                    for k in range(KD):
                        dd, gg = slice(d * P, (d + 1) * P), slice(g * GN, (g + 1) * GN)
                        last = matmul3(pe, prodT[d][:, :], WT_hi[:, k, dd], WT_lo[:, k, dd],
                                       hT_hi[:, k, gg], hT_lo[:, k, gg], k == 0, k == KD - 1)
                    last.then_inc(madeT, 1)
                if g:
                    pe.wait_ge(sums_out, g)
                for d in range(KD):
                    pe.wait_ge(sqT_done, KD * g + d + 1)
                    last = pe.matmul(sums[:, :], lhsT=ones[:, :], rhs=sqT[g % 2][d][:, :], start=d == 0, stop=d == KD - 1)
                last.then_inc(sums_done, 1)

        @block.scalar
        def _(act):
            def tile(t, p):
                act.wait_ge(made, t + 1)
                if past(t, NB):
                    act.wait_ge(sq_done, t - NB + 1)
                act.activation(junk[p][:, :], prod[p][:, 0:D], ACT.Square, scale=UNWS,
                               accum_out=squares[:, ds(t, 1)]).then_inc(sq_done, 1)
                act.activation(wh_hi[:, ds(t, 1), 0:D], prod[p][:, 0:D].unsqueeze(1), ACT.Copy, scale=UNWS).then_inc(hi_done, 1)

            each(act, T, NB, tile)
            for g in range(G):
                for d in range(KD):
                    act.wait_ge(madeT, KD * g + d + 1)
                    if g >= 2:
                        act.wait_ge(sums_done, g - 1)
                    act.activation(sqT[g % 2][d][:, :], prodT[d][:, :], ACT.Square, scale=UNWS).then_inc(sqT_done, 1)
                    act.activation(whT_hi[:, d, g * GN:(g + 1) * GN], prodT[d][:, :], ACT.Copy, scale=UNWS).then_inc(hiT_done, 1)
                act.wait_ge(sums_done, g + 1)
                act.activation(norm_row[:, g * GN:(g + 1) * GN], sums[:, :], ACT.Copy).then_inc(sums_out, 1)
            act.wait_ge(sums_out, G)
            act.activation(norm_row[:, :], norm_row[:, :], ACT.Sqrt)
            act.wait_ge(sq_done, T)
            act.activation(norm_col[:, :], squares[:, :], ACT.Sqrt)

        @block.vector
        def _(dve):
            dve.memset(wh_hi[:, :, D:D + 1], 1.0)

            def tile(t, p):
                dve.wait_ge(hi_done, t + 1)
                dve.scalar_tensor_tensor(wh_lo[:, ds(t, 1), :], prod[p][:, 0:D].unsqueeze(1), UNWS,
                                         wh_hi[:, ds(t, 1), 0:D], ALU.mult, ALU.subtract).then_inc(lo_done, 1)

            each(dve, T, NB, tile)
            for g in range(G):
                gg = slice(g * GN, (g + 1) * GN)
                for d in range(KD):
                    dve.wait_ge(hiT_done, KD * g + d + 1)
                    dve.scalar_tensor_tensor(whT_lo[:, d, gg], prodT[d][:, :], UNWS, whT_hi[:, d, gg],
                                             ALU.mult, ALU.subtract).then_inc(loT_done, 1)


def cosine_attention(nc, x, wh_hi, wh_lo, whT_hi, whT_lo, norm_row, norm_col, adjT):
    NB, LAG = 4, 3
    with ExitStack() as ctx:
        s = Scope(nc, ctx, "cos_")
        den = [s.sb(f"den{i}", [P, GN]) for i in range(2)]
        rec = [s.sb(f"rec{i}", [P, GN]) for i in range(2)]
        sim = [s.sb(f"sim{i}", [P, GN]) for i in range(2)]
        ex = [s.sb(f"ex{i}", [P, GN]) for i in range(2)]
        em = [s.sb(f"em{i}", [P, GN]) for i in range(2)]
        e_hi = [s.sb(f"e_hi{i}", [P, GN], F16) for i in range(NB)]
        e_lo = [s.sb(f"e_lo{i}", [P, GN], F16) for i in range(NB)]
        inv = s.sb("inv", [P, TG])
        dots = [s.ps(f"dots{i}", [P, GN]) for i in range(4)]
        out = [s.ps(f"out{i}", [P, 512]) for i in range(TG)]
        dots_done, den_done, rec_done, sim_done, ex_done, em_done, hi_done, lo_done, out_done, inv_done, added = (
            s.sem(n) for n in ("dots", "den", "rec", "sim", "ex", "em", "hi", "lo", "out", "inv", "added"))
        block = ctx.enter_context(nc.Block())

        @block.tensor
        def _(pe):
            def scores(g, c):
                u = T * g + c
                if past(u, 4):
                    pe.wait_ge(sim_done, u - 3)
                for k in range(KD):
                    cc, gg = slice(c * P, (c + 1) * P), ds(g * GN, GN)
                    last = matmul3(pe, dots[c % 4][:, :], whT_hi[:, k, cc], whT_lo[:, k, cc],
                                   whT_hi[:, k, gg], whT_lo[:, k, gg], k == 0, k == KD - 1)
                last.then_inc(dots_done, 1)

            def weigh(g, c):
                u = T * g + c
                pe.wait_ge(lo_done, u + 1)
                if c == 0 and past(g, 1):
                    pe.wait_ge(added, TG * g)
                for q in range(TG):
                    qq = slice(q * P, (q + 1) * P)
                    pe.matmul(out[q][:, 0:D + 1], lhsT=e_hi[c % NB][:, qq], rhs=wh_hi[:, c, 0:D + 1], start=c == 0, stop=False)
                    pe.matmul(out[q][:, 0:D], lhsT=e_hi[c % NB][:, qq], rhs=wh_lo[:, c, :], start=False, stop=False)
                    last = pe.matmul(out[q][:, 0:D + 1], lhsT=e_lo[c % NB][:, qq], rhs=wh_hi[:, c, 0:D + 1], start=False, stop=c == T - 1)
                last.then_inc(out_done, 1)

            def group(g, _):
                for c in range(T):
                    scores(g, c)
                    if c >= LAG:
                        weigh(g, c - LAG)
                    elif past(g, 1):
                        weigh(g - 1, T - LAG + c)

            each(pe, G, 1, group)
            for c in range(T - LAG, T):
                weigh(G - 1, c)

        @block.scalar
        def _(act):
            def expo(g, c):
                u = T * g + c
                act.wait_ge(sim_done, u + 1)
                if past(u, 2):
                    act.wait_ge(em_done, u - 1)
                act.activation(ex[c % 2][:, :], sim[c % 2][:, :], ACT.Exp).then_inc(ex_done, 1)

            def high(g, c):
                u = T * g + c
                act.wait_ge(em_done, u + 1)
                if past(u, NB):
                    act.wait_ge(out_done, u - NB + 1)
                act.activation(e_hi[c % NB][:, :], em[c % 2][:, :], ACT.Copy).then_inc(hi_done, 1)

            def group(g, _):
                for c in range(T):
                    expo(g, c)
                    if c >= 1:
                        high(g, c - 1)
                    elif past(g, 1):
                        high(g - 1, T - 1)

            each(act, G, 1, group)
            high(G - 1, T - 1)

        @block.vector
        def _(dve):
            def similarity(g, c):
                u, b = T * g + c, c % 2
                dve.tensor_scalar(den[b][:, :], norm_row[:, ds(g * GN, GN)], norm_col[:, c:c + 1], SIM_EPS,
                                  ALU.mult, ALU.add).then_inc(den_done, 1)
                dve.wait_ge(den_done, u + 1)
                dve.reciprocal(rec[b][:, :], den[b][:, :]).then_inc(rec_done, 1)
                dve.wait_ge(rec_done, u + 1)
                dve.wait_ge(dots_done, u + 1)
                if past(u, 2):
                    dve.wait_ge(ex_done, u - 1)
                dve.tensor_tensor(sim[b][:, :], dots[c % 4][:, :], rec[b][:, :], ALU.mult).then_inc(sim_done, 1)

            def mask(g, c):
                u, b = T * g + c, c % 2
                dve.wait_ge(ex_done, u + 1)
                if past(u, 2):
                    dve.wait_ge(lo_done, u - 1)
                dve.tensor_tensor(em[b][:, :], ex[b][:, :], adjT[:, c, ds(g * GN, GN)], ALU.mult).then_inc(em_done, 1)

            def low(g, c):
                u = T * g + c
                dve.wait_ge(hi_done, u + 1)
                dve.tensor_tensor(e_lo[c % NB][:, :], em[c % 2][:, :], e_hi[c % NB][:, :], ALU.subtract).then_inc(lo_done, 1)

            def add(g):
                dve.wait_ge(out_done, T * g + T)
                for q in range(TG):
                    dve.reciprocal(inv[:, q:q + 1], out[q][:, D:D + 1]).then_inc(inv_done, 1)
                for q in range(TG):
                    dve.wait_ge(inv_done, TG * g + q + 1)
                    dve.scalar_tensor_tensor(x[:, ds(TG * g + q, 1), :], out[q][:, 0:D].unsqueeze(1), inv[:, q:q + 1],
                                             x[:, ds(TG * g + q, 1), :], ALU.mult, ALU.add).then_inc(added, 1)

            def group(g, _):
                for c in range(T):
                    similarity(g, c)
                    if c >= 1:
                        mask(g, c - 1)
                    elif past(g, 1):
                        mask(g - 1, T - 1)
                    if c >= 2:
                        low(g, c - 2)
                    elif past(g, 1):
                        low(g - 1, T - 2 + c)
                    if c == 2 and past(g, 1):
                        add(g - 1)

            each(dve, G, 1, group)
            mask(G - 1, T - 1)
            low(G - 1, T - 2)
            low(G - 1, T - 1)
            add(G - 1)


def l0_gnn(nc, a, x, ident, ident16, ones, adjT, diag):
    with ExitStack() as ctx:
        s = Scope(nc, ctx, "g0_")
        hT = s.sb("hT_hi", [P, KD, N], F16), s.sb("hT_lo", [P, KD, N], F16)
        WT = s.sb("WT_hi", [P, KD, D], F16), s.sb("WT_lo", [P, KD, D], F16)
        wh_hi, wh_lo = s.sb("wh_hi", [P, T, D + 2], F16), s.sb("wh_lo", [P, T, D], F16)
        whT_hi, whT_lo = s.sb("whT_hi", [P, KD, N], F16), s.sb("whT_lo", [P, KD, N], F16)
        norm_row, norm_col = s.sb("norm_row", [P, N]), s.sb("norm_col", [P, T])
        split_transposed_weights(nc, "g0w_", ident, [(a["L0_gnn_W"], WT[0][:, :, :], WT[1][:, :, :])])
        normalize_and_turn(nc, "g0n_", ident, x, D, "layer", *hT)
        project_gnn(nc, hT, WT, wh_hi, wh_lo, whT_hi, whT_lo, norm_row, norm_col, ones)
        cosine_attention(nc, x, wh_hi, wh_lo, whT_hi, whT_lo, norm_row, norm_col, adjT)


def route(nc, prefix, ident, experts, top, hT, Wg, bias, comb, b2=None, x=None):
    with ExitStack() as ctx:
        s = Scope(nc, ctx, prefix)
        shape = [P, T, experts]
        rank_i, rank = s.sb("rank_i", [P, experts], I32), s.sb("rank", [P, experts])
        scores, work, same, chosen = (s.sb(n, shape) for n in ("scores", "work", "same", "chosen"))
        best, first, peak = s.sb("best", [P, T]), s.sb("first", [P, T]), s.sb("peak", [P, T])
        logits = s.ps("logits", shape)
        made, rank_done, loaded, steps, ready, squashed = (s.sem(n) for n in ("made", "rank", "loaded", "steps", "ready", "squashed"))
        (hT_hi, hT_lo), (Wg_hi, Wg_lo) = hT, Wg
        over = lambda row: row.unsqueeze(1).to_broadcast(shape)
        along = lambda col: col.unsqueeze(2).to_broadcast(shape)
        if bias is not None:
            bias_sb = s.sb("bias", [P, experts])
        if b2 is not None:
            b2_sb = s.sb("b2", [experts, D])
            combT = s.sb("combT", [experts, T, P])
            combT_ps = s.ps("combT_ps", [experts, T, P])
            extra = [s.ps(f"extra{i}", [P, D]) for i in range(2)]
            comb_done, combT_done, combT_out, extra_done, added = (
                s.sem(n) for n in ("comb", "combT", "combT_out", "extra", "added"))
        block = ctx.enter_context(nc.Block())

        @block.sync
        def _(sp):
            if bias is not None:
                sp.dma_start(bias_sb[:, :], bias.unsqueeze(0).to_broadcast([P, experts])).then_inc(loaded, 16)
            if b2 is not None:
                sp.dma_start(b2_sb[:, :], b2).then_inc(loaded, 16)

        @block.gpsimd
        def _(pool):
            pool.iota(rank_i[:, :], pattern=[[-1, experts]], base=experts, channel_multiplier=0).then_inc(rank_done, 1)

        @block.tensor
        def _(pe):
            def step(t, p):
                for k in range(KD):
                    last = matmul3(pe, logits[:, ds(t, 1), :], hT_hi[:, k, ds(t * P, P)], hT_lo[:, k, ds(t * P, P)],
                                   Wg_hi[:, k, :], Wg_lo[:, k, :], k == 0, k == KD - 1)
                last.then_inc(made, 1)

            each(pe, T, 1, step)
            if b2 is not None:
                pe.wait_ge(comb_done, 1)
                for t in range(T):
                    last = pe.transpose(combT_ps[:, t, :], comb[:, t, :], ident[:, :])
                last.then_inc(combT_done, 1)
                pe.wait_ge(combT_out, 1)
                for t in range(T):
                    if t >= 2:
                        pe.wait_ge(added, t - 1)
                    pe.matmul(extra[t % 2][:, :], lhsT=combT[:, t, :], rhs=b2_sb[:, :], start=True, stop=True).then_inc(extra_done, 1)

        @block.scalar
        def _(act):
            act.wait_ge(ready, 1)
            if bias is None:
                act.activation(scores[:, :, :], logits[:, :, :], ACT.Sigmoid, scale=UNWS).then_inc(squashed, 1)
            else:
                act.activation(same[:, :, :], work[:, :, :], ACT.Exp).then_inc(squashed, 1)
            if b2 is not None:
                act.wait_ge(combT_done, 1)
                act.activation(combT[:, :, :], combT_ps[:, :, :], ACT.Copy).then_inc(combT_out, 1)

        @block.vector
        def _(dve):
            link = Chain(dve, steps)
            dve.wait_ge(rank_done, 1)
            link(dve.tensor_copy(rank[:, :], rank_i[:, :]))
            dve.wait_ge(made, T)
            if bias is None:
                dve.engine_nop().then_inc(ready, 1)
                dve.wait_ge(squashed, 1)
            else:
                dve.wait_ge(loaded, 16 if b2 is None else 32)
                link(dve.scalar_tensor_tensor(scores[:, :, :], logits[:, :, :], UNWS, over(bias_sb[:, :]), ALU.mult, ALU.add))
            link(dve.tensor_copy(work[:, :, :], scores[:, :, :]))
            link(dve.memset(chosen[:, :, :], 0.0))
            for k in range(top):
                peak_k = first if k == 0 else peak
                link(dve.tensor_reduce(peak_k[:, :], work[:, :, :], AXF, ALU.max))
                link(dve.tensor_tensor(same[:, :, :], work[:, :, :], along(peak_k[:, :]), ALU.is_equal))
                link(dve.tensor_tensor(same[:, :, :], same[:, :, :], over(rank[:, :]), ALU.mult))
                link(dve.tensor_reduce(best[:, :], same[:, :, :], AXF, ALU.max))
                link(dve.tensor_tensor(same[:, :, :], over(rank[:, :]), along(best[:, :]), ALU.is_equal))
                link(dve.tensor_tensor(chosen[:, :, :], chosen[:, :, :], same[:, :, :], ALU.add))
                link(dve.scalar_tensor_tensor(work[:, :, :], same[:, :, :], -BIG, work[:, :, :], ALU.mult, ALU.add))
            if bias is None:
                link(dve.tensor_tensor(comb[:, :, :], scores[:, :, :], chosen[:, :, :], ALU.mult))
            else:
                link(dve.tensor_tensor(work[:, :, :], scores[:, :, :], along(first[:, :]), ALU.subtract))
                dve.engine_nop().then_inc(ready, 1)
                dve.wait_ge(squashed, 1)
                link(dve.tensor_tensor(comb[:, :, :], same[:, :, :], chosen[:, :, :], ALU.mult))
            link(dve.tensor_reduce(peak[:, :], comb[:, :, :], AXF, ALU.add))
            link(dve.reciprocal(best[:, :], peak[:, :]))
            link(dve.tensor_tensor(comb[:, :, :], comb[:, :, :], along(best[:, :]), ALU.mult))
            if b2 is not None:
                dve.engine_nop().then_inc(comb_done, 1)
                for t in range(T):
                    dve.wait_ge(extra_done, t + 1)
                    dve.tensor_tensor(x[:, t, :], extra[t % 2][:, :], x[:, t, :], ALU.add).then_inc(added, 1)
                dve.wait_ge(added, T)
                dve.wait_ge(combT_done, 1)
            dve.tensor_scalar(comb[:, :, :], comb[:, :, :], UNWS, None, ALU.mult)


def load_turned_bias(nc, prefix, ident, src, rows, biasT):
    with ExitStack() as ctx:
        s = Scope(nc, ctx, prefix)
        raw, flipped = s.sb("raw", [rows, P]), s.ps("flipped", [P, rows])
        loaded, turned = s.sem("loaded"), s.sem("turned")
        block = ctx.enter_context(nc.Block())

        @block.sync
        def _(sp):
            sp.dma_start(raw[:, :], src).then_inc(loaded, 16)

        @block.tensor
        def _(pe):
            pe.wait_ge(loaded, 16)
            pe.transpose(flipped[:, :], raw[:, :], ident[0:rows, 0:rows]).then_inc(turned, 1)

        @block.vector
        def _(dve):
            dve.wait_ge(turned, 1)
            dve.tensor_copy(biasT[:, :], flipped[:, :])


def l0_experts(nc, x, hT, W1, b1T, W2, comb):
    UB = 4
    with ExitStack() as ctx:
        s = Scope(nc, ctx, "e0_")
        raw1, raw2 = s.sb("raw1", [P, KD, L0_F]), s.sb("raw2", [P, FC, D])
        w1 = [(s.sb(f"w1_hi{i}", [P, KD, L0_F], F16), s.sb(f"w1_lo{i}", [P, KD, L0_F], F16)) for i in range(2)]
        w2 = [(s.sb(f"w2_hi{i}", [P, FC, D], F16), s.sb(f"w2_lo{i}", [P, FC, D], F16)) for i in range(2)]
        b1 = [s.sb(f"b1_{i}", [P, FC]) for i in range(2)]
        act_out = [s.sb(f"act{i}", [P, GN]) for i in range(UB)]
        hid = [(s.sb(f"hid_hi{i}", [P, FC, GN], F16), s.sb(f"hid_lo{i}", [P, FC, GN], F16)) for i in range(2)]
        up = [s.ps(f"up{i}", [P, GN]) for i in range(UB)]
        down = [s.ps(f"down{i}", [P, 512]) for i in range(TG)]
        loaded, w_hi, w_lo, up_done, act_done, hi_done, lo_done, down_done, added, b1_done = (
            s.sem(n) for n in ("loaded", "w_hi", "w_lo", "up", "act", "hi", "lo", "down", "added", "b1"))
        hT_hi, hT_lo = hT
        block = ctx.enter_context(nc.Block())

        @block.sync
        def _(sp):
            for e in range(L0_E):
                if e:
                    sp.wait_ge(w_lo, 2 * e)
                sp.dma_start(raw1[:, :, :], W1[e].rearrange("(k p) f -> p k f", p=P)).then_inc(loaded, 16)
                sp.dma_start(raw2[:, :, :], W2[e].rearrange("(k p) d -> p k d", p=P)).then_inc(loaded, 16)

        @block.tensor
        def _(pe):
            def project_up(e, g, p):
                u = G * e + g
                if g == 0:
                    pe.wait_ge(w_lo, 2 * e + 2)
                for f in range(FC):
                    n = FC * u + f
                    if past(n, UB):
                        pe.wait_ge(act_done, n - UB + 1)
                    ff, gg = slice(f * P, (f + 1) * P), slice(g * GN, (g + 1) * GN)
                    for k in range(KD):
                        last = matmul3(pe, up[f % UB][:, :], w1[p][0][:, k, ff], w1[p][1][:, k, ff],
                                       hT_hi[:, k, gg], hT_lo[:, k, gg], k == 0, k == KD - 1)
                    last.then_inc(up_done, 1)

            def project_down(e, g, p):
                u = G * e + g
                pe.wait_ge(lo_done, FC * u + FC)
                for q in range(TG):
                    if past(u, 1):
                        pe.wait_ge(added, TG * (u - 1) + q + 1)
                    qq = slice(q * P, (q + 1) * P)
                    for f in range(FC):
                        last = matmul3(pe, down[q][:, 0:D], hid[g % 2][0][:, f, qq], hid[g % 2][1][:, f, qq],
                                       w2[p][0][:, f, :], w2[p][1][:, f, :], f == 0, f == FC - 1)
                    last.then_inc(down_done, 1)

            def expert(e, p):
                for g in range(G):
                    project_up(e, g, p)
                    if g:
                        project_down(e, g - 1, p)
                    elif past(e, 1):
                        project_down(e - 1, G - 1, 1 - p)

            each(pe, L0_E, 2, expert)
            project_down(L0_E - 1, G - 1, (L0_E - 1) % 2)

        @block.scalar
        def _(act):
            def expert(e, p):
                act.wait_ge(loaded, 32 * e + 32)
                if past(e, 2):
                    act.wait_ge(down_done, TG * G * (e - 1))
                act.activation(w1[p][0][:, :, :], raw1[:, :, :], ACT.Copy, scale=WS).then_inc(w_hi, 1)
                act.activation(w2[p][0][:, :, :], raw2[:, :, :], ACT.Copy, scale=WS).then_inc(w_hi, 1)
                act.wait_ge(b1_done, e + 1)
                for g in range(G):
                    for f in range(FC):
                        n = FC * (G * e + g) + f
                        act.wait_ge(up_done, n + 1)
                        if past(n, UB):
                            act.wait_ge(lo_done, n - UB + 1)
                        act.activation(act_out[f % UB][:, :], up[f % UB][:, :], ACT.Silu, bias=b1[p][:, f:f + 1],
                                       scale=UNWS).then_inc(act_done, 1)

            each(act, L0_E, 2, expert)

        @block.vector
        def _(dve):
            def hidden(e, g):
                u = G * e + g
                if past(u, 2):
                    dve.wait_ge(down_done, TG * (u - 1))
                for f in range(FC):
                    n = FC * u + f
                    dve.wait_ge(act_done, n + 1)
                    dve.tensor_copy(hid[g % 2][0][:, f, :], act_out[f % UB][:, :]).then_inc(hi_done, 1)
                    dve.wait_ge(hi_done, n + 1)
                    dve.tensor_tensor(hid[g % 2][1][:, f, :], act_out[f % UB][:, :], hid[g % 2][0][:, f, :],
                                      ALU.subtract).then_inc(lo_done, 1)

            def add(e, g):
                u = G * e + g
                for q in range(TG):
                    n = TG * u + q
                    dve.wait_ge(down_done, n + 1)
                    if past(u, G):
                        dve.wait_ge(added, n - TG * G + 1)
                    dve.scalar_tensor_tensor(x[:, TG * g + q, :], down[q][:, 0:D], comb[:, TG * g + q, ds(e, 1)],
                                             x[:, TG * g + q, :], ALU.mult, ALU.add).then_inc(added, 1)

            def expert(e, p):
                dve.tensor_scalar(b1[p][:, :], b1T[:, ds(FC * e, FC)], 1.0, None, ALU.mult).then_inc(b1_done, 1)
                dve.wait_ge(w_hi, 2 * e + 2)
                dve.scalar_tensor_tensor(w1[p][1][:, :, :], raw1[:, :, :], WS, w1[p][0][:, :, :], ALU.mult,
                                         ALU.subtract).then_inc(w_lo, 1)
                dve.scalar_tensor_tensor(w2[p][1][:, :, :], raw2[:, :, :], WS, w2[p][0][:, :, :], ALU.mult,
                                         ALU.subtract).then_inc(w_lo, 1)
                for g in range(G):
                    hidden(e, g)
                    if g:
                        add(e, g - 1)
                    elif past(e, 1):
                        add(e - 1, G - 1)

            each(dve, L0_E, 2, expert)
            add(L0_E - 1, G - 1)


def l0_ffn(nc, a, x, ident):
    with ExitStack() as ctx:
        s = Scope(nc, ctx, "f0_")
        hT = s.sb("hT_hi", [P, KD, N], F16), s.sb("hT_lo", [P, KD, N], F16)
        Wg = s.sb("Wg_hi", [P, KD, L0_E], F16), s.sb("Wg_lo", [P, KD, L0_E], F16)
        comb, b1T = s.sb("comb", [P, T, L0_E]), s.sb("b1T", [P, L0_E * FC])
        load_turned_bias(nc, "f0b_", ident, a["L0_ffn_b1"].rearrange("e (f p) -> (e f) p", p=P), L0_E * FC, b1T)
        split_weights(nc, "f0w_", [(a["L0_ffn_Wg"].rearrange("(k p) e -> p k e", p=P), None, Wg[0][:, :, :], Wg[1][:, :, :])])
        normalize_and_turn(nc, "f0n_", ident, x, D, "layer", *hT)
        route(nc, "f0r_", ident, L0_E, L0_K, hT, Wg, a["L0_ffn_bg"], comb, a["L0_ffn_b2"], x)
        l0_experts(nc, x, hT, a["L0_ffn_W1"], b1T, a["L0_ffn_W2"], comb)


def keep_first_neighbors(nc, adjT, diag, upper, ones16):
    with ExitStack() as ctx:
        s = Scope(nc, ctx, "keep_")
        before = [s.sb(f"before{i}", [P, N], F16) for i in range(2)]
        count = [s.ps(f"count{i}", [P, GN]) for i in range(8)]
        restored, cleared, summed, counted, kept = (s.sem(n) for n in ("restored", "cleared", "summed", "counted", "kept"))
        block = ctx.enter_context(nc.Block())

        @block.tensor
        def _(pe):
            def chunk(c, p):
                if not past(c, 1):
                    pe.wait_ge(restored, T)
                    pe.wait_ge(cleared, 1)
                else:
                    pe.wait_ge(summed, c)
                for g in range(G):
                    n = G * c + g
                    if past(n, 8):
                        pe.wait_ge(kept, n - 7)
                    gg = slice(g * GN, (g + 1) * GN)
                    b = G * (p % 2) + g
                    pe.matmul(count[b][:, :], lhsT=upper[:, :], rhs=adjT[:, ds(c, 1), gg], start=True, stop=False)
                    pe.matmul(count[b][:, :], lhsT=ones16[:, :], rhs=before[p % 2][:, gg], start=False, stop=True).then_inc(counted, 1)

            each(pe, T, 2, chunk)

        @block.vector
        def _(dve):
            with dve.Fori(0, T) as c:
                dve.tensor_copy(adjT[:, ds(c, 1), ds(c * P, P)], diag[:, ds(c, 1), :]).then_inc(restored, 1)
            dve.wait_ge(restored, T)
            dve.memset(before[0][:, :], 0.0).then_inc(cleared, 1)
            dve.wait_ge(cleared, 1)

            def chunk(c, p):
                if past(c, 1):
                    dve.wait_ge(summed, c)
                    dve.wait_ge(counted, G * c)
                dve.tensor_tensor(before[1 - p % 2][:, :].unsqueeze(1), before[p % 2][:, :].unsqueeze(1), adjT[:, ds(c, 1), :],
                                  ALU.add).then_inc(summed, 1)
                dve.wait_ge(summed, c + 1)
                for g in range(G):
                    b, gg = G * (p % 2) + g, slice(g * GN, (g + 1) * GN)
                    dve.wait_ge(counted, G * c + g + 1)
                    dve.scalar_tensor_tensor(adjT[:, ds(c, 1), gg], count[b][:, :].unsqueeze(1), float(NEIGHBORS),
                                             adjT[:, ds(c, 1), gg], ALU.is_le, ALU.mult).then_inc(kept, 1)

            each(dve, T, 2, chunk)


def neighbor_mean(nc, keep, xn_hi, xn_lo, mean, has):
    NB = 4
    with ExitStack() as ctx:
        s = Scope(nc, ctx, "mean_")
        inv, cnt = [s.sb(f"inv{i}", [P, 1]) for i in range(NB)], [s.sb(f"cnt{i}", [P, 1]) for i in range(NB)]
        total = [s.ps(f"total{i}", [P, 512]) for i in range(NB)]
        summed, counted, inverted, used = (s.sem(n) for n in ("summed", "counted", "inverted", "used"))
        block = ctx.enter_context(nc.Block())

        @block.tensor
        def _(pe):
            def tile(t, p):
                if past(t, NB):
                    pe.wait_ge(used, t - NB + 1)
                for c in range(T):
                    pe.matmul(total[p][:, 0:D + 1], lhsT=keep[:, c, ds(t * P, P)], rhs=xn_hi[:, c, 0:D + 1], start=c == 0, stop=False)
                    last = pe.matmul(total[p][:, 0:D], lhsT=keep[:, c, ds(t * P, P)], rhs=xn_lo[:, c, :], start=False, stop=c == T - 1)
                last.then_inc(summed, 1)

            each(pe, T, NB, tile)

        @block.vector
        def _(dve):
            def tile(t, p):
                if past(t, NB):
                    dve.wait_ge(used, t - NB + 1)
                dve.wait_ge(summed, t + 1)
                dve.tensor_scalar(has[:, ds(t, 1)], total[p][:, D:D + 1], 0.0, None, ALU.is_gt)
                dve.tensor_scalar(cnt[p][:, :], total[p][:, D:D + 1], 1.0, None, ALU.max).then_inc(counted, 1)
                dve.wait_ge(counted, t + 1)
                dve.reciprocal(inv[p][:, :], cnt[p][:, :]).then_inc(inverted, 1)
                dve.wait_ge(inverted, t + 1)
                dve.tensor_scalar(mean[:, ds(t, 1), :], total[p][:, 0:D].unsqueeze(1), inv[p][:, :], None, ALU.mult).then_inc(used, 1)

            each(dve, T, NB, tile)


def gnn_outputs(nc, a, x, xnT, meanT, W_line, W_nb, has):
    NB = 4
    with ExitStack() as ctx:
        s = Scope(nc, ctx, "go_")
        biases = [s.sb(n, [P, D]) for n in ("b_line", "b_nb")]
        val = [[s.sb(f"val{j}{i}", [P, D]) for i in range(NB)] for j in range(2)]
        leaky = [[s.sb(f"leaky{j}{i}", [P, D]) for i in range(NB)] for j in range(2)]
        prod = [[s.ps(f"prod{j}{i}", [P, 512]) for i in range(NB)] for j in range(2)]
        loaded, made, biased, bent, added = (s.sem(n) for n in ("loaded", "made", "biased", "bent", "added"))
        block = ctx.enter_context(nc.Block())

        @block.sync
        def _(sp):
            for b, src in zip(biases, (a["L1_gnn_b_line"], a["L1_gnn_b_nb"])):
                sp.dma_start(b[:, :], src.unsqueeze(0).to_broadcast([P, D])).then_inc(loaded, 16)

        @block.tensor
        def _(pe):
            def tile(t, p):
                for j, (hT, W) in enumerate(((xnT, W_line), (meanT, W_nb))):
                    if past(t, NB):
                        pe.wait_ge(biased, 2 * (t - NB) + j + 1)
                    for k in range(KD):
                        last = matmul3(pe, prod[j][p][:, 0:D], hT[0][:, k, ds(t * P, P)], hT[1][:, k, ds(t * P, P)],
                                       W[0][:, k, :], W[1][:, k, :], k == 0, k == KD - 1)
                    last.then_inc(made, 1)

            each(pe, T, NB, tile)

        @block.vector
        def _(dve):
            dve.wait_ge(loaded, 32)

            def tile(t, p):
                for j in range(2):
                    dve.wait_ge(made, 2 * t + j + 1)
                    dve.scalar_tensor_tensor(val[j][p][:, :], prod[j][p][:, 0:D], UNWS, biases[j][:, :], ALU.mult,
                                             ALU.add).then_inc(biased, 1)
                for j in range(2):
                    dve.wait_ge(biased, 2 * t + j + 1)
                    dve.scalar_tensor_tensor(leaky[j][p][:, :], val[j][p][:, :], 0.01, val[j][p][:, :], ALU.mult,
                                             ALU.max).then_inc(bent, 1)
                xt = x[:, ds(t, 1), :]
                dve.wait_ge(bent, 2 * t + 1)
                dve.tensor_tensor(xt, leaky[0][p][:, :].unsqueeze(1), xt, ALU.add).then_inc(added, 1)
                dve.wait_ge(bent, 2 * t + 2)
                dve.wait_ge(added, 2 * t + 1)
                dve.scalar_tensor_tensor(xt, leaky[1][p][:, :].unsqueeze(1), has[:, ds(t, 1)], xt, ALU.mult, ALU.add).then_inc(added, 1)

            each(dve, T, NB, tile)


def make_triangle(nc, upper, ones16):
    with ExitStack() as ctx:
        s = Scope(nc, ctx, "tri_")
        filled = s.sem("filled")
        block = ctx.enter_context(nc.Block())

        @block.gpsimd
        def _(pool):
            pool.memset(ones16[:, :], 1.0)
            pool.memset(upper[:, :], 1.0).then_inc(filled, 1)
            pool.wait_ge(filled, 1)
            pool.affine_select(out=upper[:, :], in_=upper[:, :], compare_op=ALU.is_ge, fill=0.0, base=0,
                               pattern=[[1, P]], channel_multiplier=-1)


def l1_gnn(nc, a, x, ident, adjT, diag):
    with ExitStack() as ctx:
        s = Scope(nc, ctx, "g1_")
        xnT = s.sb("xnT_hi", [P, KD, N], F16), s.sb("xnT_lo", [P, KD, N], F16)
        meanT = s.sb("meanT_hi", [P, KD, N], F16), s.sb("meanT_lo", [P, KD, N], F16)
        xn_hi, xn_lo = s.sb("xn_hi", [P, T, D + 2], F16), s.sb("xn_lo", [P, T, D], F16)
        mean, has = s.sb("mean", [P, T, D]), s.sb("has", [P, T])
        W_line = s.sb("W_line_hi", [P, KD, D], F16), s.sb("W_line_lo", [P, KD, D], F16)
        W_nb = s.sb("W_nb_hi", [P, KD, D], F16), s.sb("W_nb_lo", [P, KD, D], F16)
        upper, ones16 = s.sb("upper", [P, P], F16), s.sb("ones16", [P, P], F16)
        make_triangle(nc, upper, ones16)
        split_transposed_weights(nc, "g1w_", ident, [(a["L1_gnn_W_line"], W_line[0][:, :, :], W_line[1][:, :, :]),
                                                     (a["L1_gnn_W_nb"], W_nb[0][:, :, :], W_nb[1][:, :, :])])
        normalize_and_turn(nc, "g1n_", ident, x, D, "layer", *xnT, tok_hi=xn_hi, tok_lo=xn_lo)
        keep_first_neighbors(nc, adjT, diag, upper, ones16)
        neighbor_mean(nc, adjT, xn_hi, xn_lo, mean, has)
        normalize_and_turn(nc, "g1m_", ident, mean, D, None, *meanT)
        gnn_outputs(nc, a, x, xnT, meanT, W_line, W_nb, has)


def latent_project(nc, a, xT, W_hi, W_lo, c_q, c_kv, k_rope, cos, sin):
    NB = 4
    with ExitStack() as ctx:
        s = Scope(nc, ctx, "lat_")
        raw_k = s.sb("raw_k", [P, T, ROPE])
        turned = s.sb("turned", [P, T, ROPE])
        prod = [s.ps(f"prod{i}", [P, 512]) for i in range(NB)]
        made, out_done, loaded, parts = (s.sem(n) for n in ("made", "out", "loaded", "parts"))
        block = ctx.enter_context(nc.Block())
        H = ROPE // 2

        @block.sync
        def _(sp):
            sp.dma_start(cos[:, :, :], a["rope_cos"].rearrange("(t p) d -> p t d", p=P)).then_inc(loaded, 16)
            sp.dma_start(sin[:, :, :], a["rope_sin"].rearrange("(t p) d -> p t d", p=P)).then_inc(loaded, 16)

        @block.tensor
        def _(pe):
            def tile(t, p):
                if past(t, NB):
                    pe.wait_ge(out_done, 3 * (t - NB) + 3)
                for k in range(KD):
                    last = matmul3(pe, prod[p][:, 0:DQ + DKV + ROPE], xT[0][:, k, ds(t * P, P)], xT[1][:, k, ds(t * P, P)],
                                   W_hi[:, k, :], W_lo[:, k, :], k == 0, k == KD - 1)
                last.then_inc(made, 1)

            each(pe, T, NB, tile)

        @block.scalar
        def _(act):
            def tile(t, p):
                act.wait_ge(made, t + 1)
                for dst, at, w in ((c_q, 0, DQ), (c_kv, DQ, DKV), (raw_k, DQ + DKV, ROPE)):
                    act.activation(dst[:, ds(t, 1), :], prod[p][:, at:at + w].unsqueeze(1), ACT.Copy, scale=UNWS).then_inc(out_done, 1)

            each(act, T, NB, tile)

        @block.vector
        def _(dve):
            dve.wait_ge(loaded, 32)
            dve.wait_ge(out_done, 3 * T)
            dve.tensor_tensor(turned[:, :, 0:H], raw_k[:, :, H:ROPE], sin[:, :, 0:H], ALU.mult).then_inc(parts, 1)
            dve.tensor_tensor(turned[:, :, H:ROPE], raw_k[:, :, 0:H], sin[:, :, H:ROPE], ALU.mult).then_inc(parts, 1)
            dve.tensor_tensor(k_rope[:, :, :], raw_k[:, :, :], cos[:, :, :], ALU.mult).then_inc(parts, 1)
            dve.wait_ge(parts, 3)
            dve.tensor_tensor(k_rope[:, :, :], k_rope[:, :, :], turned[:, :, :], ALU.add)


def queries_keys_values(nc, prefix, ident, cqT, ckvT, W_uq, W_ukv, k_rope, cos, sin, qT, kT, V):
    H = ROPE // 2
    with ExitStack() as ctx:
        s = Scope(nc, ctx, prefix)
        tok = [[s.sb(f"tok{j}{i}", [P, HH, QK]) for i in range(2)] for j in range(2)]
        kept = [s.sb(f"kept{i}", [P, HH, ROPE]) for i in range(2)]
        swapped = [s.sb(f"swapped{i}", [P, HH, ROPE]) for i in range(2)]
        q_ps = [s.ps(f"q{i}", [P, HH, P]) for i in range(2)]
        kv_ps = [s.ps(f"kv{i}", [P, HH, 2 * UP]) for i in range(2)]
        flipped = [[s.ps(f"flipped{j}{i}", [P, HH, P]) for i in range(2)] for j in range(2)]
        q_made, kv_made, q_out, kv_out, v_lo, rot, rotated, k_ready, turned, hi_done, lo_done = (
            s.sem(n) for n in ("q_made", "kv_made", "q_out", "kv_out", "v_lo", "rot", "rotated", "k_ready",
                               "turned", "hi", "lo"))
        block = ctx.enter_context(nc.Block())

        @block.tensor
        def _(pe):
            def turn(t, p):
                pe.wait_ge(rotated, t + 1)
                pe.wait_ge(k_ready, t + 1)
                pe.wait_ge(kv_out, t + 1)
                for j in range(2):
                    if past(t, 2):
                        pe.wait_ge(lo_done, 2 * (t - 2) + j + 1)
                    for h in range(HH):
                        last = pe.transpose(flipped[j][p][0:QK, h, :], tok[j][p][:, h, :], ident[:, :])
                    last.then_inc(turned, 1)

            def tile(t, p):
                p = p % 2
                if past(t, 2):
                    pe.wait_ge(q_out, t - 1)
                matmul3(pe, q_ps[p][:, :, :].rearrange("p h d -> p (h d)")[:, 0:HH * QK], cqT[0][:, 0, ds(t * P, P)],
                        cqT[1][:, 0, ds(t * P, P)], W_uq[0], W_uq[1], True, True).then_inc(q_made, 1)
                if past(t, 2):
                    pe.wait_ge(kv_out, t - 1)
                    pe.wait_ge(v_lo, t - 1)
                matmul3(pe, kv_ps[p][:, :, :], ckvT[0][:, 0, ds(t * P, P)], ckvT[1][:, 0, ds(t * P, P)],
                        W_ukv[0], W_ukv[1], True, True).then_inc(kv_made, 1)
                if past(t, 1):
                    turn(t - 1, 1 - p)

            each(pe, T, 4, tile)
            turn(T - 1, (T - 1) % 2)

        @block.scalar
        def _(act):
            def high(t, p):
                for j, dst in enumerate((qT, kT)):
                    act.wait_ge(turned, 2 * t + j + 1)
                    act.activation(dst[0][0:QK, :, ds(t * P, P)], flipped[j][p][0:QK, :, :], ACT.Copy).then_inc(hi_done, 1)

            def tile(t, p):
                p = p % 2
                act.wait_ge(q_made, t + 1)
                if past(t, 2):
                    act.wait_ge(turned, 2 * (t - 2) + 2)
                act.activation(tok[0][p][:, :, :].rearrange("p h d -> p (h d)"),
                               q_ps[p][:, :, :].rearrange("p h d -> p (h d)")[:, 0:HH * QK], ACT.Copy,
                               scale=UNWS * ATT_SCALE).then_inc(q_out, 1)
                act.wait_ge(kv_made, t + 1)
                act.activation(V[:, ds(t, 1), :, UP:2 * UP], kv_ps[p][:, :, UP:2 * UP].unsqueeze(1), ACT.Copy, scale=UNWS)
                act.activation(tok[1][p][:, :, 0:UP], kv_ps[p][:, :, 0:UP], ACT.Copy, scale=UNWS).then_inc(kv_out, 1)
                if past(t, 1):
                    high(t - 1, 1 - p)

            each(act, T, 4, tile)
            high(T - 1, (T - 1) % 2)

        @block.vector
        def _(dve):
            dve.memset(V[:, :, :, 2 * UP:2 * UP + 1], 1.0)
            dve.memset(kT[0][QK:QK + 1, :, :], 1.0)

            def low(t, p):
                for j, dst in enumerate((qT, kT)):
                    dve.wait_ge(hi_done, 2 * t + j + 1)
                    dve.tensor_tensor(dst[1][0:QK, :, ds(t * P, P)], flipped[j][p][0:QK, :, :], dst[0][0:QK, :, ds(t * P, P)],
                                      ALU.subtract).then_inc(lo_done, 1)

            def tile(t, p):
                p = p % 2
                r = tok[0][p][:, :, UP:QK]
                wide = lambda table: table.to_broadcast([P, HH, table.shape[-1]])
                if past(t, 2):
                    dve.wait_ge(turned, 2 * (t - 2) + 2)
                    dve.wait_ge(rotated, t - 1)
                dve.tensor_tensor(tok[1][p][:, :, UP:QK], wide(k_rope[:, ds(t, 1), :]), wide(k_rope[:, ds(t, 1), :]),
                                  ALU.max).then_inc(k_ready, 1)
                dve.wait_ge(q_out, t + 1)
                dve.tensor_tensor(kept[p][:, :, :], r, wide(cos[:, ds(t, 1), :]), ALU.mult).then_inc(rot, 1)
                dve.tensor_tensor(swapped[p][:, :, 0:H], r[:, :, H:ROPE], wide(sin[:, ds(t, 1), 0:H]), ALU.mult).then_inc(rot, 1)
                dve.tensor_tensor(swapped[p][:, :, H:ROPE], r[:, :, 0:H], wide(sin[:, ds(t, 1), H:ROPE]), ALU.mult).then_inc(rot, 1)
                dve.wait_ge(rot, 3 * t + 3)
                dve.tensor_tensor(r, kept[p][:, :, :], swapped[p][:, :, :], ALU.add).then_inc(rotated, 1)
                dve.wait_ge(kv_out, t + 1)
                dve.scalar_tensor_tensor(V[:, ds(t, 1), :, 0:UP], kv_ps[p][:, :, UP:2 * UP].unsqueeze(1), UNWS,
                                         V[:, ds(t, 1), :, UP:2 * UP], ALU.mult, ALU.subtract).then_inc(v_lo, 1)
                if past(t, 1):
                    low(t - 1, 1 - p)

            each(dve, T, 4, tile)
            low(T - 1, (T - 1) % 2)


def query_maxima(nc, prefix, ident, qT, kT):
    with ExitStack() as ctx:
        s = Scope(nc, ctx, prefix)
        head_max = s.sb("head_max", [P, T])
        negated = s.sb("negated", [P, HH * T])
        rows = s.sb("rows", [HH * T, P], F16)
        scores = [s.ps(f"scores{i}", [P, N]) for i in range(2)]
        made, reduced, put, turned, rounded, moved = (s.sem(n) for n in ("made", "reduced", "put", "turned", "rounded", "moved"))
        block = ctx.enter_context(nc.Block())

        @block.tensor
        def _(pe):
            def head(h, _):
                for t in range(T):
                    n = T * h + t
                    if past(n, 2):
                        pe.wait_ge(reduced, n - 1)
                    for g in range(G):
                        gg = slice(g * GN, (g + 1) * GN)
                        last = pe.matmul(scores[t % 2][:, gg], lhsT=qT[0][0:QK, ds(h, 1), t * P:(t + 1) * P],
                                         rhs=kT[0][0:QK, ds(h, 1), gg], start=True, stop=True)
                    last.then_inc(made, 1)

            each(pe, HH, 1, head)
            pe.wait_ge(put, HH)
            pe.transpose(scores[0][0:HH * T, 0:P], negated[:, :], ident[:, :]).then_inc(turned, 1)

        @block.vector
        def _(dve):
            def head(h, _):
                if past(h, 1):
                    dve.wait_ge(put, h)
                for t in range(T):
                    dve.wait_ge(made, T * h + t + 1)
                    dve.tensor_reduce(head_max[:, t:t + 1], scores[t % 2][:, :], AXF, ALU.max).then_inc(reduced, 1)
                dve.wait_ge(reduced, T * h + T)
                dve.tensor_scalar(negated[:, ds(T * h, T)], head_max[:, :], -1.0, None, ALU.mult).then_inc(put, 1)

            each(dve, HH, 1, head)

        @block.scalar
        def _(act):
            act.wait_ge(turned, 1)
            act.activation(rows[:, :], scores[0][0:HH * T, 0:P], ACT.Copy).then_inc(rounded, 1)

        @block.sync
        def _(sp):
            sp.wait_ge(rounded, 1)
            sp.dma_start(qT[0][QK:QK + 1, :, :].rearrange("o h (t j) -> o (h t) j", j=P), rows[:, :]).then_inc(moved, 16)
            sp.wait_ge(moved, 16)


def attention(nc, prefix, qT, kT, V, heads_out, first_head):
    NB, LAG, FIN = 4, 2, 5
    STEPS = G * T
    with ExitStack() as ctx:
        s = Scope(nc, ctx, prefix)
        prob = [s.sb(f"prob{i}", [P, GN]) for i in range(NB)]
        p_hi = [s.sb(f"p_hi{i}", [P, GN], F16) for i in range(NB)]
        p_lo = [s.sb(f"p_lo{i}", [P, GN], F16) for i in range(NB)]
        v_low = [s.sb(f"v_low{i}", [P, TG, UP]) for i in range(2)]
        total = [s.sb(f"total{i}", [P, TG, UP]) for i in range(2)]
        o_sb = [s.sb(f"o_sb{i}", [P, TG, UP]) for i in range(2)]
        inv = [s.sb(f"inv{i}", [P, TG]) for i in range(2)]
        score = [s.ps(f"score{i}", [P, GN]) for i in range(4)]
        out = [s.ps(f"out{i}", [P, TG, 256]) for i in range(2)]
        scored, prob_done, hi_done, lo_done, weighed, low_out, summed, inverted, o_ready = (
            s.sem(n) for n in ("scored", "prob", "hi", "lo", "weighed", "low_out", "summed", "inverted", "o_ready"))
        stored = [s.sem(f"stored{i}") for i in range(2)]
        block = ctx.enter_context(nc.Block())

        def lagged(h, g, c, lag, do):
            if c >= lag:
                do(h, g, c - lag)
            elif g:
                do(h, g - 1, T + c - lag)
            elif past(h, 1):
                do(h - 1, G - 1, T + c - lag)

        def groups(h, g, c, do):
            if c == FIN:
                if g:
                    do(h, g - 1)
                elif past(h, 1):
                    do(h - 1, G - 1)

        @block.tensor
        def _(pe):
            def scores(h, g, c):
                m = STEPS * h + T * g + c
                if past(m, 4):
                    pe.wait_ge(hi_done, m - 3)
                cc, gg, hh, b = slice(c * P, (c + 1) * P), slice(g * GN, (g + 1) * GN), ds(h, 1), c % 4
                pe.matmul(score[b][:, :], lhsT=kT[0][0:QK + 1, hh, cc], rhs=qT[0][0:QK + 1, hh, gg], start=True, stop=False)
                pe.matmul(score[b][:, :], lhsT=kT[0][0:QK, hh, cc], rhs=qT[1][0:QK, hh, gg], start=False, stop=False)
                pe.matmul(score[b][:, :], lhsT=kT[1][0:QK, hh, cc], rhs=qT[0][0:QK, hh, gg], start=False,
                          stop=True).then_inc(scored, 1)

            def weigh(h, g, c):
                m = STEPS * h + T * g + c
                pe.wait_ge(lo_done, m + 1)
                if c == 0 and past(G * h + g, 2):
                    pe.wait_ge(summed, G * h + g - 1)
                for q in range(TG):
                    qq = slice(q * P, (q + 1) * P)
                    pe.matmul(out[g % 2][:, q, 0:2 * UP + 1], lhsT=p_hi[c % NB][:, qq], rhs=V[:, c, ds(h, 1), 0:2 * UP + 1],
                              start=c == 0 and q % 2 == 0, stop=False, skip_group_check=True)
                    last = pe.matmul(out[g % 2][:, q, UP:2 * UP + 1], lhsT=p_lo[c % NB][:, qq], rhs=V[:, c, ds(h, 1), UP:2 * UP + 1],
                                     start=False, stop=c == T - 1, skip_group_check=True)
                last.then_inc(weighed, 1)

            def head(h, _):
                for g in range(G):
                    for c in range(T):
                        scores(h, g, c)
                        lagged(h, g, c, LAG, weigh)

            each(pe, HH, 1, head)
            for c in range(T - LAG, T):
                weigh(HH - 1, G - 1, c)

        @block.scalar
        def _(act):
            def low_sum(h, g):
                act.wait_ge(weighed, STEPS * h + T * (g + 1))
                if past(G * h + g, 2):
                    act.wait_ge(summed, G * h + g - 1)
                act.activation(v_low[g % 2][:, :, :], out[g % 2][:, :, 0:UP], ACT.Copy).then_inc(low_out, 1)

            def head(h, _):
                for g in range(G):
                    for c in range(T):
                        m, b = STEPS * h + T * g + c, c % NB
                        act.wait_ge(scored, m + 1)
                        if past(m, NB):
                            act.wait_ge(lo_done, m - NB + 1)
                            act.wait_ge(weighed, m - NB + 1)
                        act.activation(prob[b][:, :], score[c % 4][:, :], ACT.Exp).then_inc(prob_done, 1)
                        act.activation(p_hi[b][:, :], score[c % 4][:, :], ACT.Exp).then_inc(hi_done, 1)
                        groups(h, g, c, low_sum)

            each(act, HH, 1, head)
            low_sum(HH - 1, G - 1)

        @block.vector
        def _(dve):
            def finish(h, g):
                n, b = G * h + g, g % 2
                dve.wait_ge(low_out, n + 1)
                dve.reciprocal(inv[b][:, :], out[b][:, :, 2 * UP]).then_inc(inverted, 1)
                dve.tensor_tensor(total[b][:, :, :], out[b][:, :, UP:2 * UP], v_low[b][:, :, :], ALU.add).then_inc(summed, 1)
                dve.wait_ge(inverted, n + 1)
                dve.wait_ge(summed, n + 1)
                if past(n, 2):
                    dve.wait_ge(stored[b], 16 * (G // 2 * h + g // 2))
                dve.tensor_tensor(o_sb[b][:, :, :], total[b][:, :, :], inv[b][:, :].unsqueeze(2).to_broadcast([P, TG, UP]),
                                  ALU.mult).then_inc(o_ready, 1)

            def head(h, _):
                for g in range(G):
                    for c in range(T):
                        m, b = STEPS * h + T * g + c, c % NB
                        dve.wait_ge(prob_done, m + 1)
                        dve.wait_ge(hi_done, m + 1)
                        dve.tensor_tensor(p_lo[b][:, :], prob[b][:, :], p_hi[b][:, :], ALU.subtract).then_inc(lo_done, 1)
                        groups(h, g, c, finish)

            each(dve, HH, 1, head)
            finish(HH - 1, G - 1)

        @block.sync
        def _(sp):
            def head(h, _):
                for g in range(G):
                    n = G * h + g
                    sp.wait_ge(o_ready, n + 1)
                    rows = heads_out[g * GN:(g + 1) * GN, :].rearrange("(q p) d -> p q d", p=P)
                    sp.dma_start(rows[:, :, ds((h + first_head) * UP, UP)], o_sb[g % 2][:, :, :]).then_inc(stored[g % 2], 16)

            each(sp, HH, 1, head)
            for b in range(2):
                sp.wait_ge(stored[b], 16 * HH * G // 2)


def project_out(nc, oT, W_o, res):
    NB, K = 4, HEADS * UP // P
    with ExitStack() as ctx:
        s = Scope(nc, ctx, "wo_")
        prod = [s.ps(f"prod{i}", [P, 512]) for i in range(NB)]
        made, added = s.sem("made"), s.sem("added")
        block = ctx.enter_context(nc.Block())

        @block.tensor
        def _(pe):
            def tile(t, p):
                if past(t, NB):
                    pe.wait_ge(added, t - NB + 1)
                for k in range(K):
                    last = matmul3(pe, prod[p][:, 0:D], oT[0][:, k, ds(t * P, P)], oT[1][:, k, ds(t * P, P)],
                                   W_o[0][:, k, :], W_o[1][:, k, :], k == 0, k == K - 1)
                last.then_inc(made, 1)

            each(pe, T, NB, tile)

        @block.vector
        def _(dve):
            def tile(t, p):
                dve.wait_ge(made, t + 1)
                dve.scalar_tensor_tensor(res[:, ds(t, 1), :], prod[p][:, 0:D].unsqueeze(1), UNWS, res[:, ds(t, 1), :],
                                         ALU.mult, ALU.add).then_inc(added, 1)

            each(dve, T, NB, tile)


def l1_attention(nc, a, x, res, ident):
    heads_out = nc.dram_tensor("heads_out", (N, HEADS * UP), F32, kind="Internal").ap()
    col = lambda ap: ap.rearrange("(k p) -> p k", p=P)
    rows = lambda ap: ap.rearrange("(k p) n -> p k n", p=P)
    normalize_and_turn(nc, "a1n_", ident, x, D, "layer", None, None, tok=res)
    with ExitStack() as ctx:
        s = Scope(nc, ctx, "a1_")
        cqT = s.sb("cqT_hi", [P, 1, N], F16), s.sb("cqT_lo", [P, 1, N], F16)
        ckvT = s.sb("ckvT_hi", [P, 1, N], F16), s.sb("ckvT_lo", [P, 1, N], F16)
        cos, sin, k_rope = (s.sb(n, [P, T, ROPE]) for n in ("cos", "sin", "k_rope"))
        W_uq = s.sb("uq_hi", [P, 1, HEADS * QK], F16), s.sb("uq_lo", [P, 1, HEADS * QK], F16)
        W_ukv = s.sb("ukv_hi", [P, 1, HEADS * 2 * UP], F16), s.sb("ukv_lo", [P, 1, HEADS * 2 * UP], F16)
        with ExitStack() as early:
            s = Scope(nc, early, "a1e_")
            xT = s.sb("xT_hi", [P, KD, N], F16), s.sb("xT_lo", [P, KD, N], F16)
            c_q, c_kv = s.sb("c_q", [P, T, DQ]), s.sb("c_kv", [P, T, DKV])
            W = s.sb("W_hi", [P, KD, DQ + DKV + ROPE], F16), s.sb("W_lo", [P, KD, DQ + DKV + ROPE], F16)
            dq, dkv = slice(0, DQ), slice(DQ, DQ + DKV + ROPE)
            split_weights(nc, "a1w_", [
                (rows(a["L1_ffn_w_dq"]), col(a["L1_ffn_w_in_norm"]), W[0][:, :, dq], W[1][:, :, dq]),
                (rows(a["L1_ffn_w_dkv"]), col(a["L1_ffn_w_in_norm"]), W[0][:, :, dkv], W[1][:, :, dkv]),
                (rows(a["L1_ffn_w_uq"]), col(a["L1_ffn_w_qnorm"]), W_uq[0][:, :, :], W_uq[1][:, :, :]),
                (rows(a["L1_ffn_w_ukv"]), col(a["L1_ffn_w_kvnorm"]), W_ukv[0][:, :, :], W_ukv[1][:, :, :])])
            normalize_and_turn(nc, "a1r_", ident, res, D, "rms", *xT)
            latent_project(nc, a, xT, W[0], W[1], c_q, c_kv, k_rope, cos, sin)
            normalize_and_turn(nc, "a1q_", ident, c_q, DQ, "rms", *cqT)
            normalize_and_turn(nc, "a1k_", ident, c_kv, DKV, "rms", *ckvT)
        s = Scope(nc, ctx, "a1h_")
        qT = s.sb("qT_hi", [P, HH, N], F16), s.sb("qT_lo", [P, HH, N], F16)
        kT = s.sb("kT_hi", [P, HH, N], F16), s.sb("kT_lo", [P, HH, N], F16)
        V = s.sb("V", [P, T, HH, 2 * UP + 2], F16)
        for n, first in enumerate(range(0, HEADS, HH)):
            uq, ukv = slice(first * QK, (first + HH) * QK), slice(first * 2 * UP, (first + HH) * 2 * UP)
            queries_keys_values(nc, f"qkv{n}_", ident, cqT, ckvT, [w[:, 0, uq] for w in W_uq], [w[:, 0, ukv] for w in W_ukv],
                                k_rope, cos, sin, qT, kT, V)
            query_maxima(nc, f"max{n}_", ident, qT, kT)
            nc.disable_value_cache = True
            attention(nc, f"att{n}_", qT, kT, V, heads_out, first)
            nc.disable_value_cache = False
    with ExitStack() as ctx:
        s = Scope(nc, ctx, "a1o_")
        heads = s.sb("heads", [P, T, HEADS * UP])
        oT = s.sb("oT_hi", [P, HEADS * UP // P, N], F16), s.sb("oT_lo", [P, HEADS * UP // P, N], F16)
        W_o = s.sb("W_o_hi", [P, HEADS * UP // P, D], F16), s.sb("W_o_lo", [P, HEADS * UP // P, D], F16)
        load_or_store(nc, "heads_", heads[:, :, :], heads_out.rearrange("(t p) d -> p t d", p=P))
        split_weights(nc, "a1ow_", [(rows(a["L1_ffn_w_o"]), None, W_o[0][:, :, :], W_o[1][:, :, :])])
        normalize_and_turn(nc, "a1t_", ident, heads, HEADS * UP, None, *oT)
        project_out(nc, oT, W_o, res)


def load_experts(nc, a, raw):
    with ExitStack() as ctx:
        s = Scope(nc, ctx, "le_")
        loaded = s.sem("loaded")
        block = ctx.enter_context(nc.Block())

        @block.sync
        def _(sp):
            for j, (routed, shared) in enumerate((("r_wg", "sh_wg"), ("r_wu", "sh_wu"))):
                for k in range(KD):
                    kk = slice(k * P, (k + 1) * P)
                    sp.dma_start(raw[:, 2 * j + k, 0:L1_E, :], a["L1_ffn_" + routed][:, kk, :].rearrange("e p i -> p e i")).then_inc(loaded, 16)
                    sp.dma_start(raw[:, 2 * j + k, L1_E, :], a["L1_ffn_" + shared][kk, :]).then_inc(loaded, 16)
            for k in range(KD):
                kk = slice(k * P, (k + 1) * P)
                sp.dma_start(raw[:, 4 + k, 0:L1_E, :], a["L1_ffn_r_wd"][:, :, kk].rearrange("e p i -> p e i")).then_inc(loaded, 16)
                sp.dma_start(raw[:, 4 + k, L1_E, :], a["L1_ffn_sh_wd"][:, kk]).then_inc(loaded, 16)
            sp.wait_ge(loaded, 16 * 12)


def l1_experts(nc, x, res, hT, raw, scale, w_hi, w_lo, comb):
    E = L1_E + 1
    LAG = 2
    with ExitStack() as ctx:
        s = Scope(nc, ctx, "e1_")
        gate_out = [s.sb(f"gate{i}", [P, GN]) for i in range(2)]
        mixed = [s.sb(f"mixed{i}", [P, GN]) for i in range(2)]
        hid = [(s.sb(f"hid_hi{i}", [P, GN], F16), s.sb(f"hid_lo{i}", [P, GN], F16)) for i in range(4)]
        up = [[s.ps(f"up{j}{i}", [P, GN]) for i in range(2)] for j in range(2)]
        down = [s.ps(f"down{i}", [P, 512]) for i in range(TG)]
        w_high, w_low, up_done, gated, mixed_done, hi_done, lo_done, down_done, added = (
            s.sem(n) for n in ("w_high", "w_low", "up", "gated", "mixed", "hi", "lo", "down", "added"))
        block = ctx.enter_context(nc.Block())
        WROWS = 6
        AHEAD = 2

        def all_experts(eng, expert, prepare):
            for e in range(AHEAD):
                prepare(e)

            def body(e, _):
                prepare(e + AHEAD)
                expert(e)

            each(eng, E - AHEAD, 1, body)
            for e in range(E - AHEAD, E):
                expert(e)

        def lagged(e, g, do):
            if g >= LAG:
                do(e, g - LAG)
            elif past(e, 1):
                do(e - 1, G + g - LAG)

        @block.tensor
        def _(pe):
            def project_down(e, g):
                u = G * e + g
                pe.wait_ge(lo_done, u + 1)
                for q in range(TG):
                    if past(u, 1):
                        pe.wait_ge(added, TG * (u - 1) + q + 1)
                    qq = slice(q * P, (q + 1) * P)
                    last = matmul3(pe, down[q][:, 0:D], hid[g][0][:, qq], hid[g][1][:, qq],
                                   w_hi[:, 4:6, ds(e, 1), :], w_lo[:, 4:6, ds(e, 1), :], True, True)
                    last.then_inc(down_done, 1)

            def expert(e):
                pe.wait_ge(w_low, WROWS * e + WROWS)
                for g in range(G):
                    u, gg = G * e + g, slice(g * GN, (g + 1) * GN)
                    if past(u, 2):
                        pe.wait_ge(mixed_done, u - 1)
                    for j in range(2):
                        for k in range(KD):
                            last = matmul3(pe, up[j][g % 2][:, :], w_hi[:, 2 * j + k, ds(e, 1), :], w_lo[:, 2 * j + k, ds(e, 1), :],
                                           hT[0][:, k, gg], hT[1][:, k, gg], k == 0, k == KD - 1)
                        last.then_inc(up_done, 1)
                    lagged(e, g, project_down)

            all_experts(pe, expert, lambda e: None)
            for g in range(G - LAG, G):
                project_down(E - 1, g)

        @block.scalar
        def _(act):
            def prepare(e):
                for r in range(WROWS):
                    act.activation(w_hi[:, r, ds(e, 1), :], raw[:, r, ds(e, 1), :], ACT.Copy,
                                   scale=scale[:, r % 2:r % 2 + 1] if r < 4 else WS).then_inc(w_high, 1)

            def expert(e):
                for g in range(G):
                    u, b = G * e + g, g % 2
                    act.wait_ge(up_done, 2 * u + 1)
                    if past(u, 2):
                        act.wait_ge(mixed_done, u - 1)
                    act.activation(gate_out[b][:, :], up[0][b][:, :], ACT.Silu, scale=UNWS).then_inc(gated, 1)
                    act.wait_ge(mixed_done, u + 1)
                    if past(u, 4):
                        act.wait_ge(down_done, TG * (u - 3))
                    act.activation(hid[g][0][:, :], mixed[b][:, :], ACT.Copy).then_inc(hi_done, 1)

            all_experts(act, expert, prepare)

        @block.vector
        def _(dve):
            def prepare(e):
                for r in range(WROWS):
                    dve.wait_ge(w_high, WROWS * e + r + 1)
                    dve.scalar_tensor_tensor(w_lo[:, r, ds(e, 1), :], raw[:, r, ds(e, 1), :],
                                             scale[:, r % 2:r % 2 + 1] if r < 4 else WS, w_hi[:, r, ds(e, 1), :],
                                             ALU.mult, ALU.subtract).then_inc(w_low, 1)

            def add(e, g):
                u = G * e + g
                for q in range(TG):
                    n = TG * u + q
                    dve.wait_ge(down_done, n + 1)
                    if past(u, 1):
                        dve.wait_ge(added, n - TG + 1)
                    dve.scalar_tensor_tensor(res[:, TG * g + q, :], down[q][:, 0:D], comb[:, TG * g + q, ds(e, 1)],
                                             res[:, TG * g + q, :], ALU.mult, ALU.add).then_inc(added, 1)

            def expert(e):
                for g in range(G):
                    u, b = G * e + g, g % 2
                    dve.wait_ge(gated, u + 1)
                    dve.wait_ge(up_done, 2 * u + 2)
                    if past(u, 2):
                        dve.wait_ge(hi_done, u - 1)
                        dve.wait_ge(lo_done, u - 1)
                    dve.scalar_tensor_tensor(mixed[b][:, :], up[1][b][:, :], UNWS, gate_out[b][:, :], ALU.mult,
                                             ALU.mult).then_inc(mixed_done, 1)
                    dve.wait_ge(hi_done, u + 1)
                    dve.tensor_tensor(hid[g][1][:, :], mixed[b][:, :], hid[g][0][:, :], ALU.subtract).then_inc(lo_done, 1)
                    lagged(e, g, add)

            all_experts(dve, expert, prepare)
            for g in range(G - LAG, G):
                add(E - 1, g)
            for t in range(T):
                dve.wait_ge(added, TG * (G * (E - 1)) + t + 1)
                dve.tensor_tensor(x[:, t, :], x[:, t, :], res[:, t, :], ALU.add)


def prepare_scale(nc, src, scale, shared):
    with ExitStack() as ctx:
        s = Scope(nc, ctx, "sc_")
        loaded, steps = s.sem("loaded"), s.sem("steps")
        block = ctx.enter_context(nc.Block())

        @block.sync
        def _(sp):
            with nc.allow_non_contiguous_dma(reason="a short column of norm weights"):
                sp.dma_start(scale[:, :], src).then_inc(loaded, 16)

        @block.vector
        def _(dve):
            dve.memset(shared, UNWS)
            dve.wait_ge(loaded, 16)
            dve.tensor_scalar(scale[:, :], scale[:, :], WS, None, ALU.mult)


def l1_moe(nc, a, x, res, ident):
    with ExitStack() as ctx:
        s = Scope(nc, ctx, "m1_")
        raw = s.sb("raw", [P, 6, L1_E + 1, P])
        w_hi, w_lo = s.sb("w_hi", [P, 6, L1_E + 1, P], F16), s.sb("w_lo", [P, 6, L1_E + 1, P], F16)
        hT = s.sb("hT_hi", [P, KD, N], F16), s.sb("hT_lo", [P, KD, N], F16)
        Wg = s.sb("Wg_hi", [P, KD, L1_E], F16), s.sb("Wg_lo", [P, KD, L1_E], F16)
        scale = s.sb("scale", [P, KD])
        comb = s.sb("comb", [P, T, L1_E + 1])
        norm = a["L1_ffn_w_post_norm"].rearrange("(k p) -> p k", p=P)
        load_experts(nc, a, raw)
        prepare_scale(nc, norm, scale, comb[:, :, L1_E:L1_E + 1])
        split_weights(nc, "m1w_", [(a["L1_ffn_w_gate"].rearrange("(k p) e -> p k e", p=P), norm, Wg[0][:, :, :], Wg[1][:, :, :])])
        normalize_and_turn(nc, "m1n_", ident, res, D, "rms", *hT)
        route(nc, "m1r_", ident, L1_E, L1_K, hT, Wg, None, comb[:, :, 0:L1_E])
        l1_experts(nc, x, res, hT, raw, scale, w_hi, w_lo, comb)


def l1_ffn(nc, a, x, ident):
    with ExitStack() as ctx:
        res = Scope(nc, ctx, "").sb("res", [P, T, D])
        l1_attention(nc, a, x, res, ident)
        recycle_semaphores(nc)
        l1_moe(nc, a, x, res, ident)


def load_or_store(nc, prefix, out, in_):
    with ExitStack() as ctx:
        done = Scope(nc, ctx, prefix).sem("done")
        block = ctx.enter_context(nc.Block())

        @block.sync
        def _(sp):
            sp.dma_start(out, in_).then_inc(done, 16)
            sp.wait_ge(done, 16)


def build(nc, a, out):
    Scope.used.clear()
    with ExitStack() as ctx:
        s = Scope(nc, ctx, "")
        ident, ident16, ones = s.sb("ident", [P, P]), s.sb("ident16", [P, P], F16), s.sb("ones", [P, P])
        x = s.sb("x", [P, T, D])
        tiles = lambda ap: ap.rearrange("(t p) d -> p t d", p=P)
        make_identities(nc, ident, ident16, ones)
        load_or_store(nc, "in_", x[:, :, :], tiles(a["x"]))
        with ExitStack() as adj_ctx:
            s2 = Scope(nc, adj_ctx, "")
            adjT, diag = s2.sb("adjT", [P, T, N], F16), s2.sb("diag", [P, T, P], F16)
            transpose_adjacency(nc, a["adj"], ident16, adjT, diag)
            l0_gnn(nc, a, x, ident, ident16, ones, adjT, diag)
            recycle_semaphores(nc)
            l0_ffn(nc, a, x, ident); recycle_semaphores(nc); l1_gnn(nc, a, x, ident, adjT, diag)
            recycle_semaphores(nc)
        l1_ffn(nc, a, x, ident)
        load_or_store(nc, "out_", tiles(out), x[:, :, :])


INPUTS = ["x", "adj", "L0_gnn_W", "L0_ffn_Wg", "L0_ffn_bg", "L0_ffn_W1", "L0_ffn_b1", "L0_ffn_W2", "L0_ffn_b2",
          "L1_gnn_W_nb", "L1_gnn_b_nb", "L1_gnn_W_line", "L1_gnn_b_line", "L1_ffn_w_in_norm", "L1_ffn_w_dq",
          "L1_ffn_w_qnorm", "L1_ffn_w_uq", "L1_ffn_w_dkv", "L1_ffn_w_kvnorm", "L1_ffn_w_ukv", "L1_ffn_w_o",
          "L1_ffn_w_post_norm", "L1_ffn_w_gate", "L1_ffn_sh_wg", "L1_ffn_sh_wu", "L1_ffn_sh_wd", "L1_ffn_r_wg",
          "L1_ffn_r_wu", "L1_ffn_r_wd"]


def kernel(**inputs):
    import numpy as np
    import concourse.bacc as bacc
    from concourse.bass_utils import run_bass_kernel_spmd

    nc = bacc.Bacc("TRN2", target_bir_lowering=False, num_devices=1)
    arrays = {name: np.ascontiguousarray(inputs[name]) for name in INPUTS}
    freq = (np.float32(1.0) / np.float32(10000.0) ** (np.arange(0, ROPE, 2, dtype=np.float32) / np.float32(ROPE))).astype(np.float32)
    angle = np.outer(np.arange(N, dtype=np.float32), freq).astype(np.float32)
    arrays["rope_cos"] = np.concatenate([np.cos(angle), np.cos(angle)], axis=-1).astype(np.float32)
    arrays["rope_sin"] = np.concatenate([-np.sin(angle), np.sin(angle)], axis=-1).astype(np.float32)
    args = {name: nc.dram_tensor("in_" + name, v.shape, mybir.dt.from_np(v.dtype), kind="ExternalInput").ap()
            for name, v in arrays.items()}
    out = nc.dram_tensor("out_0", (N, D), F32, kind="ExternalOutput").ap()
    build(nc, args, out)
    r = run_bass_kernel_spmd(nc, [{"in_" + name: v for name, v in arrays.items()}], core_ids=[0])
    return r.results[0]["out_0"]
```

```python
import concourse.bass as bass
from concourse import mybir
from contextlib import ExitStack

F32 = mybir.dt.float32
F16 = mybir.dt.float16
I32 = mybir.dt.int32
ALU = mybir.AluOpType
ACT = mybir.ActivationFunctionType
AXF = mybir.AxisListType.X
ds = bass.ds

P = 128
N = 2048
D = 256
T = N // P
KD = D // P
G = 4
GN = N // G
TG = GN // P
WS = 64.0
UNWS = 1.0 / WS
LN_EPS = 1e-5
RMS_EPS = 1.1920929e-07
SIM_EPS = 1e-8
NEIGHBORS = 64
L0_E, L0_F, L0_K = 8, 1024, 2
FC = L0_F // P
L1_E, L1_I, L1_K = 16, 128, 4
HEADS, UP, ROPE = 8, 64, 32
QK = UP + ROPE
HH = 4
DQ = DKV = 128
Q_HI, K_HI, Q_LO, K_LO = range(4)
ATT_SCALE = 1.0 / float(QK) ** 0.5
BIG = 1.0e30


class Scope:

    used = []

    def __init__(self, nc, ctx, prefix):
        self.nc, self.ctx, self.prefix = nc, ctx, prefix

    def sb(self, name, shape, dt=F32):
        return self.ctx.enter_context(self.nc.sbuf_tensor(self.prefix + name, shape, dt))

    def ps(self, name, shape, dt=F32):
        return self.ctx.enter_context(self.nc.psum_tensor(self.prefix + name, shape, dt))

    def sem(self, name):
        handle = self.nc.alloc_semaphore(self.prefix + name)
        Scope.used.append(handle)
        return handle


def recycle_semaphores(nc):
    nc.clear_and_free_semaphores(Scope.used)
    nc.all_engine_barrier()
    Scope.used.clear()


class Chain:

    def __init__(self, eng, sem):
        self.eng, self.sem, self.n = eng, sem, 0

    def __call__(self, ins):
        ins.then_inc(self.sem, 1)
        self.n += 1
        self.eng.wait_ge(self.sem, self.n)


def each(eng, n, step, body):
    for i in range(step):
        body(i, i)
    if n > step:
        with eng.Fori(1, n // step) as j:
            for p in range(step):
                body(j * step + p, p)


def past(i, n):
    return not isinstance(i, int) or i >= n


def make_identities(nc, ident, ident16, ones):
    with ExitStack() as ctx:
        s = Scope(nc, ctx, "id_")
        cleared, done = s.sem("cleared"), s.sem("done")
        block = ctx.enter_context(nc.Block())

        @block.gpsimd
        def _(pool):
            pool.memset(ident[:, :], 0.0).then_inc(cleared, 1)
            pool.wait_ge(cleared, 1)
            pool.affine_select(out=ident[:, :], in_=ident[:, :], compare_op=ALU.not_equal, fill=1.0, base=0,
                               pattern=[[-1, P]], channel_multiplier=1).then_inc(done, 1)

        @block.vector
        def _(dve):
            dve.memset(ones[:, :], 1.0)
            dve.wait_ge(done, 1)
            dve.tensor_copy(ident16[:, :], ident[:, :])


def split_weights(nc, prefix, items):
    with ExitStack() as ctx:
        s = Scope(nc, ctx, prefix)
        raw = [s.sb(f"raw{i}", list(src.shape)) for i, (src, *_) in enumerate(items)]
        scale = [s.sb(f"scale{i}", list(sc.shape)) if sc is not None else None for i, (_, sc, _, _) in enumerate(items)]
        loaded = [s.sem(f"loaded{i}") for i in range(len(items))]
        scaled, hi_done, lo_done = s.sem("scaled"), s.sem("hi"), s.sem("lo")
        block = ctx.enter_context(nc.Block())

        @block.sync
        def _(sp):
            for i, (src, sc, _, _) in enumerate(items):
                sp.dma_start(raw[i][:, :, :], src).then_inc(loaded[i], 16)
                if sc is not None:
                    with nc.allow_non_contiguous_dma(reason="a short column of norm weights"):
                        sp.dma_start(scale[i][:, :], sc).then_inc(loaded[i], 16)

        @block.scalar
        def _(act):
            for i, (src, sc, hi, _) in enumerate(items):
                act.wait_ge(scaled, i + 1)
                act.activation(hi, raw[i][:, :, :], ACT.Copy, scale=WS).then_inc(hi_done, 1)

        @block.vector
        def _(dve):
            steps = s_steps = 0
            for i, (src, sc, hi, lo) in enumerate(items):
                dve.wait_ge(loaded[i], 16 if sc is None else 32)
                if sc is not None:
                    for k in range(src.shape[1]):
                        last = dve.tensor_scalar(raw[i][:, k, :], raw[i][:, k, :], scale[i][:, k:k + 1], None, ALU.mult)
                    last.then_inc(scaled, 1)
                else:
                    dve.engine_nop().then_inc(scaled, 1)
            for i, (src, sc, hi, lo) in enumerate(items):
                dve.wait_ge(scaled, i + 1)
                dve.wait_ge(hi_done, i + 1)
                dve.scalar_tensor_tensor(lo, raw[i][:, :, :], WS, hi, ALU.mult, ALU.subtract).then_inc(lo_done, 1)


def split_transposed_weights(nc, prefix, ident, items):
    with ExitStack() as ctx:
        s = Scope(nc, ctx, prefix)
        raw = [s.sb(f"raw{i}", [P, KD, D]) for i in range(len(items))]
        flipped = [s.ps(f"flipped{i}", [P, KD, D]) for i in range(len(items))]
        loaded = [s.sem(f"loaded{i}") for i in range(len(items))]
        turned, hi_done = s.sem("turned"), s.sem("hi")
        block = ctx.enter_context(nc.Block())

        @block.sync
        def _(sp):
            for i, (src, _, _) in enumerate(items):
                sp.dma_start(raw[i][:, :, :], src.rearrange("(o p) i -> p o i", p=P)).then_inc(loaded[i], 16)

        @block.tensor
        def _(pe):
            for i in range(len(items)):
                pe.wait_ge(loaded[i], 16)
                for o in range(KD):
                    for k in range(KD):
                        last = pe.transpose(flipped[i][:, k, o * P:(o + 1) * P], raw[i][:, o, k * P:(k + 1) * P], ident[:, :])
                last.then_inc(turned, 1)

        @block.scalar
        def _(act):
            for i, (_, hi, _) in enumerate(items):
                act.wait_ge(turned, i + 1)
                act.activation(hi, flipped[i][:, :, :], ACT.Copy, scale=WS).then_inc(hi_done, 1)

        @block.vector
        def _(dve):
            for i, (_, hi, lo) in enumerate(items):
                dve.wait_ge(hi_done, i + 1)
                dve.scalar_tensor_tensor(lo, flipped[i][:, :, :], WS, hi, ALU.mult, ALU.subtract)


def normalize_and_turn(nc, prefix, ident, src, width, kind, xT_hi, xT_lo, tok=None, tok_hi=None, tok_lo=None):
    chunks, NB = width // P, 4
    with ExitStack() as ctx:
        s = Scope(nc, ctx, prefix)
        stats = s.sb("stats", [P, T, 6])
        dif, mean, second, var = (s.sb(n, [P, T]) for n in ("dif", "mean", "second", "var"))
        std, rstd = s.sb("std", [P, T]), s.sb("rstd", [P, T])
        stage = [s.sb(f"stage{i}", [P, width]) for i in range(NB)]
        turned = [s.ps(f"turned{i}", [P, 512]) for i in range(NB)]
        stat_done, steps, var_done, std_done = s.sem("stat"), s.sem("steps"), s.sem("var"), s.sem("std")
        staged, flipped, hi_done, lo_done = s.sem("staged"), s.sem("flipped"), s.sem("hi"), s.sem("lo")
        copied, tok_hi_done = s.sem("copied"), s.sem("tok_hi")
        block = ctx.enter_context(nc.Block())
        keeps = tok is not None or tok_hi is not None

        @block.vector
        def _(dve):
            if tok_hi is not None:
                dve.memset(tok_hi[:, :, width:width + 1], 1.0)
            if kind:
                with dve.Fori(0, T) as t:
                    dve.bn_stats(stats[:, ds(t, 1), :], src[:, ds(t, 1), :]).then_inc(stat_done, 1)
                dve.wait_ge(stat_done, T)
                link = Chain(dve, steps)
                me, mo = stats[:, :, 1], stats[:, :, 4]
                link(dve.tensor_tensor(dif[:, :], me, mo, ALU.subtract))
                link(dve.tensor_tensor(mean[:, :], me, mo, ALU.add))
                link(dve.tensor_scalar(mean[:, :], mean[:, :], 0.5, None, ALU.mult))
                link(dve.tensor_tensor(second[:, :], stats[:, :, 2], stats[:, :, 5], ALU.add))
                link(dve.tensor_tensor(dif[:, :], dif[:, :], dif[:, :], ALU.mult))
                link(dve.tensor_scalar(second[:, :], second[:, :], 1.0 / width, LN_EPS if kind == "layer" else RMS_EPS,
                                       ALU.mult, ALU.add))
                link(dve.scalar_tensor_tensor(var[:, :], dif[:, :], 0.25, second[:, :], ALU.mult, ALU.add))
                if kind == "rms":
                    link(dve.tensor_tensor(dif[:, :], mean[:, :], mean[:, :], ALU.mult))
                    link(dve.tensor_tensor(var[:, :], var[:, :], dif[:, :], ALU.add))
                dve.engine_nop().then_inc(var_done, 1)
                dve.wait_ge(std_done, 1)
                link(dve.reciprocal(rstd[:, :], std[:, :]))
            if xT_hi is None:
                with dve.Fori(0, T) as t:
                    dve.tensor_scalar(tok[:, ds(t, 1), :], src[:, ds(t, 1), :], mean[:, ds(t, 1)], rstd[:, ds(t, 1)],
                                      ALU.subtract, ALU.mult)
                return

            def finish(t, p):
                dve.wait_ge(hi_done, t + 1)
                dve.tensor_tensor(xT_lo[:, :, ds(t * P, P)], turned[p][:, 0:width].rearrange("p (k n) -> p k n", k=chunks),
                                  xT_hi[:, :, ds(t * P, P)], ALU.subtract).then_inc(lo_done, 1)
                if tok_lo is not None:
                    dve.wait_ge(tok_hi_done, t + 1)
                    dve.tensor_tensor(tok_lo[:, ds(t, 1), 0:width], stage[p][:, :].unsqueeze(1),
                                      tok_hi[:, ds(t, 1), 0:width], ALU.subtract)

            def step(t, p):
                if past(t, NB):
                    dve.wait_ge(flipped, t - NB + 1)
                    if keeps:
                        dve.wait_ge(copied, t - NB + 1)
                out = stage[p][:, :].unsqueeze(1)
                if kind == "layer":
                    ins = dve.tensor_scalar(out, src[:, ds(t, 1), :], mean[:, ds(t, 1)], rstd[:, ds(t, 1)],
                                            ALU.subtract, ALU.mult)
                elif kind == "rms":
                    ins = dve.tensor_scalar(out, src[:, ds(t, 1), :], rstd[:, ds(t, 1)], None, ALU.mult)
                else:
                    ins = dve.tensor_copy(out, src[:, ds(t, 1), :])
                ins.then_inc(staged, 1)
                if past(t, 1):
                    finish(t - 1, (p - 1) % NB)

            each(dve, T, NB, step)
            finish(T - 1, (T - 1) % NB)

        @block.tensor
        def _(pe):
            if xT_hi is None:
                return

            def step(t, p):
                pe.wait_ge(staged, t + 1)
                if past(t, NB):
                    pe.wait_ge(lo_done, t - NB + 1)
                for k in range(chunks):
                    last = pe.transpose(turned[p][:, k * P:(k + 1) * P], stage[p][:, k * P:(k + 1) * P], ident[:, :])
                last.then_inc(flipped, 1)

            each(pe, T, NB, step)

        @block.scalar
        def _(act):
            if kind:
                act.wait_ge(var_done, 1)
                act.activation(std[:, :], var[:, :], ACT.Sqrt).then_inc(std_done, 1)
            if xT_hi is None:
                return

            def step(t, p):
                if keeps:
                    act.wait_ge(staged, t + 1)
                    if tok_hi is not None:
                        ins = act.activation(tok_hi[:, ds(t, 1), 0:width], stage[p][:, :].unsqueeze(1), ACT.Copy)
                        ins.then_inc(tok_hi_done, 1)
                    if tok is not None:
                        ins = act.activation(tok[:, ds(t, 1), 0:width], stage[p][:, :].unsqueeze(1), ACT.Copy)
                    else:
                        ins = act.nop()
                    ins.then_inc(copied, 1)
                act.wait_ge(flipped, t + 1)
                act.activation(xT_hi[:, :, ds(t * P, P)], turned[p][:, 0:width].rearrange("p (k n) -> p k n", k=chunks),
                               ACT.Copy).then_inc(hi_done, 1)

            each(act, T, NB, step)


def matmul3(pe, out, a_hi, a_lo, b_hi, b_lo, first, last):
    pe.matmul(out, lhsT=a_hi, rhs=b_hi, start=first, stop=False)
    pe.matmul(out, lhsT=a_hi, rhs=b_lo, start=False, stop=False)
    return pe.matmul(out, lhsT=a_lo, rhs=b_hi, start=False, stop=last)


def transpose_adjacency(nc, adj, ident16, adjT, diag):
    NB, RB = 2, 3
    with ExitStack() as ctx:
        s = Scope(nc, ctx, "adj_")
        raw = [s.sb(f"raw{i}", [P, N], I32) for i in range(RB)]
        mask = [s.sb(f"mask{i}", [P, N], F16) for i in range(NB)]
        flipped = [s.ps(f"flipped{i}", [P, T, P], F16) for i in range(NB)]
        loaded = [s.sem(f"loaded{i}") for i in range(RB)]
        masked, turned, act_out, dve_out, kept = (s.sem(n) for n in ("masked", "turned", "act_out", "dve_out", "kept"))
        half = T // 2
        block = ctx.enter_context(nc.Block())

        @block.sync
        def _(sp):
            for t in range(T):
                if t >= RB:
                    sp.wait_ge(masked, t - RB + 1)
                sp.dma_start(raw[t % RB][:, :], adj[t * P:(t + 1) * P, :]).then_inc(loaded[t % RB], 16)

        @block.vector
        def _(dve):
            def out(t, p):
                dve.wait_ge(turned, t + 1)
                dve.tensor_copy(adjT[:, half:T, ds(t * P, P)], flipped[p][:, half:T, :]).then_inc(dve_out, 1)

            for t in range(T):
                dve.wait_ge(loaded[t % RB], 16 * (t // RB + 1))
                if t >= NB:
                    dve.wait_ge(turned, t - NB + 1)
                dve.tensor_scalar(mask[t % NB][:, :], raw[t % RB][:, :], 0, None, ALU.is_gt).then_inc(masked, 1)
                if t >= 1:
                    out(t - 1, (t - 1) % NB)
            out(T - 1, (T - 1) % NB)
            dve.wait_ge(act_out, T)
            dve.wait_ge(dve_out, T)
            with dve.Fori(0, T) as c:
                dve.tensor_copy(diag[:, ds(c, 1), :], adjT[:, ds(c, 1), ds(c * P, P)]).then_inc(kept, 1)
            dve.wait_ge(kept, T)
            with dve.Fori(0, T) as c:
                dve.tensor_tensor(adjT[:, ds(c, 1), ds(c * P, P)], diag[:, ds(c, 1), :], ident16[:, :].unsqueeze(1), ALU.max)

        @block.tensor
        def _(pe):
            def step(t, p):
                pe.wait_ge(masked, t + 1)
                if past(t, NB):
                    pe.wait_ge(act_out, t - NB + 1)
                    pe.wait_ge(dve_out, t - NB + 1)
                for c in range(T):
                    last = pe.transpose(flipped[p][:, c, :], mask[p][:, c * P:(c + 1) * P], ident16[:, :])
                last.then_inc(turned, 1)

            each(pe, T, NB, step)

        @block.scalar
        def _(act):
            def step(t, p):
                act.wait_ge(turned, t + 1)
                act.activation(adjT[:, 0:half, ds(t * P, P)], flipped[p][:, 0:half, :], ACT.Copy).then_inc(act_out, 1)

            each(act, T, NB, step)


def project_gnn(nc, hT, WT, wh_hi, wh_lo, whT_hi, whT_lo, norm_row, norm_col, ones):
    NB = 2
    with ExitStack() as ctx:
        s = Scope(nc, ctx, "wh_")
        junk = [s.sb(f"junk{i}", [P, D]) for i in range(NB)]
        squares = s.sb("squares", [P, T])
        sqT = [[s.sb(f"sqT{b}{d}", [P, GN]) for d in range(KD)] for b in range(2)]
        prod = [s.ps(f"prod{i}", [P, 512]) for i in range(NB)]
        prodT = [s.ps(f"prodT{i}", [P, GN]) for i in range(KD)]
        sums = s.ps("sums", [P, GN])
        made, sq_done, hi_done, lo_done = (s.sem(n) for n in ("made", "sq", "hi", "lo"))
        madeT, sqT_done, hiT_done, loT_done, sums_done, sums_out = (
            s.sem(n) for n in ("madeT", "sqT", "hiT", "loT", "sums", "sums_out"))
        (hT_hi, hT_lo), (WT_hi, WT_lo) = hT, WT
        block = ctx.enter_context(nc.Block())

        @block.tensor
        def _(pe):
            def tile(t, p):
                if past(t, NB):
                    pe.wait_ge(lo_done, t - NB + 1)
                for k in range(KD):
                    last = matmul3(pe, prod[p][:, 0:D], hT_hi[:, k, ds(t * P, P)], hT_lo[:, k, ds(t * P, P)],
                                   WT_hi[:, k, :], WT_lo[:, k, :], k == 0, k == KD - 1)
                last.then_inc(made, 1)

            each(pe, T, NB, tile)
            for g in range(G):
                for d in range(KD):
                    if g:
                        pe.wait_ge(loT_done, KD * (g - 1) + d + 1)
                    for k in range(KD):
                        dd, gg = slice(d * P, (d + 1) * P), slice(g * GN, (g + 1) * GN)
                        last = matmul3(pe, prodT[d][:, :], WT_hi[:, k, dd], WT_lo[:, k, dd],
                                       hT_hi[:, k, gg], hT_lo[:, k, gg], k == 0, k == KD - 1)
                    last.then_inc(madeT, 1)
                if g:
                    pe.wait_ge(sums_out, g)
                for d in range(KD):
                    pe.wait_ge(sqT_done, KD * g + d + 1)
                    last = pe.matmul(sums[:, :], lhsT=ones[:, :], rhs=sqT[g % 2][d][:, :], start=d == 0, stop=d == KD - 1)
                last.then_inc(sums_done, 1)

        @block.scalar
        def _(act):
            def tile(t, p):
                act.wait_ge(made, t + 1)
                if past(t, NB):
                    act.wait_ge(sq_done, t - NB + 1)
                act.activation(junk[p][:, :], prod[p][:, 0:D], ACT.Square, scale=UNWS,
                               accum_out=squares[:, ds(t, 1)]).then_inc(sq_done, 1)
                act.activation(wh_hi[:, ds(t, 1), 0:D], prod[p][:, 0:D].unsqueeze(1), ACT.Copy, scale=UNWS).then_inc(hi_done, 1)

            each(act, T, NB, tile)
            for g in range(G):
                for d in range(KD):
                    act.wait_ge(madeT, KD * g + d + 1)
                    if g >= 2:
                        act.wait_ge(sums_done, g - 1)
                    act.activation(sqT[g % 2][d][:, :], prodT[d][:, :], ACT.Square, scale=UNWS).then_inc(sqT_done, 1)
                    act.activation(whT_hi[:, d, g * GN:(g + 1) * GN], prodT[d][:, :], ACT.Copy, scale=UNWS).then_inc(hiT_done, 1)
                act.wait_ge(sums_done, g + 1)
                act.activation(norm_row[:, g * GN:(g + 1) * GN], sums[:, :], ACT.Copy).then_inc(sums_out, 1)
            act.wait_ge(sums_out, G)
            act.activation(norm_row[:, 0:N], norm_row[:, 0:N], ACT.Sqrt)
            act.wait_ge(sq_done, T)
            act.activation(norm_col[:, :], squares[:, :], ACT.Sqrt)

        @block.vector
        def _(dve):
            dve.memset(wh_hi[:, :, D:D + 1], 1.0)
            dve.memset(norm_row[:, N:N + GN], 1.0)

            def tile(t, p):
                dve.wait_ge(hi_done, t + 1)
                dve.scalar_tensor_tensor(wh_lo[:, ds(t, 1), :], prod[p][:, 0:D].unsqueeze(1), UNWS,
                                         wh_hi[:, ds(t, 1), 0:D], ALU.mult, ALU.subtract).then_inc(lo_done, 1)

            each(dve, T, NB, tile)
            for g in range(G):
                gg = slice(g * GN, (g + 1) * GN)
                for d in range(KD):
                    dve.wait_ge(hiT_done, KD * g + d + 1)
                    dve.scalar_tensor_tensor(whT_lo[:, d, gg], prodT[d][:, :], UNWS, whT_hi[:, d, gg],
                                             ALU.mult, ALU.subtract).then_inc(loT_done, 1)


def cosine_attention(nc, x, wh_hi, wh_lo, whT_hi, whT_lo, norm_row, norm_col, adjT):
    NB, LAG, RB, BATCH = 8, 6, 4, T // 2
    with ExitStack() as ctx:
        s = Scope(nc, ctx, "cos_")
        log_den = s.sb("log_den", [P, T, GN])
        eps = s.sb("eps", [P, 1])
        rec = [s.sb(f"rec{i}", [P, GN]) for i in range(RB)]
        sim = [s.sb(f"sim{i}", [P, GN]) for i in range(2)]
        ex = [s.sb(f"ex{i}", [P, GN]) for i in range(2)]
        em = [s.sb(f"em{i}", [P, GN]) for i in range(2)]
        e_hi = [s.sb(f"e_hi{i}", [P, GN], F16) for i in range(NB)]
        e_lo = [s.sb(f"e_lo{i}", [P, GN], F16) for i in range(NB)]
        inv = s.sb("inv", [P, TG])
        dots = [s.ps(f"dots{i}", [P, GN]) for i in range(4)]
        out = [s.ps(f"out{i}", [P, 512]) for i in range(TG)]
        dots_done, eps_set, log_done, rec_done, sim_done, ex_done, em_done, hi_done, lo_done, out_done, inv_done, added = (
            s.sem(n) for n in ("dots", "eps", "log", "rec", "sim", "ex", "em", "hi", "lo", "out", "inv", "added"))
        block = ctx.enter_context(nc.Block())

        @block.tensor
        def _(pe):
            def scores(g, c):
                u = T * g + c
                if past(u, 4):
                    pe.wait_ge(sim_done, u - 3)
                for k in range(KD):
                    cc, gg = slice(c * P, (c + 1) * P), ds(g * GN, GN)
                    last = matmul3(pe, dots[c % 4][:, :], whT_hi[:, k, cc], whT_lo[:, k, cc],
                                   whT_hi[:, k, gg], whT_lo[:, k, gg], k == 0, k == KD - 1)
                last.then_inc(dots_done, 1)

            def weigh(g, c):
                u = T * g + c
                pe.wait_ge(lo_done, u + 1)
                if c == 0 and past(g, 1):
                    pe.wait_ge(added, TG * g)
                for q in range(TG):
                    qq = slice(q * P, (q + 1) * P)
                    pe.matmul(out[q][:, 0:D + 1], lhsT=e_hi[c % NB][:, qq], rhs=wh_hi[:, c, 0:D + 1], start=c == 0, stop=False)
                    pe.matmul(out[q][:, 0:D], lhsT=e_hi[c % NB][:, qq], rhs=wh_lo[:, c, :], start=False, stop=False)
                    last = pe.matmul(out[q][:, 0:D + 1], lhsT=e_lo[c % NB][:, qq], rhs=wh_hi[:, c, 0:D + 1], start=False, stop=c == T - 1)
                last.then_inc(out_done, 1)

            def group(g, _):
                for c in range(T):
                    scores(g, c)
                    if c >= LAG:
                        weigh(g, c - LAG)
                    elif past(g, 1):
                        weigh(g - 1, T - LAG + c)

            each(pe, G, 1, group)
            for c in range(T - LAG, T):
                weigh(G - 1, c)

        @block.scalar
        def _(act):
            def logarithms(g, first):
                for c in range(first, first + BATCH):
                    act.activation(log_den[:, c, :], norm_row[:, ds(g * GN, GN)], ACT.Ln, scale=norm_col[:, c:c + 1],
                                   bias=eps[:, :]).then_inc(log_done, 1)

            def inverse(g, c):
                u = T * g + c
                if past(u, RB):
                    act.wait_ge(sim_done, u - RB + 1)
                act.wait_ge(log_done, u + 1)
                act.activation(rec[c % RB][:, :], log_den[:, c, :], ACT.Exp, scale=-1.0).then_inc(rec_done, 1)

            def expo(g, c):
                u = T * g + c
                act.wait_ge(sim_done, u + 1)
                if past(u, 2):
                    act.wait_ge(em_done, u - 1)
                act.activation(ex[c % 2][:, :], sim[c % 2][:, :], ACT.Exp).then_inc(ex_done, 1)

            def high(g, c):
                u = T * g + c
                act.wait_ge(em_done, u + 1)
                if past(u, NB):
                    act.wait_ge(out_done, u - NB + 1)
                act.activation(e_hi[c % NB][:, :], em[c % 2][:, :], ACT.Copy).then_inc(hi_done, 1)

            def lagged(g, c, lag, do):
                if c >= lag:
                    do(g, c - lag)
                elif past(g, 1):
                    do(g - 1, c - lag + T)

            def group(g, _):
                for c in range(T):
                    turn = c == 2 or c == BATCH + 2
                    if turn and past(T * g + c, BATCH):
                        act.wait_ge(rec_done, T * g + c - 2)
                    inverse(g, c)
                    lagged(g, c, 2, expo)
                    lagged(g, c, 3, high)
                    if turn:
                        logarithms(g + c // BATCH, BATCH + 2 - c)

            act.wait_ge(eps_set, 1)
            logarithms(0, 0)
            each(act, G, 1, group)
            for c in range(T - 2, T):
                expo(G - 1, c)
                high(G - 1, c - 1)
            high(G - 1, T - 1)

        @block.vector
        def _(dve):
            dve.memset(eps[:, :], SIM_EPS).then_inc(eps_set, 1)

            def similarity(g, c):
                u, b = T * g + c, c % 2
                dve.wait_ge(rec_done, u + 1)
                dve.wait_ge(dots_done, u + 1)
                if past(u, 2):
                    dve.wait_ge(ex_done, u - 1)
                dve.tensor_tensor(sim[b][:, :], dots[c % 4][:, :], rec[c % RB][:, :], ALU.mult).then_inc(sim_done, 1)

            def mask(g, c):
                u, b = T * g + c, c % 2
                dve.wait_ge(ex_done, u + 1)
                if past(u, 2):
                    dve.wait_ge(lo_done, u - 1)
                dve.tensor_tensor(em[b][:, :], ex[b][:, :], adjT[:, c, ds(g * GN, GN)], ALU.mult).then_inc(em_done, 1)

            def low(g, c):
                u = T * g + c
                dve.wait_ge(hi_done, u + 1)
                dve.tensor_tensor(e_lo[c % NB][:, :], em[c % 2][:, :], e_hi[c % NB][:, :], ALU.subtract).then_inc(lo_done, 1)

            def add(g):
                dve.wait_ge(out_done, T * g + T)
                for q in range(TG):
                    dve.reciprocal(inv[:, q:q + 1], out[q][:, D:D + 1]).then_inc(inv_done, 1)
                for q in range(TG):
                    dve.wait_ge(inv_done, TG * g + q + 1)
                    dve.scalar_tensor_tensor(x[:, ds(TG * g + q, 1), :], out[q][:, 0:D].unsqueeze(1), inv[:, q:q + 1],
                                             x[:, ds(TG * g + q, 1), :], ALU.mult, ALU.add).then_inc(added, 1)

            def group(g, _):
                for c in range(T):
                    similarity(g, c)
                    if c >= 1:
                        mask(g, c - 1)
                    elif past(g, 1):
                        mask(g - 1, T - 1)
                    if c >= 2:
                        low(g, c - 2)
                    elif past(g, 1):
                        low(g - 1, T - 2 + c)
                    if c == LAG and past(g, 1):
                        add(g - 1)

            each(dve, G, 1, group)
            mask(G - 1, T - 1)
            low(G - 1, T - 2)
            low(G - 1, T - 1)
            add(G - 1)


def l0_gnn(nc, a, x, ident, ident16, ones, adjT, diag):
    with ExitStack() as ctx:
        s = Scope(nc, ctx, "g0_")
        wh_hi, wh_lo = s.sb("wh_hi", [P, T, D + 2], F16), s.sb("wh_lo", [P, T, D], F16)
        whT_hi, whT_lo = s.sb("whT_hi", [P, KD, N], F16), s.sb("whT_lo", [P, KD, N], F16)
        norm_row, norm_col = s.sb("norm_row", [P, N + GN]), s.sb("norm_col", [P, T])
        with ExitStack() as inner:
            s = Scope(nc, inner, "g0_")
            hT = s.sb("hT_hi", [P, KD, N], F16), s.sb("hT_lo", [P, KD, N], F16)
            WT = s.sb("WT_hi", [P, KD, D], F16), s.sb("WT_lo", [P, KD, D], F16)
            split_transposed_weights(nc, "g0w_", ident, [(a["L0_gnn_W"], WT[0][:, :, :], WT[1][:, :, :])])
            normalize_and_turn(nc, "g0n_", ident, x, D, "layer", *hT)
            project_gnn(nc, hT, WT, wh_hi, wh_lo, whT_hi, whT_lo, norm_row, norm_col, ones)
        cosine_attention(nc, x, wh_hi, wh_lo, whT_hi, whT_lo, norm_row, norm_col, adjT)


def route(nc, prefix, ident, experts, top, hT, Wg, bias, comb, b2=None, x=None):
    with ExitStack() as ctx:
        s = Scope(nc, ctx, prefix)
        shape = [P, T, experts]
        rank_i, rank = s.sb("rank_i", [P, experts], I32), s.sb("rank", [P, experts])
        scores, work, same, chosen = (s.sb(n, shape) for n in ("scores", "work", "same", "chosen"))
        best, first, peak = s.sb("best", [P, T]), s.sb("first", [P, T]), s.sb("peak", [P, T])
        logits = s.ps("logits", shape)
        made, rank_done, loaded, steps, ready, squashed = (s.sem(n) for n in ("made", "rank", "loaded", "steps", "ready", "squashed"))
        (hT_hi, hT_lo), (Wg_hi, Wg_lo) = hT, Wg
        over = lambda row: row.unsqueeze(1).to_broadcast(shape)
        along = lambda col: col.unsqueeze(2).to_broadcast(shape)
        if bias is not None:
            bias_sb = s.sb("bias", [P, experts])
        if b2 is not None:
            b2_sb = s.sb("b2", [experts, D])
            combT = s.sb("combT", [experts, T, P])
            combT_ps = s.ps("combT_ps", [experts, T, P])
            extra = [s.ps(f"extra{i}", [P, D]) for i in range(2)]
            comb_done, combT_done, combT_out, extra_done, added = (
                s.sem(n) for n in ("comb", "combT", "combT_out", "extra", "added"))
        block = ctx.enter_context(nc.Block())

        @block.sync
        def _(sp):
            if bias is not None:
                sp.dma_start(bias_sb[:, :], bias.unsqueeze(0).to_broadcast([P, experts])).then_inc(loaded, 16)
            if b2 is not None:
                sp.dma_start(b2_sb[:, :], b2).then_inc(loaded, 16)

        @block.gpsimd
        def _(pool):
            pool.iota(rank_i[:, :], pattern=[[-1, experts]], base=experts, channel_multiplier=0).then_inc(rank_done, 1)

        @block.tensor
        def _(pe):
            def step(t, p):
                for k in range(KD):
                    last = matmul3(pe, logits[:, ds(t, 1), :], hT_hi[:, k, ds(t * P, P)], hT_lo[:, k, ds(t * P, P)],
                                   Wg_hi[:, k, :], Wg_lo[:, k, :], k == 0, k == KD - 1)
                last.then_inc(made, 1)

            each(pe, T, 1, step)
            if b2 is not None:
                pe.wait_ge(comb_done, 1)
                for t in range(T):
                    last = pe.transpose(combT_ps[:, t, :], comb[:, t, :], ident[:, :])
                last.then_inc(combT_done, 1)
                pe.wait_ge(combT_out, 1)
                for t in range(T):
                    if t >= 2:
                        pe.wait_ge(added, t - 1)
                    pe.matmul(extra[t % 2][:, :], lhsT=combT[:, t, :], rhs=b2_sb[:, :], start=True, stop=True).then_inc(extra_done, 1)

        @block.scalar
        def _(act):
            act.wait_ge(ready, 1)
            if bias is None:
                act.activation(scores[:, :, :], logits[:, :, :], ACT.Sigmoid, scale=UNWS).then_inc(squashed, 1)
            else:
                act.activation(same[:, :, :], work[:, :, :], ACT.Exp).then_inc(squashed, 1)
            if b2 is not None:
                act.wait_ge(combT_done, 1)
                act.activation(combT[:, :, :], combT_ps[:, :, :], ACT.Copy).then_inc(combT_out, 1)

        @block.vector
        def _(dve):
            link = Chain(dve, steps)
            dve.wait_ge(rank_done, 1)
            link(dve.tensor_copy(rank[:, :], rank_i[:, :]))
            dve.wait_ge(made, T)
            if bias is None:
                dve.engine_nop().then_inc(ready, 1)
                dve.wait_ge(squashed, 1)
            else:
                dve.wait_ge(loaded, 16 if b2 is None else 32)
                link(dve.scalar_tensor_tensor(scores[:, :, :], logits[:, :, :], UNWS, over(bias_sb[:, :]), ALU.mult, ALU.add))
            link(dve.tensor_copy(work[:, :, :], scores[:, :, :]))
            link(dve.memset(chosen[:, :, :], 0.0))
            for k in range(top):
                peak_k = first if k == 0 else peak
                link(dve.tensor_reduce(peak_k[:, :], work[:, :, :], AXF, ALU.max))
                link(dve.tensor_tensor(same[:, :, :], work[:, :, :], along(peak_k[:, :]), ALU.is_equal))
                link(dve.tensor_tensor(same[:, :, :], same[:, :, :], over(rank[:, :]), ALU.mult))
                link(dve.tensor_reduce(best[:, :], same[:, :, :], AXF, ALU.max))
                link(dve.tensor_tensor(same[:, :, :], over(rank[:, :]), along(best[:, :]), ALU.is_equal))
                link(dve.tensor_tensor(chosen[:, :, :], chosen[:, :, :], same[:, :, :], ALU.add))
                link(dve.scalar_tensor_tensor(work[:, :, :], same[:, :, :], -BIG, work[:, :, :], ALU.mult, ALU.add))
            if bias is None:
                link(dve.tensor_tensor(comb[:, :, :], scores[:, :, :], chosen[:, :, :], ALU.mult))
            else:
                link(dve.tensor_tensor(work[:, :, :], scores[:, :, :], along(first[:, :]), ALU.subtract))
                dve.engine_nop().then_inc(ready, 1)
                dve.wait_ge(squashed, 1)
                link(dve.tensor_tensor(comb[:, :, :], same[:, :, :], chosen[:, :, :], ALU.mult))
            link(dve.tensor_reduce(peak[:, :], comb[:, :, :], AXF, ALU.add))
            link(dve.reciprocal(best[:, :], peak[:, :]))
            link(dve.tensor_tensor(comb[:, :, :], comb[:, :, :], along(best[:, :]), ALU.mult))
            if b2 is not None:
                dve.engine_nop().then_inc(comb_done, 1)
                for t in range(T):
                    dve.wait_ge(extra_done, t + 1)
                    dve.tensor_tensor(x[:, t, :], extra[t % 2][:, :], x[:, t, :], ALU.add).then_inc(added, 1)
                dve.wait_ge(added, T)
                dve.wait_ge(combT_done, 1)
            dve.tensor_scalar(comb[:, :, :], comb[:, :, :], UNWS, None, ALU.mult)


def load_turned_bias(nc, prefix, ident, src, rows, biasT):
    with ExitStack() as ctx:
        s = Scope(nc, ctx, prefix)
        raw, flipped = s.sb("raw", [rows, P]), s.ps("flipped", [P, rows])
        loaded, turned = s.sem("loaded"), s.sem("turned")
        block = ctx.enter_context(nc.Block())

        @block.sync
        def _(sp):
            sp.dma_start(raw[:, :], src).then_inc(loaded, 16)

        @block.tensor
        def _(pe):
            pe.wait_ge(loaded, 16)
            pe.transpose(flipped[:, :], raw[:, :], ident[0:rows, 0:rows]).then_inc(turned, 1)

        @block.vector
        def _(dve):
            dve.wait_ge(turned, 1)
            dve.tensor_copy(biasT[:, :], flipped[:, :])


def l0_experts(nc, x, hT, W1, b1T, W2, comb):
    UB = 4
    with ExitStack() as ctx:
        s = Scope(nc, ctx, "e0_")
        raw1, raw2 = s.sb("raw1", [P, KD, L0_F]), s.sb("raw2", [P, FC, D])
        w1 = [(s.sb(f"w1_hi{i}", [P, KD, L0_F], F16), s.sb(f"w1_lo{i}", [P, KD, L0_F], F16)) for i in range(2)]
        w2 = [(s.sb(f"w2_hi{i}", [P, FC, D], F16), s.sb(f"w2_lo{i}", [P, FC, D], F16)) for i in range(2)]
        b1 = [s.sb(f"b1_{i}", [P, FC]) for i in range(2)]
        act_out = [s.sb(f"act{i}", [P, GN]) for i in range(UB)]
        hid = [(s.sb(f"hid_hi{i}", [P, FC, GN], F16), s.sb(f"hid_lo{i}", [P, FC, GN], F16)) for i in range(2)]
        up = [s.ps(f"up{i}", [P, GN]) for i in range(UB)]
        down = [s.ps(f"down{i}", [P, 512]) for i in range(TG)]
        loaded, w_hi, w_lo, up_done, act_done, hi_done, lo_done, down_done, added, b1_done = (
            s.sem(n) for n in ("loaded", "w_hi", "w_lo", "up", "act", "hi", "lo", "down", "added", "b1"))
        hT_hi, hT_lo = hT
        block = ctx.enter_context(nc.Block())

        @block.sync
        def _(sp):
            for e in range(L0_E):
                if e:
                    sp.wait_ge(w_lo, 2 * e)
                sp.dma_start(raw1[:, :, :], W1[e].rearrange("(k p) f -> p k f", p=P)).then_inc(loaded, 16)
                sp.dma_start(raw2[:, :, :], W2[e].rearrange("(k p) d -> p k d", p=P)).then_inc(loaded, 16)

        @block.tensor
        def _(pe):
            def project_up(e, g, p):
                u = G * e + g
                if g == 0:
                    pe.wait_ge(w_lo, 2 * e + 2)
                for f in range(FC):
                    n = FC * u + f
                    if past(n, UB):
                        pe.wait_ge(act_done, n - UB + 1)
                    ff, gg = slice(f * P, (f + 1) * P), slice(g * GN, (g + 1) * GN)
                    for k in range(KD):
                        last = matmul3(pe, up[f % UB][:, :], w1[p][0][:, k, ff], w1[p][1][:, k, ff],
                                       hT_hi[:, k, gg], hT_lo[:, k, gg], k == 0, k == KD - 1)
                    last.then_inc(up_done, 1)

            def project_down(e, g, p):
                u = G * e + g
                pe.wait_ge(lo_done, FC * u + FC)
                for q in range(TG):
                    if past(u, 1):
                        pe.wait_ge(added, TG * (u - 1) + q + 1)
                    qq = slice(q * P, (q + 1) * P)
                    for f in range(FC):
                        last = matmul3(pe, down[q][:, 0:D], hid[g % 2][0][:, f, qq], hid[g % 2][1][:, f, qq],
                                       w2[p][0][:, f, :], w2[p][1][:, f, :], f == 0, f == FC - 1)
                    last.then_inc(down_done, 1)

            def expert(e, p):
                for g in range(G):
                    project_up(e, g, p)
                    if g:
                        project_down(e, g - 1, p)
                    elif past(e, 1):
                        project_down(e - 1, G - 1, 1 - p)

            each(pe, L0_E, 2, expert)
            project_down(L0_E - 1, G - 1, (L0_E - 1) % 2)

        @block.scalar
        def _(act):
            def expert(e, p):
                act.wait_ge(loaded, 32 * e + 32)
                if past(e, 2):
                    act.wait_ge(down_done, TG * G * (e - 1))
                act.activation(w1[p][0][:, :, :], raw1[:, :, :], ACT.Copy, scale=WS).then_inc(w_hi, 1)
                act.activation(w2[p][0][:, :, :], raw2[:, :, :], ACT.Copy, scale=WS).then_inc(w_hi, 1)
                act.wait_ge(b1_done, e + 1)
                for g in range(G):
                    for f in range(FC):
                        n = FC * (G * e + g) + f
                        act.wait_ge(up_done, n + 1)
                        if past(n, UB):
                            act.wait_ge(lo_done, n - UB + 1)
                        act.activation(act_out[f % UB][:, :], up[f % UB][:, :], ACT.Silu, bias=b1[p][:, f:f + 1],
                                       scale=UNWS).then_inc(act_done, 1)

            each(act, L0_E, 2, expert)

        @block.vector
        def _(dve):
            def hidden(e, g):
                u = G * e + g
                if past(u, 2):
                    dve.wait_ge(down_done, TG * (u - 1))
                for f in range(FC):
                    n = FC * u + f
                    dve.wait_ge(act_done, n + 1)
                    dve.tensor_copy(hid[g % 2][0][:, f, :], act_out[f % UB][:, :]).then_inc(hi_done, 1)
                    dve.wait_ge(hi_done, n + 1)
                    dve.tensor_tensor(hid[g % 2][1][:, f, :], act_out[f % UB][:, :], hid[g % 2][0][:, f, :],
                                      ALU.subtract).then_inc(lo_done, 1)

            def add(e, g):
                u = G * e + g
                for q in range(TG):
                    n = TG * u + q
                    dve.wait_ge(down_done, n + 1)
                    if past(u, G):
                        dve.wait_ge(added, n - TG * G + 1)
                    dve.scalar_tensor_tensor(x[:, TG * g + q, :], down[q][:, 0:D], comb[:, TG * g + q, ds(e, 1)],
                                             x[:, TG * g + q, :], ALU.mult, ALU.add).then_inc(added, 1)

            def expert(e, p):
                dve.tensor_scalar(b1[p][:, :], b1T[:, ds(FC * e, FC)], 1.0, None, ALU.mult).then_inc(b1_done, 1)
                dve.wait_ge(w_hi, 2 * e + 2)
                dve.scalar_tensor_tensor(w1[p][1][:, :, :], raw1[:, :, :], WS, w1[p][0][:, :, :], ALU.mult,
                                         ALU.subtract).then_inc(w_lo, 1)
                dve.scalar_tensor_tensor(w2[p][1][:, :, :], raw2[:, :, :], WS, w2[p][0][:, :, :], ALU.mult,
                                         ALU.subtract).then_inc(w_lo, 1)
                for g in range(G):
                    hidden(e, g)
                    if g:
                        add(e, g - 1)
                    elif past(e, 1):
                        add(e - 1, G - 1)

            each(dve, L0_E, 2, expert)
            add(L0_E - 1, G - 1)


def l0_ffn(nc, a, x, ident):
    with ExitStack() as ctx:
        s = Scope(nc, ctx, "f0_")
        hT = s.sb("hT_hi", [P, KD, N], F16), s.sb("hT_lo", [P, KD, N], F16)
        Wg = s.sb("Wg_hi", [P, KD, L0_E], F16), s.sb("Wg_lo", [P, KD, L0_E], F16)
        comb, b1T = s.sb("comb", [P, T, L0_E]), s.sb("b1T", [P, L0_E * FC])
        load_turned_bias(nc, "f0b_", ident, a["L0_ffn_b1"].rearrange("e (f p) -> (e f) p", p=P), L0_E * FC, b1T)
        split_weights(nc, "f0w_", [(a["L0_ffn_Wg"].rearrange("(k p) e -> p k e", p=P), None, Wg[0][:, :, :], Wg[1][:, :, :])])
        normalize_and_turn(nc, "f0n_", ident, x, D, "layer", *hT)
        route(nc, "f0r_", ident, L0_E, L0_K, hT, Wg, a["L0_ffn_bg"], comb, a["L0_ffn_b2"], x)
        l0_experts(nc, x, hT, a["L0_ffn_W1"], b1T, a["L0_ffn_W2"], comb)


def keep_first_neighbors(nc, adjT, diag, upper, ones16):
    with ExitStack() as ctx:
        s = Scope(nc, ctx, "keep_")
        before = [s.sb(f"before{i}", [P, N], F16) for i in range(2)]
        count = [s.ps(f"count{i}", [P, GN]) for i in range(8)]
        restored, cleared, summed, counted, kept = (s.sem(n) for n in ("restored", "cleared", "summed", "counted", "kept"))
        block = ctx.enter_context(nc.Block())

        @block.tensor
        def _(pe):
            def chunk(c, p):
                if not past(c, 1):
                    pe.wait_ge(restored, T)
                    pe.wait_ge(cleared, 1)
                else:
                    pe.wait_ge(summed, c)
                for g in range(G):
                    n = G * c + g
                    if past(n, 8):
                        pe.wait_ge(kept, n - 7)
                    gg = slice(g * GN, (g + 1) * GN)
                    b = G * (p % 2) + g
                    pe.matmul(count[b][:, :], lhsT=upper[:, :], rhs=adjT[:, ds(c, 1), gg], start=True, stop=False)
                    pe.matmul(count[b][:, :], lhsT=ones16[:, :], rhs=before[p % 2][:, gg], start=False, stop=True).then_inc(counted, 1)

            each(pe, T, 2, chunk)

        @block.vector
        def _(dve):
            with dve.Fori(0, T) as c:
                dve.tensor_copy(adjT[:, ds(c, 1), ds(c * P, P)], diag[:, ds(c, 1), :]).then_inc(restored, 1)
            dve.wait_ge(restored, T)
            dve.memset(before[0][:, :], 0.0).then_inc(cleared, 1)
            dve.wait_ge(cleared, 1)

            def chunk(c, p):
                if past(c, 1):
                    dve.wait_ge(summed, c)
                    dve.wait_ge(counted, G * c)
                dve.tensor_tensor(before[1 - p % 2][:, :].unsqueeze(1), before[p % 2][:, :].unsqueeze(1), adjT[:, ds(c, 1), :],
                                  ALU.add).then_inc(summed, 1)
                dve.wait_ge(summed, c + 1)
                for g in range(G):
                    b, gg = G * (p % 2) + g, slice(g * GN, (g + 1) * GN)
                    dve.wait_ge(counted, G * c + g + 1)
                    dve.scalar_tensor_tensor(adjT[:, ds(c, 1), gg], count[b][:, :].unsqueeze(1), float(NEIGHBORS),
                                             adjT[:, ds(c, 1), gg], ALU.is_le, ALU.mult).then_inc(kept, 1)

            each(dve, T, 2, chunk)


def neighbor_mean(nc, keep, xn_hi, xn_lo, mean, has):
    NB = 4
    with ExitStack() as ctx:
        s = Scope(nc, ctx, "mean_")
        inv, cnt = [s.sb(f"inv{i}", [P, 1]) for i in range(NB)], [s.sb(f"cnt{i}", [P, 1]) for i in range(NB)]
        total = [s.ps(f"total{i}", [P, 512]) for i in range(NB)]
        summed, counted, inverted, used = (s.sem(n) for n in ("summed", "counted", "inverted", "used"))
        block = ctx.enter_context(nc.Block())

        @block.tensor
        def _(pe):
            def tile(t, p):
                if past(t, NB):
                    pe.wait_ge(used, t - NB + 1)
                for c in range(T):
                    pe.matmul(total[p][:, 0:D + 1], lhsT=keep[:, c, ds(t * P, P)], rhs=xn_hi[:, c, 0:D + 1], start=c == 0, stop=False)
                    last = pe.matmul(total[p][:, 0:D], lhsT=keep[:, c, ds(t * P, P)], rhs=xn_lo[:, c, :], start=False, stop=c == T - 1)
                last.then_inc(summed, 1)

            each(pe, T, NB, tile)

        @block.vector
        def _(dve):
            def tile(t, p):
                if past(t, NB):
                    dve.wait_ge(used, t - NB + 1)
                dve.wait_ge(summed, t + 1)
                dve.tensor_scalar(has[:, ds(t, 1)], total[p][:, D:D + 1], 0.0, None, ALU.is_gt)
                dve.tensor_scalar(cnt[p][:, :], total[p][:, D:D + 1], 1.0, None, ALU.max).then_inc(counted, 1)
                dve.wait_ge(counted, t + 1)
                dve.reciprocal(inv[p][:, :], cnt[p][:, :]).then_inc(inverted, 1)
                dve.wait_ge(inverted, t + 1)
                dve.tensor_scalar(mean[:, ds(t, 1), :], total[p][:, 0:D].unsqueeze(1), inv[p][:, :], None, ALU.mult).then_inc(used, 1)

            each(dve, T, NB, tile)


def gnn_outputs(nc, a, x, xnT, meanT, W_line, W_nb, has):
    NB = 4
    with ExitStack() as ctx:
        s = Scope(nc, ctx, "go_")
        biases = [s.sb(n, [P, D]) for n in ("b_line", "b_nb")]
        val = [[s.sb(f"val{j}{i}", [P, D]) for i in range(NB)] for j in range(2)]
        leaky = [[s.sb(f"leaky{j}{i}", [P, D]) for i in range(NB)] for j in range(2)]
        prod = [[s.ps(f"prod{j}{i}", [P, 512]) for i in range(NB)] for j in range(2)]
        loaded, made, biased, bent, added = (s.sem(n) for n in ("loaded", "made", "biased", "bent", "added"))
        block = ctx.enter_context(nc.Block())

        @block.sync
        def _(sp):
            for b, src in zip(biases, (a["L1_gnn_b_line"], a["L1_gnn_b_nb"])):
                sp.dma_start(b[:, :], src.unsqueeze(0).to_broadcast([P, D])).then_inc(loaded, 16)

        @block.tensor
        def _(pe):
            def tile(t, p):
                for j, (hT, W) in enumerate(((xnT, W_line), (meanT, W_nb))):
                    if past(t, NB):
                        pe.wait_ge(biased, 2 * (t - NB) + j + 1)
                    for k in range(KD):
                        last = matmul3(pe, prod[j][p][:, 0:D], hT[0][:, k, ds(t * P, P)], hT[1][:, k, ds(t * P, P)],
                                       W[0][:, k, :], W[1][:, k, :], k == 0, k == KD - 1)
                    last.then_inc(made, 1)

            each(pe, T, NB, tile)

        @block.vector
        def _(dve):
            dve.wait_ge(loaded, 32)

            def tile(t, p):
                for j in range(2):
                    dve.wait_ge(made, 2 * t + j + 1)
                    dve.scalar_tensor_tensor(val[j][p][:, :], prod[j][p][:, 0:D], UNWS, biases[j][:, :], ALU.mult,
                                             ALU.add).then_inc(biased, 1)
                for j in range(2):
                    dve.wait_ge(biased, 2 * t + j + 1)
                    dve.scalar_tensor_tensor(leaky[j][p][:, :], val[j][p][:, :], 0.01, val[j][p][:, :], ALU.mult,
                                             ALU.max).then_inc(bent, 1)
                xt = x[:, ds(t, 1), :]
                dve.wait_ge(bent, 2 * t + 1)
                dve.tensor_tensor(xt, leaky[0][p][:, :].unsqueeze(1), xt, ALU.add).then_inc(added, 1)
                dve.wait_ge(bent, 2 * t + 2)
                dve.wait_ge(added, 2 * t + 1)
                dve.scalar_tensor_tensor(xt, leaky[1][p][:, :].unsqueeze(1), has[:, ds(t, 1)], xt, ALU.mult, ALU.add).then_inc(added, 1)

            each(dve, T, NB, tile)


def make_triangle(nc, upper, ones16):
    with ExitStack() as ctx:
        s = Scope(nc, ctx, "tri_")
        filled = s.sem("filled")
        block = ctx.enter_context(nc.Block())

        @block.gpsimd
        def _(pool):
            pool.memset(ones16[:, :], 1.0)
            pool.memset(upper[:, :], 1.0).then_inc(filled, 1)
            pool.wait_ge(filled, 1)
            pool.affine_select(out=upper[:, :], in_=upper[:, :], compare_op=ALU.is_ge, fill=0.0, base=0,
                               pattern=[[1, P]], channel_multiplier=-1)


def l1_gnn(nc, a, x, ident, adjT, diag):
    with ExitStack() as ctx:
        s = Scope(nc, ctx, "g1_")
        xnT = s.sb("xnT_hi", [P, KD, N], F16), s.sb("xnT_lo", [P, KD, N], F16)
        meanT = s.sb("meanT_hi", [P, KD, N], F16), s.sb("meanT_lo", [P, KD, N], F16)
        xn_hi, xn_lo = s.sb("xn_hi", [P, T, D + 2], F16), s.sb("xn_lo", [P, T, D], F16)
        mean, has = s.sb("mean", [P, T, D]), s.sb("has", [P, T])
        W_line = s.sb("W_line_hi", [P, KD, D], F16), s.sb("W_line_lo", [P, KD, D], F16)
        W_nb = s.sb("W_nb_hi", [P, KD, D], F16), s.sb("W_nb_lo", [P, KD, D], F16)
        upper, ones16 = s.sb("upper", [P, P], F16), s.sb("ones16", [P, P], F16)
        make_triangle(nc, upper, ones16)
        split_transposed_weights(nc, "g1w_", ident, [(a["L1_gnn_W_line"], W_line[0][:, :, :], W_line[1][:, :, :]),
                                                     (a["L1_gnn_W_nb"], W_nb[0][:, :, :], W_nb[1][:, :, :])])
        normalize_and_turn(nc, "g1n_", ident, x, D, "layer", *xnT, tok_hi=xn_hi, tok_lo=xn_lo)
        keep_first_neighbors(nc, adjT, diag, upper, ones16)
        neighbor_mean(nc, adjT, xn_hi, xn_lo, mean, has)
        normalize_and_turn(nc, "g1m_", ident, mean, D, None, *meanT)
        gnn_outputs(nc, a, x, xnT, meanT, W_line, W_nb, has)


def latent_project(nc, a, xT, W_hi, W_lo, c_q, c_kv, k_rope, cos, sin):
    NB = 4
    with ExitStack() as ctx:
        s = Scope(nc, ctx, "lat_")
        raw_k = s.sb("raw_k", [P, T, ROPE])
        turned = s.sb("turned", [P, T, ROPE])
        prod = [s.ps(f"prod{i}", [P, 512]) for i in range(NB)]
        made, out_done, loaded, parts = (s.sem(n) for n in ("made", "out", "loaded", "parts"))
        block = ctx.enter_context(nc.Block())
        H = ROPE // 2

        @block.sync
        def _(sp):
            sp.dma_start(cos[:, :, :], a["rope_cos"].rearrange("(t p) d -> p t d", p=P)).then_inc(loaded, 16)
            sp.dma_start(sin[:, :, :], a["rope_sin"].rearrange("(t p) d -> p t d", p=P)).then_inc(loaded, 16)

        @block.tensor
        def _(pe):
            def tile(t, p):
                if past(t, NB):
                    pe.wait_ge(out_done, 3 * (t - NB) + 3)
                for k in range(KD):
                    last = matmul3(pe, prod[p][:, 0:DQ + DKV + ROPE], xT[0][:, k, ds(t * P, P)], xT[1][:, k, ds(t * P, P)],
                                   W_hi[:, k, :], W_lo[:, k, :], k == 0, k == KD - 1)
                last.then_inc(made, 1)

            each(pe, T, NB, tile)

        @block.scalar
        def _(act):
            def tile(t, p):
                act.wait_ge(made, t + 1)
                for dst, at, w in ((c_q, 0, DQ), (c_kv, DQ, DKV), (raw_k, DQ + DKV, ROPE)):
                    act.activation(dst[:, ds(t, 1), :], prod[p][:, at:at + w].unsqueeze(1), ACT.Copy, scale=UNWS).then_inc(out_done, 1)

            each(act, T, NB, tile)

        @block.vector
        def _(dve):
            dve.wait_ge(loaded, 32)
            dve.wait_ge(out_done, 3 * T)
            dve.tensor_tensor(turned[:, :, 0:H], raw_k[:, :, H:ROPE], sin[:, :, 0:H], ALU.mult).then_inc(parts, 1)
            dve.tensor_tensor(turned[:, :, H:ROPE], raw_k[:, :, 0:H], sin[:, :, H:ROPE], ALU.mult).then_inc(parts, 1)
            dve.tensor_tensor(k_rope[:, :, :], raw_k[:, :, :], cos[:, :, :], ALU.mult).then_inc(parts, 1)
            dve.wait_ge(parts, 3)
            dve.tensor_tensor(k_rope[:, :, :], k_rope[:, :, :], turned[:, :, :], ALU.add)


def queries_keys_values(nc, prefix, ident, cqT, ckvT, W_uq, W_ukv, k_rope, cos, sin, qT, kT, V, qk_dram, v_dram, first):
    H = ROPE // 2
    with ExitStack() as ctx:
        s = Scope(nc, ctx, prefix)
        tok = [[s.sb(f"tok{j}{i}", [P, HH, QK]) for i in range(2)] for j in range(2)]
        kept = [s.sb(f"kept{i}", [P, HH, ROPE]) for i in range(2)]
        swapped = [s.sb(f"swapped{i}", [P, HH, ROPE]) for i in range(2)]
        q_ps = [s.ps(f"q{i}", [P, HH, P]) for i in range(2)]
        kv_ps = [s.ps(f"kv{i}", [P, HH, 2 * UP]) for i in range(2)]
        flipped = [[s.ps(f"flipped{j}{i}", [P, HH, P]) for i in range(2)] for j in range(2)]
        q_made, kv_made, q_out, kv_out, v_lo, rot, rotated, k_ready, turned, hi_done, lo_done = (
            s.sem(n) for n in ("q_made", "kv_made", "q_out", "kv_out", "v_lo", "rot", "rotated", "k_ready",
                               "turned", "hi", "lo"))
        spilled, v_ones = s.sem("spilled"), s.sem("v_ones")
        block = ctx.enter_context(nc.Block())

        @block.sync
        def _(sp):
            heads = slice(first, first + HH)
            sp.wait_ge(v_ones, 1)
            for g in range(G):
                gg, tt = slice(g * GN, (g + 1) * GN), slice(g * TG, (g + 1) * TG)
                sp.wait_ge(v_lo, TG * (g + 1))
                for h in range(HH):
                    sp.dma_start(v_dram[first + h][:, tt, :], V[:, tt, h, :]).then_inc(spilled, 16)
                sp.wait_ge(lo_done, 2 * TG * (g + 1))
                for n, part in ((Q_HI, qT[0]), (K_HI, kT[0]), (Q_LO, qT[1]), (K_LO, kT[1])):
                    sp.dma_start(qk_dram[heads, :, n, gg].rearrange("h r s -> r h s"), part[0:QK, :, gg]).then_inc(spilled, 16)
            sp.wait_ge(spilled, 16 * G * (HH + 4))

        @block.tensor
        def _(pe):
            def turn(t, p):
                pe.wait_ge(rotated, t + 1)
                pe.wait_ge(k_ready, t + 1)
                pe.wait_ge(kv_out, t + 1)
                for j in range(2):
                    if past(t, 2):
                        pe.wait_ge(lo_done, 2 * (t - 2) + j + 1)
                    for h in range(HH):
                        last = pe.transpose(flipped[j][p][0:QK, h, :], tok[j][p][:, h, :], ident[:, :])
                    last.then_inc(turned, 1)

            def tile(t, p):
                p = p % 2
                if past(t, 2):
                    pe.wait_ge(q_out, t - 1)
                matmul3(pe, q_ps[p][:, :, :].rearrange("p h d -> p (h d)")[:, 0:HH * QK], cqT[0][:, 0, ds(t * P, P)],
                        cqT[1][:, 0, ds(t * P, P)], W_uq[0], W_uq[1], True, True).then_inc(q_made, 1)
                if past(t, 2):
                    pe.wait_ge(kv_out, t - 1)
                    pe.wait_ge(v_lo, t - 1)
                matmul3(pe, kv_ps[p][:, :, :], ckvT[0][:, 0, ds(t * P, P)], ckvT[1][:, 0, ds(t * P, P)],
                        W_ukv[0], W_ukv[1], True, True).then_inc(kv_made, 1)
                if past(t, 1):
                    turn(t - 1, 1 - p)

            each(pe, T, 4, tile)
            turn(T - 1, (T - 1) % 2)

        @block.scalar
        def _(act):
            def high(t, p):
                for j, dst in enumerate((qT, kT)):
                    act.wait_ge(turned, 2 * t + j + 1)
                    act.activation(dst[0][0:QK, :, ds(t * P, P)], flipped[j][p][0:QK, :, :], ACT.Copy).then_inc(hi_done, 1)

            def tile(t, p):
                p = p % 2
                act.wait_ge(q_made, t + 1)
                if past(t, 2):
                    act.wait_ge(turned, 2 * (t - 2) + 2)
                act.activation(tok[0][p][:, :, :].rearrange("p h d -> p (h d)"),
                               q_ps[p][:, :, :].rearrange("p h d -> p (h d)")[:, 0:HH * QK], ACT.Copy,
                               scale=UNWS * ATT_SCALE).then_inc(q_out, 1)
                act.wait_ge(kv_made, t + 1)
                act.activation(V[:, ds(t, 1), :, UP:2 * UP], kv_ps[p][:, :, UP:2 * UP].unsqueeze(1), ACT.Copy, scale=UNWS)
                act.activation(tok[1][p][:, :, 0:UP], kv_ps[p][:, :, 0:UP], ACT.Copy, scale=UNWS).then_inc(kv_out, 1)
                if past(t, 1):
                    high(t - 1, 1 - p)

            each(act, T, 4, tile)
            high(T - 1, (T - 1) % 2)

        @block.vector
        def _(dve):
            dve.memset(V[:, :, :, 2 * UP:2 * UP + 2], 1.0).then_inc(v_ones, 1)

            def low(t, p):
                for j, dst in enumerate((qT, kT)):
                    dve.wait_ge(hi_done, 2 * t + j + 1)
                    dve.tensor_tensor(dst[1][0:QK, :, ds(t * P, P)], flipped[j][p][0:QK, :, :], dst[0][0:QK, :, ds(t * P, P)],
                                      ALU.subtract).then_inc(lo_done, 1)

            def tile(t, p):
                p = p % 2
                r = tok[0][p][:, :, UP:QK]
                wide = lambda table: table.to_broadcast([P, HH, table.shape[-1]])
                if past(t, 2):
                    dve.wait_ge(turned, 2 * (t - 2) + 2)
                    dve.wait_ge(rotated, t - 1)
                dve.tensor_tensor(tok[1][p][:, :, UP:QK], wide(k_rope[:, ds(t, 1), :]), wide(k_rope[:, ds(t, 1), :]),
                                  ALU.max).then_inc(k_ready, 1)
                dve.wait_ge(q_out, t + 1)
                dve.tensor_tensor(kept[p][:, :, :], r, wide(cos[:, ds(t, 1), :]), ALU.mult).then_inc(rot, 1)
                dve.tensor_tensor(swapped[p][:, :, 0:H], r[:, :, H:ROPE], wide(sin[:, ds(t, 1), 0:H]), ALU.mult).then_inc(rot, 1)
                dve.tensor_tensor(swapped[p][:, :, H:ROPE], r[:, :, 0:H], wide(sin[:, ds(t, 1), H:ROPE]), ALU.mult).then_inc(rot, 1)
                dve.wait_ge(rot, 3 * t + 3)
                dve.tensor_tensor(r, kept[p][:, :, :], swapped[p][:, :, :], ALU.add).then_inc(rotated, 1)
                dve.wait_ge(kv_out, t + 1)
                dve.scalar_tensor_tensor(V[:, ds(t, 1), :, 0:UP], kv_ps[p][:, :, UP:2 * UP].unsqueeze(1), UNWS,
                                         V[:, ds(t, 1), :, UP:2 * UP], ALU.mult, ALU.subtract).then_inc(v_lo, 1)
                if past(t, 1):
                    low(t - 1, 1 - p)

            each(dve, T, 4, tile)
            low(T - 1, (T - 1) % 2)


def load_head(sp, h, qk, v, qk_dram, v_dram, loaded):
    sp.dma_start(qk[0:QK, :, :], qk_dram[h]).then_inc(loaded, 16)
    sp.dma_start(v[:, :, :], v_dram[h]).then_inc(loaded, 16)


def load_probe(sp, h, probe_qk, qk_dram, loaded):
    sp.dma_start(probe_qk[0:QK, :, :], qk_dram[h][:, 0:2, :]).then_inc(loaded, 16)


def first_head_maxima(nc, ident, qk, v, probe_qk, qk_dram, v_dram):
    with ExitStack() as ctx:
        s = Scope(nc, ctx, "max_")
        top, negated, rows = s.sb("top", [P, T]), s.sb("negated", [P, T]), s.sb("rows", [T, P], F16)
        scores = [s.ps(f"scores{i}", [P, N]) for i in range(2)]
        loaded, probe_loaded, made, reduced, put, turned, rounded, moved = (
            s.sem(n) for n in ("loaded", "probe_loaded", "made", "reduced", "put", "turned", "rounded", "moved"))
        block = ctx.enter_context(nc.Block())

        @block.tensor
        def _(pe):
            pe.wait_ge(loaded, 32)
            for t in range(T):
                if t >= 2:
                    pe.wait_ge(reduced, t - 1)
                for g in range(G):
                    gg = slice(g * GN, (g + 1) * GN)
                    last = pe.matmul(scores[t % 2][:, gg], lhsT=qk[0][0:QK, Q_HI, t * P:(t + 1) * P], rhs=qk[0][0:QK, K_HI, gg],
                                     start=True, stop=True)
                last.then_inc(made, 1)
            pe.wait_ge(put, 1)
            pe.transpose(scores[0][0:T, 0:P], negated[:, :], ident[:, :]).then_inc(turned, 1)

        @block.vector
        def _(dve):
            for b in range(2):
                dve.memset(qk[b][QK:QK + 1, K_HI, :], 1.0)
            for t in range(T):
                dve.wait_ge(made, t + 1)
                dve.tensor_reduce(top[:, t:t + 1], scores[t % 2][:, :], AXF, ALU.max).then_inc(reduced, 1)
            dve.wait_ge(reduced, T)
            dve.tensor_scalar(negated[:, :], top[:, :], -1.0, None, ALU.mult).then_inc(put, 1)
            dve.wait_ge(turned, 1)
            dve.tensor_copy(rows[:, :], scores[0][0:T, 0:P]).then_inc(rounded, 1)

        @block.sync
        def _(sp):
            load_head(sp, 0, qk[0], v[0], qk_dram, v_dram, loaded)
            load_probe(sp, 1, probe_qk[1], qk_dram, probe_loaded)
            sp.wait_ge(rounded, 1)
            sp.dma_start(qk[0][QK:QK + 1, Q_HI, :].rearrange("o (t j) -> o t j", j=P), rows[:, :]).then_inc(moved, 16)
            sp.wait_ge(moved, 16)
            sp.wait_ge(probe_loaded, 16)


def attention(nc, ident, qk, v, probe_qk, qk_dram, v_dram, heads_out):
    NB, SB, LAG, FIN, CUT = 4, 3, 3, 5, 2
    HEAD, ROUND, ROUNDS = G * T, 2 * G * T, HEADS // 2
    with ExitStack() as ctx:
        s = Scope(nc, ctx, "att_")
        prob = [s.sb(f"prob{i}", [P, GN]) for i in range(NB)]
        p_hi = [s.sb(f"p_hi{i}", [P, GN], F16) for i in range(NB)]
        p_lo = [s.sb(f"p_lo{i}", [P, GN], F16) for i in range(NB)]
        v_low, total, o_sb = ([s.sb(f"{n}{i}", [P, TG, UP]) for i in range(2)] for n in ("v_low", "total", "o_sb"))
        inv = [s.sb(f"inv{i}", [P, TG]) for i in range(2)]
        part = [s.sb(f"part{i}", [P, TG, G]) for i in range(2)]
        peak, negated, rows = s.sb("peak", [P, TG]), s.sb("negated", [P, TG]), s.sb("rows", [TG, P], F16)
        score = [s.ps(f"score{i}", [P, GN]) for i in range(SB)]
        probe = s.ps("probe", [P, GN])
        out = [s.ps(f"out{i}", [P, TG, 256]) for i in range(2)]
        scored, prob_done, hi_done, lo_done, weighed, low_out, summed, inverted, o_ready = (
            s.sem(n) for n in ("scored", "prob", "hi", "lo", "weighed", "low_out", "summed", "inverted", "o_ready"))
        probed, reduced, peaked, put, turned, rounded, moved = (
            s.sem(n) for n in ("probed", "reduced", "peaked", "put", "turned", "rounded", "moved"))
        stored, loaded, probe_loaded = ([s.sem(f"{n}{i}") for i in range(2)] for n in ("stored", "loaded", "probe_loaded"))
        block = ctx.enter_context(nc.Block())

        def rounds(eng, step):
            def one(j, _):
                for k in range(ROUND):
                    step(j, k)

            each(eng, ROUNDS, 1, one)

        def back(j, k, lag, do):
            if k >= lag:
                do(j, k - lag)
            elif past(j, 1):
                do(j - 1, k - lag + ROUND)

        def at_group(j, k, at, do):
            if k % T == at:
                back(j, k, T, lambda j, k: do(j, k // T))

        @block.tensor
        def _(pe):
            def scores(j, k):
                m, p, g, c, b = ROUND * j + k, k // HEAD, k // T % G, k % T, k % SB
                if k % HEAD == 0:
                    if p or past(j, 1):
                        pe.wait_ge(loaded[p], 32 * (j + p))
                    if p or past(j, 1):
                        pe.wait_ge(probe_loaded[1 - p], 16 * (j + p))
                if k % T == 0 and (p or past(j, 1)):
                    pe.wait_ge(moved, 16 * (2 * G * j + k // T - G + 1))
                if k < 2 and past(j, 1):
                    pe.wait_ge(hi_done, m - 1)
                elif past(m, SB):
                    pe.wait_ge(hi_done, m - SB + 1)
                cc, gg = slice(c * P, (c + 1) * P), slice(g * GN, (g + 1) * GN)
                pe.matmul(score[b][:, :], lhsT=qk[p][0:QK + 1, K_HI, cc], rhs=qk[p][0:QK + 1, Q_HI, gg], start=True, stop=False)
                pe.matmul(score[b][:, :], lhsT=qk[p][0:QK, K_HI, cc], rhs=qk[p][0:QK, Q_LO, gg], start=False, stop=False)
                pe.matmul(score[b][:, :], lhsT=qk[p][0:QK, K_LO, cc], rhs=qk[p][0:QK, Q_HI, gg], start=False,
                          stop=True).then_inc(scored, 1)

            def next_maxima(j, k):
                m, p, g, c = ROUND * j + k, k // HEAD, k // T % G, k % T
                if past(m, 1):
                    pe.wait_ge(reduced, m)
                if c == CUT and past(m, T):
                    n = 2 * G * j + k // T
                    pe.wait_ge(put, n)
                    pe.transpose(probe[0:TG, 0:P], negated[:, :], ident[:, :]).then_inc(turned, 1)
                    pe.wait_ge(rounded, n)
                t, gg = TG * g + c // G, slice(c % G * GN, (c % G + 1) * GN)
                pe.matmul(probe[:, :], lhsT=probe_qk[1 - p][0:QK, 0, t * P:(t + 1) * P], rhs=probe_qk[1 - p][0:QK, 1, gg],
                          start=True, stop=True).then_inc(probed, 1)

            def weigh(j, k):
                m, p, c, b = ROUND * j + k, k // HEAD, k % T, k // T % 2
                pe.wait_ge(lo_done, m + 1)
                if c == 0 and past(m, 2 * T):
                    pe.wait_ge(summed, 2 * G * j + k // T - 1)
                for q in range(TG):
                    qq = slice(q * P, (q + 1) * P)
                    pe.matmul(out[b][:, q, 0:2 * UP + 1], lhsT=p_hi[k % NB][:, qq], rhs=v[p][:, c, 0:2 * UP + 1],
                              start=c == 0 and q % 2 == 0, stop=False, skip_group_check=True)
                    last = pe.matmul(out[b][:, q, UP:2 * UP + 1], lhsT=p_lo[k % NB][:, qq], rhs=v[p][:, c, UP:2 * UP + 1],
                                     start=False, stop=c == T - 1, skip_group_check=True)
                last.then_inc(weighed, 1)

            def step(j, k):
                scores(j, k)
                next_maxima(j, k)
                back(j, k, LAG, weigh)

            rounds(pe, step)
            for k in range(ROUND - LAG, ROUND):
                weigh(ROUNDS - 1, k)

        @block.scalar
        def _(act):
            def low_sum(j, n):
                act.wait_ge(weighed, ROUND * j + T * (n + 1))
                if n >= 2 or past(j, 1):
                    act.wait_ge(summed, 2 * G * j + n - 1)
                act.activation(v_low[n % 2][:, :, :], out[n % 2][:, :, 0:UP], ACT.Copy).then_inc(low_out, 1)

            def step(j, k):
                m, b = ROUND * j + k, k % NB
                act.wait_ge(scored, m + 1)
                if past(m, NB):
                    act.wait_ge(lo_done, m - NB + 1)
                    act.wait_ge(weighed, m - NB + 1)
                act.activation(prob[b][:, :], score[k % SB][:, :], ACT.Exp).then_inc(prob_done, 1)
                act.activation(p_hi[b][:, :], score[k % SB][:, :], ACT.Exp).then_inc(hi_done, 1)
                at_group(j, k, FIN, low_sum)

            rounds(act, step)
            low_sum(ROUNDS - 1, 2 * G - 1)

        @block.vector
        def _(dve):
            def finish(j, n):
                i, b = 2 * G * j + n, n % 2
                dve.wait_ge(low_out, i + 1)
                dve.reciprocal(inv[b][:, :], out[b][:, :, 2 * UP]).then_inc(inverted, 1)
                dve.tensor_tensor(total[b][:, :, :], out[b][:, :, UP:2 * UP], v_low[b][:, :, :], ALU.add).then_inc(summed, 1)
                dve.wait_ge(inverted, i + 1)
                dve.wait_ge(summed, i + 1)
                if n >= 2 or past(j, 1):
                    dve.wait_ge(stored[b], 16 * (G * j + n // 2))
                dve.tensor_tensor(o_sb[b][:, :, :], total[b][:, :, :], inv[b][:, :].unsqueeze(2).to_broadcast([P, TG, UP]),
                                  ALU.mult).then_inc(o_ready, 1)

            def cut(j, n):
                i = 2 * G * j + n
                dve.wait_ge(reduced, T * (i + 1))
                dve.tensor_reduce(peak[:, :], part[n % 2][:, :, :], AXF, ALU.max).then_inc(peaked, 1)
                dve.wait_ge(peaked, i + 1)
                if n or past(j, 1):
                    dve.wait_ge(turned, i)
                dve.tensor_scalar(negated[:, :], peak[:, :], -1.0, None, ALU.mult).then_inc(put, 1)

            def round_row(j, n):
                i = 2 * G * j + n
                dve.wait_ge(turned, i + 1)
                if n or past(j, 1):
                    dve.wait_ge(moved, 16 * i)
                dve.tensor_copy(rows[:, :], probe[0:TG, 0:P]).then_inc(rounded, 1)

            def step(j, k):
                m, b, c = ROUND * j + k, k % NB, k % T
                at_group(j, k, 0, cut)
                at_group(j, k, CUT, round_row)
                dve.wait_ge(probed, m + 1)
                dve.tensor_reduce(part[k // T % 2][:, c // G, c % G:c % G + 1], probe[:, :], AXF, ALU.max).then_inc(reduced, 1)
                dve.wait_ge(prob_done, m + 1)
                dve.wait_ge(hi_done, m + 1)
                dve.tensor_tensor(p_lo[b][:, :], prob[b][:, :], p_hi[b][:, :], ALU.subtract).then_inc(lo_done, 1)
                at_group(j, k, FIN, finish)

            rounds(dve, step)
            finish(ROUNDS - 1, 2 * G - 1)

        @block.sync
        def _(sp):
            def store(n):
                h, g = n // G, n % G
                sp.wait_ge(o_ready, n + 1)
                sp.dma_start(heads_out[g * GN:(g + 1) * GN, h * UP:(h + 1) * UP].rearrange("(q p) d -> p q d", p=P),
                             o_sb[n % 2][:, :, :]).then_inc(stored[n % 2], 16)

            for n in range(HEADS * G + 1):
                h, g = n // G, n % G
                if g == 0 and h < HEADS:
                    if h:
                        sp.wait_ge(weighed, HEAD * h)
                    if h + 1 < HEADS:
                        load_head(sp, h + 1, qk[(h + 1) % 2], v[(h + 1) % 2], qk_dram, v_dram, loaded[(h + 1) % 2])
                    if h + 2 < HEADS:
                        load_probe(sp, h + 2, probe_qk[h % 2], qk_dram, probe_loaded[h % 2])
                    elif h + 2 == HEADS:
                        sp.nop().then_inc(probe_loaded[h % 2], 16)
                if n:
                    store(n - 1)
                if 0 < n < HEADS * G - G + 1:
                    sp.wait_ge(rounded, n)
                    sp.dma_start(qk[((n - 1) // G + 1) % 2][QK:QK + 1, Q_HI, (n - 1) % G * GN:((n - 1) % G + 1) * GN]
                                 .rearrange("o (t j) -> o t j", j=P), rows[:, :]).then_inc(moved, 16)
                elif n:
                    if n <= HEADS * G - 1:
                        sp.wait_ge(rounded, n)
                        sp.nop().then_inc(moved, 16)
            for b in range(2):
                sp.wait_ge(stored[b], 16 * HEADS * G // 2)


def project_out(nc, oT, W_o, res):
    NB, K = 4, HEADS * UP // P
    with ExitStack() as ctx:
        s = Scope(nc, ctx, "wo_")
        prod = [s.ps(f"prod{i}", [P, 512]) for i in range(NB)]
        made, added = s.sem("made"), s.sem("added")
        block = ctx.enter_context(nc.Block())

        @block.tensor
        def _(pe):
            def tile(t, p):
                if past(t, NB):
                    pe.wait_ge(added, t - NB + 1)
                for k in range(K):
                    last = matmul3(pe, prod[p][:, 0:D], oT[0][:, k, ds(t * P, P)], oT[1][:, k, ds(t * P, P)],
                                   W_o[0][:, k, :], W_o[1][:, k, :], k == 0, k == K - 1)
                last.then_inc(made, 1)

            each(pe, T, NB, tile)

        @block.vector
        def _(dve):
            def tile(t, p):
                dve.wait_ge(made, t + 1)
                dve.scalar_tensor_tensor(res[:, ds(t, 1), :], prod[p][:, 0:D].unsqueeze(1), UNWS, res[:, ds(t, 1), :],
                                         ALU.mult, ALU.add).then_inc(added, 1)

            each(dve, T, NB, tile)


def l1_attention(nc, a, x, res, ident):
    heads_out = nc.dram_tensor("heads_out", (N, HEADS * UP), F32, kind="Internal").ap()
    qk_dram = nc.dram_tensor("qk_dram", (HEADS, QK, 4, N), F16, kind="Internal").ap()
    v_dram = nc.dram_tensor("v_dram", (HEADS, P, T, 2 * UP + 2), F16, kind="Internal").ap()
    col = lambda ap: ap.rearrange("(k p) -> p k", p=P)
    rows = lambda ap: ap.rearrange("(k p) n -> p k n", p=P)
    normalize_and_turn(nc, "a1n_", ident, x, D, "layer", None, None, tok=res)
    with ExitStack() as ctx:
        s = Scope(nc, ctx, "a1_")
        cqT = s.sb("cqT_hi", [P, 1, N], F16), s.sb("cqT_lo", [P, 1, N], F16)
        ckvT = s.sb("ckvT_hi", [P, 1, N], F16), s.sb("ckvT_lo", [P, 1, N], F16)
        cos, sin, k_rope = (s.sb(n, [P, T, ROPE]) for n in ("cos", "sin", "k_rope"))
        W_uq = s.sb("uq_hi", [P, 1, HEADS * QK], F16), s.sb("uq_lo", [P, 1, HEADS * QK], F16)
        W_ukv = s.sb("ukv_hi", [P, 1, HEADS * 2 * UP], F16), s.sb("ukv_lo", [P, 1, HEADS * 2 * UP], F16)
        with ExitStack() as early:
            s = Scope(nc, early, "a1e_")
            xT = s.sb("xT_hi", [P, KD, N], F16), s.sb("xT_lo", [P, KD, N], F16)
            c_q, c_kv = s.sb("c_q", [P, T, DQ]), s.sb("c_kv", [P, T, DKV])
            W = s.sb("W_hi", [P, KD, DQ + DKV + ROPE], F16), s.sb("W_lo", [P, KD, DQ + DKV + ROPE], F16)
            dq, dkv = slice(0, DQ), slice(DQ, DQ + DKV + ROPE)
            split_weights(nc, "a1w_", [
                (rows(a["L1_ffn_w_dq"]), col(a["L1_ffn_w_in_norm"]), W[0][:, :, dq], W[1][:, :, dq]),
                (rows(a["L1_ffn_w_dkv"]), col(a["L1_ffn_w_in_norm"]), W[0][:, :, dkv], W[1][:, :, dkv]),
                (rows(a["L1_ffn_w_uq"]), col(a["L1_ffn_w_qnorm"]), W_uq[0][:, :, :], W_uq[1][:, :, :]),
                (rows(a["L1_ffn_w_ukv"]), col(a["L1_ffn_w_kvnorm"]), W_ukv[0][:, :, :], W_ukv[1][:, :, :])])
            normalize_and_turn(nc, "a1r_", ident, res, D, "rms", *xT)
            latent_project(nc, a, xT, W[0], W[1], c_q, c_kv, k_rope, cos, sin)
            normalize_and_turn(nc, "a1q_", ident, c_q, DQ, "rms", *cqT)
            normalize_and_turn(nc, "a1k_", ident, c_kv, DKV, "rms", *ckvT)
        s = Scope(nc, ctx, "a1h_")
        qT = s.sb("qT_hi", [P, HH, N], F16), s.sb("qT_lo", [P, HH, N], F16)
        kT = s.sb("kT_hi", [P, HH, N], F16), s.sb("kT_lo", [P, HH, N], F16)
        V = s.sb("V", [P, T, HH, 2 * UP + 2], F16)
        for n, first in enumerate(range(0, HEADS, HH)):
            uq, ukv = slice(first * QK, (first + HH) * QK), slice(first * 2 * UP, (first + HH) * 2 * UP)
            queries_keys_values(nc, f"qkv{n}_", ident, cqT, ckvT, [w[:, 0, uq] for w in W_uq], [w[:, 0, ukv] for w in W_ukv],
                                k_rope, cos, sin, qT, kT, V, qk_dram, v_dram, first)
    with ExitStack() as ctx:
        s = Scope(nc, ctx, "a1m_")
        qk = [s.sb(f"qk{i}", [P, 4, N], F16) for i in range(2)]
        probe_qk = [s.sb(f"probe_qk{i}", [P, 2, N], F16) for i in range(2)]
        v = [s.sb(f"v{i}", [P, T, 2 * UP + 2], F16) for i in range(2)]
        first_head_maxima(nc, ident, qk, v, probe_qk, qk_dram, v_dram)
        nc.disable_value_cache = True
        attention(nc, ident, qk, v, probe_qk, qk_dram, v_dram, heads_out)
        nc.disable_value_cache = False
    with ExitStack() as ctx:
        s = Scope(nc, ctx, "a1o_")
        heads = s.sb("heads", [P, T, HEADS * UP])
        oT = s.sb("oT_hi", [P, HEADS * UP // P, N], F16), s.sb("oT_lo", [P, HEADS * UP // P, N], F16)
        W_o = s.sb("W_o_hi", [P, HEADS * UP // P, D], F16), s.sb("W_o_lo", [P, HEADS * UP // P, D], F16)
        load_or_store(nc, "heads_", heads[:, :, :], heads_out.rearrange("(t p) d -> p t d", p=P))
        split_weights(nc, "a1ow_", [(rows(a["L1_ffn_w_o"]), None, W_o[0][:, :, :], W_o[1][:, :, :])])
        normalize_and_turn(nc, "a1t_", ident, heads, HEADS * UP, None, *oT)
        project_out(nc, oT, W_o, res)


def load_experts(nc, a, raw):
    with ExitStack() as ctx:
        s = Scope(nc, ctx, "le_")
        loaded = s.sem("loaded")
        block = ctx.enter_context(nc.Block())

        @block.sync
        def _(sp):
            for j, (routed, shared) in enumerate((("r_wg", "sh_wg"), ("r_wu", "sh_wu"))):
                for k in range(KD):
                    kk = slice(k * P, (k + 1) * P)
                    sp.dma_start(raw[:, 2 * j + k, 0:L1_E, :], a["L1_ffn_" + routed][:, kk, :].rearrange("e p i -> p e i")).then_inc(loaded, 16)
                    sp.dma_start(raw[:, 2 * j + k, L1_E, :], a["L1_ffn_" + shared][kk, :]).then_inc(loaded, 16)
            for k in range(KD):
                kk = slice(k * P, (k + 1) * P)
                sp.dma_start(raw[:, 4 + k, 0:L1_E, :], a["L1_ffn_r_wd"][:, :, kk].rearrange("e p i -> p e i")).then_inc(loaded, 16)
                sp.dma_start(raw[:, 4 + k, L1_E, :], a["L1_ffn_sh_wd"][:, kk]).then_inc(loaded, 16)
            sp.wait_ge(loaded, 16 * 12)


def l1_experts(nc, x, res, hT, raw, scale, w_hi, w_lo, comb):
    E = L1_E + 1
    LAG = 2
    with ExitStack() as ctx:
        s = Scope(nc, ctx, "e1_")
        gate_out = [s.sb(f"gate{i}", [P, GN]) for i in range(2)]
        mixed = [s.sb(f"mixed{i}", [P, GN]) for i in range(2)]
        hid = [(s.sb(f"hid_hi{i}", [P, GN], F16), s.sb(f"hid_lo{i}", [P, GN], F16)) for i in range(4)]
        up = [[s.ps(f"up{j}{i}", [P, GN]) for i in range(2)] for j in range(2)]
        down = [s.ps(f"down{i}", [P, 512]) for i in range(TG)]
        w_high, w_low, up_done, gated, mixed_done, hi_done, lo_done, down_done, added = (
            s.sem(n) for n in ("w_high", "w_low", "up", "gated", "mixed", "hi", "lo", "down", "added"))
        block = ctx.enter_context(nc.Block())
        WROWS = 6
        AHEAD = 2

        def all_experts(eng, expert, prepare):
            for e in range(AHEAD):
                prepare(e)

            def body(e, _):
                prepare(e + AHEAD)
                expert(e)

            each(eng, E - AHEAD, 1, body)
            for e in range(E - AHEAD, E):
                expert(e)

        def lagged(e, g, do):
            if g >= LAG:
                do(e, g - LAG)
            elif past(e, 1):
                do(e - 1, G + g - LAG)

        @block.tensor
        def _(pe):
            def project_down(e, g):
                u = G * e + g
                pe.wait_ge(lo_done, u + 1)
                for q in range(TG):
                    if past(u, 1):
                        pe.wait_ge(added, TG * (u - 1) + q + 1)
                    qq = slice(q * P, (q + 1) * P)
                    last = matmul3(pe, down[q][:, 0:D], hid[g][0][:, qq], hid[g][1][:, qq],
                                   w_hi[:, 4:6, ds(e, 1), :], w_lo[:, 4:6, ds(e, 1), :], True, True)
                    last.then_inc(down_done, 1)

            def expert(e):
                pe.wait_ge(w_low, WROWS * e + WROWS)
                for g in range(G):
                    u, gg = G * e + g, slice(g * GN, (g + 1) * GN)
                    if past(u, 2):
                        pe.wait_ge(mixed_done, u - 1)
                    for j in range(2):
                        for k in range(KD):
                            last = matmul3(pe, up[j][g % 2][:, :], w_hi[:, 2 * j + k, ds(e, 1), :], w_lo[:, 2 * j + k, ds(e, 1), :],
                                           hT[0][:, k, gg], hT[1][:, k, gg], k == 0, k == KD - 1)
                        last.then_inc(up_done, 1)
                    lagged(e, g, project_down)

            all_experts(pe, expert, lambda e: None)
            for g in range(G - LAG, G):
                project_down(E - 1, g)

        @block.scalar
        def _(act):
            def prepare(e):
                for r in range(WROWS):
                    act.activation(w_hi[:, r, ds(e, 1), :], raw[:, r, ds(e, 1), :], ACT.Copy,
                                   scale=scale[:, r % 2:r % 2 + 1] if r < 4 else WS).then_inc(w_high, 1)

            def expert(e):
                for g in range(G):
                    u, b = G * e + g, g % 2
                    act.wait_ge(up_done, 2 * u + 1)
                    if past(u, 2):
                        act.wait_ge(mixed_done, u - 1)
                    act.activation(gate_out[b][:, :], up[0][b][:, :], ACT.Silu, scale=UNWS).then_inc(gated, 1)
                    act.wait_ge(mixed_done, u + 1)
                    if past(u, 4):
                        act.wait_ge(down_done, TG * (u - 3))
                    act.activation(hid[g][0][:, :], mixed[b][:, :], ACT.Copy).then_inc(hi_done, 1)

            all_experts(act, expert, prepare)

        @block.vector
        def _(dve):
            def prepare(e):
                for r in range(WROWS):
                    dve.wait_ge(w_high, WROWS * e + r + 1)
                    dve.scalar_tensor_tensor(w_lo[:, r, ds(e, 1), :], raw[:, r, ds(e, 1), :],
                                             scale[:, r % 2:r % 2 + 1] if r < 4 else WS, w_hi[:, r, ds(e, 1), :],
                                             ALU.mult, ALU.subtract).then_inc(w_low, 1)

            def add(e, g):
                u = G * e + g
                for q in range(TG):
                    n = TG * u + q
                    dve.wait_ge(down_done, n + 1)
                    if past(u, 1):
                        dve.wait_ge(added, n - TG + 1)
                    dve.scalar_tensor_tensor(res[:, TG * g + q, :], down[q][:, 0:D], comb[:, TG * g + q, ds(e, 1)],
                                             res[:, TG * g + q, :], ALU.mult, ALU.add).then_inc(added, 1)

            def expert(e):
                for g in range(G):
                    u, b = G * e + g, g % 2
                    dve.wait_ge(gated, u + 1)
                    dve.wait_ge(up_done, 2 * u + 2)
                    if past(u, 2):
                        dve.wait_ge(hi_done, u - 1)
                        dve.wait_ge(lo_done, u - 1)
                    dve.scalar_tensor_tensor(mixed[b][:, :], up[1][b][:, :], UNWS, gate_out[b][:, :], ALU.mult,
                                             ALU.mult).then_inc(mixed_done, 1)
                    dve.wait_ge(hi_done, u + 1)
                    dve.tensor_tensor(hid[g][1][:, :], mixed[b][:, :], hid[g][0][:, :], ALU.subtract).then_inc(lo_done, 1)
                    lagged(e, g, add)

            all_experts(dve, expert, prepare)
            for g in range(G - LAG, G):
                add(E - 1, g)
            for t in range(T):
                dve.wait_ge(added, TG * (G * (E - 1)) + t + 1)
                dve.tensor_tensor(x[:, t, :], x[:, t, :], res[:, t, :], ALU.add)


def prepare_scale(nc, src, scale, shared):
    with ExitStack() as ctx:
        s = Scope(nc, ctx, "sc_")
        loaded, steps = s.sem("loaded"), s.sem("steps")
        block = ctx.enter_context(nc.Block())

        @block.sync
        def _(sp):
            with nc.allow_non_contiguous_dma(reason="a short column of norm weights"):
                sp.dma_start(scale[:, :], src).then_inc(loaded, 16)

        @block.vector
        def _(dve):
            dve.memset(shared, UNWS)
            dve.wait_ge(loaded, 16)
            dve.tensor_scalar(scale[:, :], scale[:, :], WS, None, ALU.mult)


def l1_moe(nc, a, x, res, ident):
    with ExitStack() as ctx:
        s = Scope(nc, ctx, "m1_")
        raw = s.sb("raw", [P, 6, L1_E + 1, P])
        w_hi, w_lo = s.sb("w_hi", [P, 6, L1_E + 1, P], F16), s.sb("w_lo", [P, 6, L1_E + 1, P], F16)
        hT = s.sb("hT_hi", [P, KD, N], F16), s.sb("hT_lo", [P, KD, N], F16)
        Wg = s.sb("Wg_hi", [P, KD, L1_E], F16), s.sb("Wg_lo", [P, KD, L1_E], F16)
        scale = s.sb("scale", [P, KD])
        comb = s.sb("comb", [P, T, L1_E + 1])
        norm = a["L1_ffn_w_post_norm"].rearrange("(k p) -> p k", p=P)
        load_experts(nc, a, raw)
        prepare_scale(nc, norm, scale, comb[:, :, L1_E:L1_E + 1])
        split_weights(nc, "m1w_", [(a["L1_ffn_w_gate"].rearrange("(k p) e -> p k e", p=P), norm, Wg[0][:, :, :], Wg[1][:, :, :])])
        normalize_and_turn(nc, "m1n_", ident, res, D, "rms", *hT)
        route(nc, "m1r_", ident, L1_E, L1_K, hT, Wg, None, comb[:, :, 0:L1_E])
        l1_experts(nc, x, res, hT, raw, scale, w_hi, w_lo, comb)


def l1_ffn(nc, a, x, ident):
    with ExitStack() as ctx:
        res = Scope(nc, ctx, "").sb("res", [P, T, D])
        l1_attention(nc, a, x, res, ident)
        recycle_semaphores(nc)
        l1_moe(nc, a, x, res, ident)


def load_or_store(nc, prefix, out, in_):
    with ExitStack() as ctx:
        done = Scope(nc, ctx, prefix).sem("done")
        block = ctx.enter_context(nc.Block())

        @block.sync
        def _(sp):
            sp.dma_start(out, in_).then_inc(done, 16)
            sp.wait_ge(done, 16)


def build(nc, a, out):
    Scope.used.clear()
    with ExitStack() as ctx:
        s = Scope(nc, ctx, "")
        ident, ident16, ones = s.sb("ident", [P, P]), s.sb("ident16", [P, P], F16), s.sb("ones", [P, P])
        x = s.sb("x", [P, T, D])
        tiles = lambda ap: ap.rearrange("(t p) d -> p t d", p=P)
        make_identities(nc, ident, ident16, ones)
        load_or_store(nc, "in_", x[:, :, :], tiles(a["x"]))
        with ExitStack() as adj_ctx:
            s2 = Scope(nc, adj_ctx, "")
            adjT, diag = s2.sb("adjT", [P, T, N], F16), s2.sb("diag", [P, T, P], F16)
            transpose_adjacency(nc, a["adj"], ident16, adjT, diag)
            l0_gnn(nc, a, x, ident, ident16, ones, adjT, diag)
            recycle_semaphores(nc)
            l0_ffn(nc, a, x, ident); recycle_semaphores(nc); l1_gnn(nc, a, x, ident, adjT, diag)
            recycle_semaphores(nc)
        l1_ffn(nc, a, x, ident)
        load_or_store(nc, "out_", tiles(out), x[:, :, :])


INPUTS = ["x", "adj", "L0_gnn_W", "L0_ffn_Wg", "L0_ffn_bg", "L0_ffn_W1", "L0_ffn_b1", "L0_ffn_W2", "L0_ffn_b2",
          "L1_gnn_W_nb", "L1_gnn_b_nb", "L1_gnn_W_line", "L1_gnn_b_line", "L1_ffn_w_in_norm", "L1_ffn_w_dq",
          "L1_ffn_w_qnorm", "L1_ffn_w_uq", "L1_ffn_w_dkv", "L1_ffn_w_kvnorm", "L1_ffn_w_ukv", "L1_ffn_w_o",
          "L1_ffn_w_post_norm", "L1_ffn_w_gate", "L1_ffn_sh_wg", "L1_ffn_sh_wu", "L1_ffn_sh_wd", "L1_ffn_r_wg",
          "L1_ffn_r_wu", "L1_ffn_r_wd"]


def kernel(**inputs):
    import numpy as np
    import concourse.bacc as bacc
    from concourse.bass_utils import run_bass_kernel_spmd

    nc = bacc.Bacc("TRN2", target_bir_lowering=False, num_devices=1)
    arrays = {name: np.ascontiguousarray(inputs[name]) for name in INPUTS}
    freq = (np.float32(1.0) / np.float32(10000.0) ** (np.arange(0, ROPE, 2, dtype=np.float32) / np.float32(ROPE))).astype(np.float32)
    angle = np.outer(np.arange(N, dtype=np.float32), freq).astype(np.float32)
    arrays["rope_cos"] = np.concatenate([np.cos(angle), np.cos(angle)], axis=-1).astype(np.float32)
    arrays["rope_sin"] = np.concatenate([-np.sin(angle), np.sin(angle)], axis=-1).astype(np.float32)
    args = {name: nc.dram_tensor("in_" + name, v.shape, mybir.dt.from_np(v.dtype), kind="ExternalInput").ap()
            for name, v in arrays.items()}
    out = nc.dram_tensor("out_0", (N, D), F32, kind="ExternalOutput").ap()
    build(nc, args, out)
    r = run_bass_kernel_spmd(nc, [{"in_" + name: v for name, v in arrays.items()}], core_ids=[0])
    return r.results[0]["out_0"]
```

```python
import concourse.bass as bass
from concourse import mybir
from contextlib import ExitStack

F32 = mybir.dt.float32
F16 = mybir.dt.float16
I32 = mybir.dt.int32
ALU = mybir.AluOpType
ACT = mybir.ActivationFunctionType
AXF = mybir.AxisListType.X
ds = bass.ds

P = 128
N = 2048
D = 256
T = N // P
KD = D // P
G = 4
GN = N // G
TG = GN // P
WS = 64.0
UNWS = 1.0 / WS
LN_EPS = 1e-5
RMS_EPS = 1.1920929e-07
SIM_EPS = 1e-8
NEIGHBORS = 64
L0_E, L0_F, L0_K = 8, 1024, 2
ST = 256
NT = (N * L0_K + L0_E * (ST - 1)) // ST
FC = L0_F // P
L1_E, L1_I, L1_K = 16, 128, 4
HEADS, UP, ROPE = 8, 64, 32
QK = UP + ROPE
HH = 4
DQ = DKV = 128
Q_HI, K_HI, Q_LO, K_LO = range(4)
ATT_SCALE = 1.0 / float(QK) ** 0.5
BIG = 1.0e30


class Scope:

    used = []

    def __init__(self, nc, ctx, prefix):
        self.nc, self.ctx, self.prefix = nc, ctx, prefix

    def sb(self, name, shape, dt=F32):
        return self.ctx.enter_context(self.nc.sbuf_tensor(self.prefix + name, shape, dt))

    def ps(self, name, shape, dt=F32):
        return self.ctx.enter_context(self.nc.psum_tensor(self.prefix + name, shape, dt))

    def sem(self, name):
        handle = self.nc.alloc_semaphore(self.prefix + name)
        Scope.used.append(handle)
        return handle


class Together:

    def __init__(self, nc, ctx):
        self.ctx, self.block = ctx, ctx.enter_context(nc.Block())


def recycle_semaphores(nc):
    nc.clear_and_free_semaphores(Scope.used)
    nc.all_engine_barrier()
    Scope.used.clear()


class Chain:

    def __init__(self, eng, sem):
        self.eng, self.sem, self.n = eng, sem, 0

    def __call__(self, ins):
        ins.then_inc(self.sem, 1)
        self.n += 1
        self.eng.wait_ge(self.sem, self.n)


def each(eng, n, step, body):
    for i in range(step):
        body(i, i)
    if n > step:
        with eng.Fori(1, n // step) as j:
            for p in range(step):
                body(j * step + p, p)


def past(i, n):
    return not isinstance(i, int) or i >= n


def make_identities(nc, ident, ident16, ones):
    with ExitStack() as ctx:
        s = Scope(nc, ctx, "id_")
        cleared, done = s.sem("cleared"), s.sem("done")
        block = ctx.enter_context(nc.Block())

        @block.gpsimd
        def _(pool):
            pool.memset(ident[:, :], 0.0).then_inc(cleared, 1)
            pool.wait_ge(cleared, 1)
            pool.affine_select(out=ident[:, :], in_=ident[:, :], compare_op=ALU.not_equal, fill=1.0, base=0,
                               pattern=[[-1, P]], channel_multiplier=1).then_inc(done, 1)

        @block.vector
        def _(dve):
            dve.memset(ones[:, :], 1.0)
            dve.wait_ge(done, 1)
            dve.tensor_copy(ident16[:, :], ident[:, :])


def split_weights(nc, prefix, items, together=None):
    with ExitStack() as ctx:
        s = Scope(nc, together.ctx if together else ctx, prefix)
        raw = [s.sb(f"raw{i}", list(src.shape)) for i, (src, *_) in enumerate(items)]
        scale = [s.sb(f"scale{i}", list(sc.shape)) if sc is not None else None for i, (_, sc, _, _) in enumerate(items)]
        loaded = [s.sem(f"loaded{i}") for i in range(len(items))]
        scaled, hi_done, lo_done = s.sem("scaled"), s.sem("hi"), s.sem("lo")
        block = together.block if together else ctx.enter_context(nc.Block())

        @block.sync
        def _(sp):
            for i, (src, sc, _, _) in enumerate(items):
                sp.dma_start(raw[i][:, :, :], src).then_inc(loaded[i], 16)
                if sc is not None:
                    with nc.allow_non_contiguous_dma(reason="a short column of norm weights"):
                        sp.dma_start(scale[i][:, :], sc).then_inc(loaded[i], 16)

        @block.scalar
        def _(act):
            for i, (src, sc, hi, _) in enumerate(items):
                act.wait_ge(scaled, i + 1)
                act.activation(hi, raw[i][:, :, :], ACT.Copy, scale=WS).then_inc(hi_done, 1)

        @block.vector
        def _(dve):
            steps = s_steps = 0
            for i, (src, sc, hi, lo) in enumerate(items):
                dve.wait_ge(loaded[i], 16 if sc is None else 32)
                if sc is not None:
                    for k in range(src.shape[1]):
                        last = dve.tensor_scalar(raw[i][:, k, :], raw[i][:, k, :], scale[i][:, k:k + 1], None, ALU.mult)
                    last.then_inc(scaled, 1)
                else:
                    dve.engine_nop().then_inc(scaled, 1)
            for i, (src, sc, hi, lo) in enumerate(items):
                dve.wait_ge(scaled, i + 1)
                dve.wait_ge(hi_done, i + 1)
                dve.scalar_tensor_tensor(lo, raw[i][:, :, :], WS, hi, ALU.mult, ALU.subtract).then_inc(lo_done, 1)


def split_transposed_weights(nc, prefix, ident, items, together=None):
    with ExitStack() as ctx:
        s = Scope(nc, together.ctx if together else ctx, prefix)
        raw = [s.sb(f"raw{i}", [P, KD, D]) for i in range(len(items))]
        flipped = [s.ps(f"flipped{i}", [P, KD, D]) for i in range(len(items))]
        loaded = [s.sem(f"loaded{i}") for i in range(len(items))]
        turned, hi_done = s.sem("turned"), s.sem("hi")
        block = together.block if together else ctx.enter_context(nc.Block())

        @block.sync
        def _(sp):
            for i, (src, _, _) in enumerate(items):
                sp.dma_start(raw[i][:, :, :], src.rearrange("(o p) i -> p o i", p=P)).then_inc(loaded[i], 16)

        @block.tensor
        def _(pe):
            for i in range(len(items)):
                pe.wait_ge(loaded[i], 16)
                for o in range(KD):
                    for k in range(KD):
                        last = pe.transpose(flipped[i][:, k, o * P:(o + 1) * P], raw[i][:, o, k * P:(k + 1) * P], ident[:, :])
                last.then_inc(turned, 1)

        @block.scalar
        def _(act):
            for i, (_, hi, _) in enumerate(items):
                act.wait_ge(turned, i + 1)
                act.activation(hi, flipped[i][:, :, :], ACT.Copy, scale=WS).then_inc(hi_done, 1)

        @block.vector
        def _(dve):
            for i, (_, hi, lo) in enumerate(items):
                dve.wait_ge(hi_done, i + 1)
                dve.scalar_tensor_tensor(lo, flipped[i][:, :, :], WS, hi, ALU.mult, ALU.subtract)


def normalize_and_turn(nc, prefix, ident, src, width, kind, xT_hi, xT_lo, tok=None, tok_hi=None, tok_lo=None, together=None):
    chunks, NB = width // P, 4
    with ExitStack() as ctx:
        s = Scope(nc, together.ctx if together else ctx, prefix)
        stats = s.sb("stats", [P, T, 6])
        dif, mean, second, var = (s.sb(n, [P, T]) for n in ("dif", "mean", "second", "var"))
        std, rstd = s.sb("std", [P, T]), s.sb("rstd", [P, T])
        stage = [s.sb(f"stage{i}", [P, width]) for i in range(NB)]
        turned = [s.ps(f"turned{i}", [P, 512]) for i in range(NB)]
        stat_done, steps, var_done, std_done = s.sem("stat"), s.sem("steps"), s.sem("var"), s.sem("std")
        staged, flipped, hi_done, lo_done = s.sem("staged"), s.sem("flipped"), s.sem("hi"), s.sem("lo")
        copied, tok_hi_done = s.sem("copied"), s.sem("tok_hi")
        block = together.block if together else ctx.enter_context(nc.Block())
        keeps = tok is not None or tok_hi is not None

        @block.vector
        def _(dve):
            if tok_hi is not None and tok_hi.shape[-1] > width:
                dve.memset(tok_hi[:, :, width:width + 1], 1.0)
            if kind:
                each(dve, T, 4, lambda t, _:
                    dve.bn_stats(stats[:, ds(t, 1), :], src[:, ds(t, 1), :]).then_inc(stat_done, 1))
                dve.wait_ge(stat_done, T)
                link = Chain(dve, steps)
                me, mo = stats[:, :, 1], stats[:, :, 4]
                link(dve.tensor_tensor(dif[:, :], me, mo, ALU.subtract))
                link(dve.tensor_tensor(mean[:, :], me, mo, ALU.add))
                link(dve.tensor_scalar(mean[:, :], mean[:, :], 0.5, None, ALU.mult))
                link(dve.tensor_tensor(second[:, :], stats[:, :, 2], stats[:, :, 5], ALU.add))
                link(dve.tensor_tensor(dif[:, :], dif[:, :], dif[:, :], ALU.mult))
                link(dve.tensor_scalar(second[:, :], second[:, :], 1.0 / width, LN_EPS if kind == "layer" else RMS_EPS,
                                       ALU.mult, ALU.add))
                link(dve.scalar_tensor_tensor(var[:, :], dif[:, :], 0.25, second[:, :], ALU.mult, ALU.add))
                if kind == "rms":
                    link(dve.tensor_tensor(dif[:, :], mean[:, :], mean[:, :], ALU.mult))
                    link(dve.tensor_tensor(var[:, :], var[:, :], dif[:, :], ALU.add))
                dve.engine_nop().then_inc(var_done, 1)
                dve.wait_ge(std_done, 1)
                link(dve.reciprocal(rstd[:, :], std[:, :]))
            if xT_hi is None:
                each(dve, T, 4, lambda t, _:
                    dve.tensor_scalar(tok[:, ds(t, 1), :], src[:, ds(t, 1), :], mean[:, ds(t, 1)], rstd[:, ds(t, 1)],
                                      ALU.subtract, ALU.mult))
                return

            def finish(t, p):
                dve.wait_ge(hi_done, t + 1)
                dve.tensor_tensor(xT_lo[:, :, ds(t * P, P)], turned[p][:, 0:width].rearrange("p (k n) -> p k n", k=chunks),
                                  xT_hi[:, :, ds(t * P, P)], ALU.subtract).then_inc(lo_done, 1)
                if tok_lo is not None:
                    dve.wait_ge(tok_hi_done, t + 1)
                    dve.tensor_tensor(tok_lo[:, ds(t, 1), 0:width], stage[p][:, :].unsqueeze(1),
                                      tok_hi[:, ds(t, 1), 0:width], ALU.subtract)

            def step(t, p):
                if past(t, NB):
                    dve.wait_ge(flipped, t - NB + 1)
                    if keeps:
                        dve.wait_ge(copied, t - NB + 1)
                out = stage[p][:, :].unsqueeze(1)
                if kind == "layer":
                    ins = dve.tensor_scalar(out, src[:, ds(t, 1), :], mean[:, ds(t, 1)], rstd[:, ds(t, 1)],
                                            ALU.subtract, ALU.mult)
                elif kind == "rms":
                    ins = dve.tensor_scalar(out, src[:, ds(t, 1), :], rstd[:, ds(t, 1)], None, ALU.mult)
                else:
                    ins = dve.tensor_copy(out, src[:, ds(t, 1), :])
                ins.then_inc(staged, 1)
                if past(t, 1):
                    finish(t - 1, (p - 1) % NB)

            each(dve, T, NB, step)
            finish(T - 1, (T - 1) % NB)

        @block.tensor
        def _(pe):
            if xT_hi is None:
                return

            def step(t, p):
                pe.wait_ge(staged, t + 1)
                if past(t, NB):
                    pe.wait_ge(lo_done, t - NB + 1)
                for k in range(chunks):
                    last = pe.transpose(turned[p][:, k * P:(k + 1) * P], stage[p][:, k * P:(k + 1) * P], ident[:, :])
                last.then_inc(flipped, 1)

            each(pe, T, NB, step)

        @block.scalar
        def _(act):
            if kind:
                act.wait_ge(var_done, 1)
                act.activation(std[:, :], var[:, :], ACT.Sqrt).then_inc(std_done, 1)
            if xT_hi is None:
                return

            def step(t, p):
                if keeps:
                    act.wait_ge(staged, t + 1)
                    if tok_hi is not None:
                        ins = act.activation(tok_hi[:, ds(t, 1), 0:width], stage[p][:, :].unsqueeze(1), ACT.Copy)
                        ins.then_inc(tok_hi_done, 1)
                    if tok is not None:
                        ins = act.activation(tok[:, ds(t, 1), 0:width], stage[p][:, :].unsqueeze(1), ACT.Copy)
                    else:
                        ins = act.nop()
                    ins.then_inc(copied, 1)
                act.wait_ge(flipped, t + 1)
                act.activation(xT_hi[:, :, ds(t * P, P)], turned[p][:, 0:width].rearrange("p (k n) -> p k n", k=chunks),
                               ACT.Copy).then_inc(hi_done, 1)

            each(act, T, NB, step)


def matmul3(pe, out, a_hi, a_lo, b_hi, b_lo, first, last):
    pe.matmul(out, lhsT=a_hi, rhs=b_hi, start=first, stop=False)
    pe.matmul(out, lhsT=a_hi, rhs=b_lo, start=False, stop=False)
    return pe.matmul(out, lhsT=a_lo, rhs=b_hi, start=False, stop=last)


def transpose_adjacency(nc, adj, ident16, adjT, diag, x, x_in):
    NB, RB = 2, 3
    with ExitStack() as ctx:
        s = Scope(nc, ctx, "adj_")
        raw = [s.sb(f"raw{i}", [P, N], I32) for i in range(RB)]
        mask = [s.sb(f"mask{i}", [P, N], F16) for i in range(NB)]
        flipped = [s.ps(f"flipped{i}", [P, T, P], F16) for i in range(NB)]
        loaded = [s.sem(f"loaded{i}") for i in range(RB)]
        masked, turned, act_out, dve_out, kept = (s.sem(n) for n in ("masked", "turned", "act_out", "dve_out", "kept"))
        x_loaded = s.sem("x_loaded")
        half = T // 2
        block = ctx.enter_context(nc.Block())

        @block.sync
        def _(sp):
            for t in range(T):
                if t >= RB:
                    sp.wait_ge(masked, t - RB + 1)
                sp.dma_start(raw[t % RB][:, :], adj[t * P:(t + 1) * P, :]).then_inc(loaded[t % RB], 16)
            sp.dma_start(x, x_in).then_inc(x_loaded, 16)
            sp.wait_ge(x_loaded, 16)

        @block.vector
        def _(dve):
            def out(t, p):
                dve.wait_ge(turned, t + 1)
                dve.tensor_copy(adjT[:, half:T, ds(t * P, P)], flipped[p][:, half:T, :]).then_inc(dve_out, 1)

            for t in range(T):
                dve.wait_ge(loaded[t % RB], 16 * (t // RB + 1))
                if t >= NB:
                    dve.wait_ge(turned, t - NB + 1)
                dve.tensor_scalar(mask[t % NB][:, :], raw[t % RB][:, :], 0, None, ALU.is_gt).then_inc(masked, 1)
                if t >= 1:
                    out(t - 1, (t - 1) % NB)
            out(T - 1, (T - 1) % NB)
            dve.wait_ge(act_out, T)
            dve.wait_ge(dve_out, T)
            each(dve, T, 4, lambda c, _:
                dve.tensor_copy(diag[:, ds(c, 1), :], adjT[:, ds(c, 1), ds(c * P, P)]).then_inc(kept, 1))
            dve.wait_ge(kept, T)
            each(dve, T, 4, lambda c, _:
                dve.tensor_tensor(adjT[:, ds(c, 1), ds(c * P, P)], diag[:, ds(c, 1), :], ident16[:, :].unsqueeze(1), ALU.max))

        @block.tensor
        def _(pe):
            def step(t, p):
                pe.wait_ge(masked, t + 1)
                if past(t, NB):
                    pe.wait_ge(act_out, t - NB + 1)
                    pe.wait_ge(dve_out, t - NB + 1)
                for c in range(T):
                    last = pe.transpose(flipped[p][:, c, :], mask[p][:, c * P:(c + 1) * P], ident16[:, :])
                last.then_inc(turned, 1)

            each(pe, T, NB, step)

        @block.scalar
        def _(act):
            def step(t, p):
                act.wait_ge(turned, t + 1)
                act.activation(adjT[:, 0:half, ds(t * P, P)], flipped[p][:, 0:half, :], ACT.Copy).then_inc(act_out, 1)

            each(act, T, NB, step)


def project_gnn(nc, hT, WT, wh_hi, wh_lo, whT_hi, whT_lo, norm_row, norm_col, ones):
    NB = 2
    with ExitStack() as ctx:
        s = Scope(nc, ctx, "wh_")
        junk = [s.sb(f"junk{i}", [P, D]) for i in range(NB)]
        squares = s.sb("squares", [P, T])
        sqT = [[s.sb(f"sqT{b}{d}", [P, GN]) for d in range(KD)] for b in range(2)]
        prod = [s.ps(f"prod{i}", [P, 512]) for i in range(NB)]
        prodT = [s.ps(f"prodT{i}", [P, GN]) for i in range(KD)]
        sums = s.ps("sums", [P, GN])
        made, sq_done, hi_done, lo_done = (s.sem(n) for n in ("made", "sq", "hi", "lo"))
        madeT, sqT_done, hiT_done, loT_done, sums_done, sums_out = (
            s.sem(n) for n in ("madeT", "sqT", "hiT", "loT", "sums", "sums_out"))
        (hT_hi, hT_lo), (WT_hi, WT_lo) = hT, WT
        block = ctx.enter_context(nc.Block())

        @block.tensor
        def _(pe):
            def tile(t, p):
                p = p % NB
                if past(t, NB):
                    pe.wait_ge(lo_done, t - NB + 1)
                for k in range(KD):
                    last = matmul3(pe, prod[p][:, 0:D], hT_hi[:, k, ds(t * P, P)], hT_lo[:, k, ds(t * P, P)],
                                   WT_hi[:, k, :], WT_lo[:, k, :], k == 0, k == KD - 1)
                last.then_inc(made, 1)

            each(pe, T, 2 * NB, tile)
            for g in range(G):
                for d in range(KD):
                    if g:
                        pe.wait_ge(loT_done, KD * (g - 1) + d + 1)
                    for k in range(KD):
                        dd, gg = slice(d * P, (d + 1) * P), slice(g * GN, (g + 1) * GN)
                        last = matmul3(pe, prodT[d][:, :], WT_hi[:, k, dd], WT_lo[:, k, dd],
                                       hT_hi[:, k, gg], hT_lo[:, k, gg], k == 0, k == KD - 1)
                    last.then_inc(madeT, 1)
                if g:
                    pe.wait_ge(sums_out, g)
                for d in range(KD):
                    pe.wait_ge(sqT_done, KD * g + d + 1)
                    last = pe.matmul(sums[:, :], lhsT=ones[:, :], rhs=sqT[g % 2][d][:, :], start=d == 0, stop=d == KD - 1)
                last.then_inc(sums_done, 1)

        @block.scalar
        def _(act):
            def tile(t, p):
                p = p % NB
                act.wait_ge(made, t + 1)
                if past(t, NB):
                    act.wait_ge(sq_done, t - NB + 1)
                act.activation(junk[p][:, :], prod[p][:, 0:D], ACT.Square, scale=UNWS,
                               accum_out=squares[:, ds(t, 1)]).then_inc(sq_done, 1)
                act.activation(wh_hi[:, ds(t, 1), 0:D], prod[p][:, 0:D].unsqueeze(1), ACT.Copy, scale=UNWS).then_inc(hi_done, 1)

            each(act, T, 2 * NB, tile)
            for g in range(G):
                for d in range(KD):
                    act.wait_ge(madeT, KD * g + d + 1)
                    if g >= 2:
                        act.wait_ge(sums_done, g - 1)
                    act.activation(sqT[g % 2][d][:, :], prodT[d][:, :], ACT.Square, scale=UNWS).then_inc(sqT_done, 1)
                    act.activation(whT_hi[:, d, g * GN:(g + 1) * GN], prodT[d][:, :], ACT.Copy, scale=UNWS).then_inc(hiT_done, 1)
                act.wait_ge(sums_done, g + 1)
                act.activation(norm_row[:, g * GN:(g + 1) * GN], sums[:, :], ACT.Copy).then_inc(sums_out, 1)
            act.wait_ge(sums_out, G)
            act.activation(norm_row[:, 0:N], norm_row[:, 0:N], ACT.Sqrt)
            act.wait_ge(sq_done, T)
            act.activation(norm_col[:, :], squares[:, :], ACT.Sqrt)

        @block.vector
        def _(dve):
            dve.memset(wh_hi[:, :, D:D + 1], 1.0)
            dve.memset(norm_row[:, N:N + GN], 1.0)

            def tile(t, p):
                p = p % NB
                dve.wait_ge(hi_done, t + 1)
                dve.scalar_tensor_tensor(wh_lo[:, ds(t, 1), :], prod[p][:, 0:D].unsqueeze(1), UNWS,
                                         wh_hi[:, ds(t, 1), 0:D], ALU.mult, ALU.subtract).then_inc(lo_done, 1)

            each(dve, T, 2 * NB, tile)
            for g in range(G):
                gg = slice(g * GN, (g + 1) * GN)
                for d in range(KD):
                    dve.wait_ge(hiT_done, KD * g + d + 1)
                    dve.scalar_tensor_tensor(whT_lo[:, d, gg], prodT[d][:, :], UNWS, whT_hi[:, d, gg],
                                             ALU.mult, ALU.subtract).then_inc(loT_done, 1)


def cosine_attention(nc, x, wh_hi, wh_lo, whT_hi, whT_lo, norm_row, norm_col, adjT, h_slots):
    NB, LAG, RB, BATCH = 8, 6, 4, T // 2
    with ExitStack() as ctx:
        s = Scope(nc, ctx, "cos_")
        log_den = s.sb("log_den", [P, T, GN])
        eps = s.sb("eps", [P, 1])
        rec = [s.sb(f"rec{i}", [P, GN]) for i in range(RB)]
        sim = [s.sb(f"sim{i}", [P, GN]) for i in range(2)]
        ex = [s.sb(f"ex{i}", [P, GN]) for i in range(2)]
        em = [s.sb(f"em{i}", [P, GN]) for i in range(2)]
        e_hi = [s.sb(f"e_hi{i}", [P, GN], F16) for i in range(NB)]
        e_lo = [s.sb(f"e_lo{i}", [P, GN], F16) for i in range(NB)]
        inv = s.sb("inv", [P, TG])
        zeros = s.sb("zeros", [P, 2 * D], F16)
        zeros_set, cleared = s.sem("zeros_set"), s.sem("cleared")
        dots = [s.ps(f"dots{i}", [P, GN]) for i in range(4)]
        out = [s.ps(f"out{i}", [P, 512]) for i in range(TG)]
        dots_done, eps_set, log_done, rec_done, sim_done, ex_done, em_done, hi_done, lo_done, out_done, inv_done, added = (
            s.sem(n) for n in ("dots", "eps", "log", "rec", "sim", "ex", "em", "hi", "lo", "out", "inv", "added"))
        block = ctx.enter_context(nc.Block())

        @block.sync
        def _(sp):
            sp.wait_ge(zeros_set, 1)
            for i in range(NT):
                sp.dma_start(h_slots[i * ST:(i + 1) * ST, :].rearrange("(q p) d -> p q d", p=P),
                             zeros[:, :].unsqueeze(1).to_broadcast([P, ST // P, 2 * D])).then_inc(cleared, 16)
            sp.wait_ge(cleared, 16 * NT)

        @block.tensor
        def _(pe):
            def scores(g, c):
                u = T * g + c
                if past(u, 4):
                    pe.wait_ge(sim_done, u - 3)
                for k in range(KD):
                    cc, gg = slice(c * P, (c + 1) * P), ds(g * GN, GN)
                    last = matmul3(pe, dots[c % 4][:, :], whT_hi[:, k, cc], whT_lo[:, k, cc],
                                   whT_hi[:, k, gg], whT_lo[:, k, gg], k == 0, k == KD - 1)
                last.then_inc(dots_done, 1)

            def weigh(g, c):
                u = T * g + c
                pe.wait_ge(lo_done, u + 1)
                if c == 0 and past(g, 1):
                    pe.wait_ge(added, TG * g)
                for q in range(TG):
                    qq = slice(q * P, (q + 1) * P)
                    pe.matmul(out[q][:, 0:D + 1], lhsT=e_hi[c % NB][:, qq], rhs=wh_hi[:, c, 0:D + 1], start=c == 0, stop=False)
                    pe.matmul(out[q][:, 0:D], lhsT=e_hi[c % NB][:, qq], rhs=wh_lo[:, c, :], start=False, stop=False)
                    last = pe.matmul(out[q][:, 0:D + 1], lhsT=e_lo[c % NB][:, qq], rhs=wh_hi[:, c, 0:D + 1], start=False, stop=c == T - 1)
                last.then_inc(out_done, 1)

            def group(g, _):
                for c in range(T):
                    scores(g, c)
                    if c >= LAG:
                        weigh(g, c - LAG)
                    elif past(g, 1):
                        weigh(g - 1, T - LAG + c)

            each(pe, G, 1, group)
            for c in range(T - LAG, T):
                weigh(G - 1, c)

        @block.scalar
        def _(act):
            def logarithms(g, first):
                for c in range(first, first + BATCH):
                    act.activation(log_den[:, c, :], norm_row[:, ds(g * GN, GN)], ACT.Ln, scale=norm_col[:, c:c + 1],
                                   bias=eps[:, :]).then_inc(log_done, 1)

            def inverse(g, c):
                u = T * g + c
                if past(u, RB):
                    act.wait_ge(sim_done, u - RB + 1)
                act.wait_ge(log_done, u + 1)
                act.activation(rec[c % RB][:, :], log_den[:, c, :], ACT.Exp, scale=-1.0).then_inc(rec_done, 1)

            def expo(g, c):
                u = T * g + c
                act.wait_ge(sim_done, u + 1)
                if past(u, 2):
                    act.wait_ge(em_done, u - 1)
                act.activation(ex[c % 2][:, :], sim[c % 2][:, :], ACT.Exp).then_inc(ex_done, 1)

            def high(g, c):
                u = T * g + c
                act.wait_ge(em_done, u + 1)
                if past(u, NB):
                    act.wait_ge(out_done, u - NB + 1)
                act.activation(e_hi[c % NB][:, :], em[c % 2][:, :], ACT.Copy).then_inc(hi_done, 1)

            def lagged(g, c, lag, do):
                if c >= lag:
                    do(g, c - lag)
                elif past(g, 1):
                    do(g - 1, c - lag + T)

            def group(g, _):
                for c in range(T):
                    turn = c == 2 or c == BATCH + 2
                    if turn and past(T * g + c, BATCH):
                        act.wait_ge(rec_done, T * g + c - 2)
                    inverse(g, c)
                    lagged(g, c, 2, expo)
                    lagged(g, c, 3, high)
                    if turn:
                        logarithms(g + c // BATCH, BATCH + 2 - c)

            act.wait_ge(eps_set, 1)
            logarithms(0, 0)
            each(act, G, 1, group)
            for c in range(T - 2, T):
                expo(G - 1, c)
                high(G - 1, c - 1)
            high(G - 1, T - 1)

        @block.vector
        def _(dve):
            dve.memset(eps[:, :], SIM_EPS).then_inc(eps_set, 1)
            dve.memset(zeros[:, :], 0.0).then_inc(zeros_set, 1)

            def similarity(g, c):
                u, b = T * g + c, c % 2
                dve.wait_ge(rec_done, u + 1)
                dve.wait_ge(dots_done, u + 1)
                if past(u, 2):
                    dve.wait_ge(ex_done, u - 1)
                dve.tensor_tensor(sim[b][:, :], dots[c % 4][:, :], rec[c % RB][:, :], ALU.mult).then_inc(sim_done, 1)

            def mask(g, c):
                u, b = T * g + c, c % 2
                dve.wait_ge(ex_done, u + 1)
                if past(u, 2):
                    dve.wait_ge(lo_done, u - 1)
                dve.tensor_tensor(em[b][:, :], ex[b][:, :], adjT[:, c, ds(g * GN, GN)], ALU.mult).then_inc(em_done, 1)

            def low(g, c):
                u = T * g + c
                dve.wait_ge(hi_done, u + 1)
                dve.tensor_tensor(e_lo[c % NB][:, :], em[c % 2][:, :], e_hi[c % NB][:, :], ALU.subtract).then_inc(lo_done, 1)

            def add(g):
                dve.wait_ge(out_done, T * g + T)
                for q in range(TG):
                    dve.reciprocal(inv[:, q:q + 1], out[q][:, D:D + 1]).then_inc(inv_done, 1)
                for q in range(TG):
                    dve.wait_ge(inv_done, TG * g + q + 1)
                    dve.scalar_tensor_tensor(x[:, ds(TG * g + q, 1), :], out[q][:, 0:D].unsqueeze(1), inv[:, q:q + 1],
                                             x[:, ds(TG * g + q, 1), :], ALU.mult, ALU.add).then_inc(added, 1)

            def group(g, _):
                for c in range(T):
                    similarity(g, c)
                    if c >= 1:
                        mask(g, c - 1)
                    elif past(g, 1):
                        mask(g - 1, T - 1)
                    if c >= 2:
                        low(g, c - 2)
                    elif past(g, 1):
                        low(g - 1, T - 2 + c)
                    if c == LAG and past(g, 1):
                        add(g - 1)

            each(dve, G, 1, group)
            mask(G - 1, T - 1)
            low(G - 1, T - 2)
            low(G - 1, T - 1)
            add(G - 1)


def l0_gnn(nc, a, x, ident, ident16, ones, adjT, h_slots):
    with ExitStack() as ctx:
        s = Scope(nc, ctx, "g0_")
        wh_hi, wh_lo = s.sb("wh_hi", [P, T, D + 2], F16), s.sb("wh_lo", [P, T, D], F16)
        whT_hi, whT_lo = s.sb("whT_hi", [P, KD, N], F16), s.sb("whT_lo", [P, KD, N], F16)
        norm_row, norm_col = s.sb("norm_row", [P, N + GN]), s.sb("norm_col", [P, T])
        with ExitStack() as inner:
            s = Scope(nc, inner, "g0_")
            hT = s.sb("hT_hi", [P, KD, N], F16), s.sb("hT_lo", [P, KD, N], F16)
            WT = s.sb("WT_hi", [P, KD, D], F16), s.sb("WT_lo", [P, KD, D], F16)
            with ExitStack() as stages:
                both = Together(nc, stages)
                normalize_and_turn(nc, "g0n_", ident, x, D, "layer", *hT, together=both)
                split_transposed_weights(nc, "g0w_", ident, [(a["L0_gnn_W"], WT[0][:, :, :], WT[1][:, :, :])], both)
            project_gnn(nc, hT, WT, wh_hi, wh_lo, whT_hi, whT_lo, norm_row, norm_col, ones)
        cosine_attention(nc, x, wh_hi, wh_lo, whT_hi, whT_lo, norm_row, norm_col, adjT, h_slots)


def route(nc, prefix, ident, experts, top, hT, Wg, bias, comb, picks=None):
    with ExitStack() as ctx:
        s = Scope(nc, ctx, prefix)
        shape = [P, T, experts]
        rank_i, rank = s.sb("rank_i", [P, experts], I32), s.sb("rank", [P, experts])
        scores, work, same, chosen = (s.sb(n, shape) for n in ("scores", "work", "same", "chosen"))
        best, first, peak = s.sb("best", [P, T]), s.sb("first", [P, T]), s.sb("peak", [P, T])
        logits = s.ps("logits", shape)
        made, rank_done, loaded, steps, ready, squashed = (s.sem(n) for n in ("made", "rank", "loaded", "steps", "ready", "squashed"))
        (hT_hi, hT_lo), (Wg_hi, Wg_lo) = hT, Wg
        over = lambda row: row.unsqueeze(1).to_broadcast(shape)
        along = lambda col: col.unsqueeze(2).to_broadcast(shape)
        if bias is not None:
            bias_sb = s.sb("bias", [P, experts])
        block = ctx.enter_context(nc.Block())

        @block.sync
        def _(sp):
            if bias is not None:
                sp.dma_start(bias_sb[:, :], bias.unsqueeze(0).to_broadcast([P, experts])).then_inc(loaded, 16)

        @block.gpsimd
        def _(pool):
            pool.iota(rank_i[:, :], pattern=[[-1, experts]], base=experts, channel_multiplier=0).then_inc(rank_done, 1)

        @block.tensor
        def _(pe):
            def step(t, p):
                for k in range(KD):
                    last = matmul3(pe, logits[:, ds(t, 1), :], hT_hi[:, k, ds(t * P, P)], hT_lo[:, k, ds(t * P, P)],
                                   Wg_hi[:, k, :], Wg_lo[:, k, :], k == 0, k == KD - 1)
                last.then_inc(made, 1)

            each(pe, T, 4, step)

        @block.scalar
        def _(act):
            act.wait_ge(ready, 1)
            if bias is None:
                act.activation(scores[:, :, :], logits[:, :, :], ACT.Sigmoid, scale=UNWS).then_inc(squashed, 1)
            else:
                act.activation(same[:, :, :], work[:, :, :], ACT.Exp).then_inc(squashed, 1)

        @block.vector
        def _(dve):
            link = Chain(dve, steps)
            dve.wait_ge(rank_done, 1)
            link(dve.tensor_copy(rank[:, :], rank_i[:, :]))
            dve.wait_ge(made, T)
            if bias is None:
                dve.engine_nop().then_inc(ready, 1)
                dve.wait_ge(squashed, 1)
            else:
                dve.wait_ge(loaded, 16)
                link(dve.scalar_tensor_tensor(scores[:, :, :], logits[:, :, :], UNWS, over(bias_sb[:, :]), ALU.mult, ALU.add))
            link(dve.tensor_copy(work[:, :, :], scores[:, :, :]))
            link(dve.memset(chosen[:, :, :], 0.0))
            for k in range(top):
                peak_k = first if k == 0 else peak
                link(dve.tensor_reduce(peak_k[:, :], work[:, :, :], AXF, ALU.max))
                link(dve.tensor_tensor(same[:, :, :], work[:, :, :], along(peak_k[:, :]), ALU.is_equal))
                link(dve.tensor_tensor(same[:, :, :], same[:, :, :], over(rank[:, :]), ALU.mult))
                link(dve.tensor_reduce(best[:, :], same[:, :, :], AXF, ALU.max))
                link(dve.tensor_tensor(same[:, :, :], over(rank[:, :]), along(best[:, :]), ALU.is_equal))
                if picks is not None:
                    link(dve.tensor_copy(picks[k][:, :, :], same[:, :, :]))
                link(dve.tensor_tensor(chosen[:, :, :], chosen[:, :, :], same[:, :, :], ALU.add))
                link(dve.scalar_tensor_tensor(work[:, :, :], same[:, :, :], -BIG, work[:, :, :], ALU.mult, ALU.add))
            if bias is None:
                link(dve.tensor_tensor(comb[:, :, :], scores[:, :, :], chosen[:, :, :], ALU.mult))
            else:
                link(dve.tensor_tensor(work[:, :, :], scores[:, :, :], along(first[:, :]), ALU.subtract))
                dve.engine_nop().then_inc(ready, 1)
                dve.wait_ge(squashed, 1)
                link(dve.tensor_tensor(comb[:, :, :], same[:, :, :], chosen[:, :, :], ALU.mult))
            link(dve.tensor_reduce(peak[:, :], comb[:, :, :], AXF, ALU.add))
            link(dve.reciprocal(best[:, :], peak[:, :]))
            link(dve.tensor_tensor(comb[:, :, :], comb[:, :, :], along(best[:, :]), ALU.mult))
            dve.tensor_scalar(comb[:, :, :], comb[:, :, :], UNWS, None, ALU.mult)


def load_turned_bias(nc, prefix, ident, src, rows, biasT, together):
    s = Scope(nc, together.ctx, prefix)
    raw, flipped = s.sb("raw", [rows, P]), s.ps("flipped", [P, rows])
    loaded, turned = s.sem("loaded"), s.sem("turned")
    block = together.block

    @block.sync
    def _(sp):
        sp.dma_start(raw[:, :], src).then_inc(loaded, 16)

    @block.tensor
    def _(pe):
        pe.wait_ge(loaded, 16)
        pe.transpose(flipped[:, :], raw[:, :], ident[0:rows, 0:rows]).then_inc(turned, 1)

    @block.vector
    def _(dve):
        dve.wait_ge(turned, 1)
        dve.tensor_copy(biasT[:, :], flipped[:, :])


def assign_slots(nc, prefix, ones, comb, picks, slots, weights, tile_expert):
    with ExitStack() as ctx:
        s = Scope(nc, ctx, prefix)
        shape = [P, T, L0_E]
        steps_of = N // ST
        earlier = s.sb("earlier", [P, P])
        chosen, place, part = (s.sb(n, shape) for n in ("chosen", "place", "part"))
        carry, ends, needed = s.sb("carry", [P, T + 1, L0_E]), s.sb("ends", [P, L0_E + 1]), s.sb("needed", [P, L0_E])
        full_i, full = s.sb("full_i", [P, steps_of], I32), s.sb("full", [P, steps_of])
        over_full = s.sb("over_full", [P, L0_E, steps_of])
        tile_i, tile = s.sb("tile_i", [1, NT], I32), s.sb("tile", [1, NT])
        behind, owner = s.sb("behind", [1, NT, L0_E - 1]), s.sb("owner", [1, NT])
        slot = s.sb("slot", [P, L0_K, T])
        before, total = s.ps("before", shape), s.ps("total", shape)
        cleared, tables, steps, summed, counted = (s.sem(n) for n in ("cleared", "tables", "steps", "summed", "counted"))
        block = ctx.enter_context(nc.Block())

        @block.gpsimd
        def _(pool):
            pool.iota(full_i[:, :], pattern=[[ST, steps_of]], base=0, channel_multiplier=0).then_inc(tables, 1)
            pool.iota(tile_i[:, :], pattern=[[1, NT]], base=0, channel_multiplier=0).then_inc(tables, 1)
            pool.memset(earlier[:, :], 1.0).then_inc(cleared, 1)
            pool.wait_ge(cleared, 1)
            pool.affine_select(out=earlier[:, :], in_=earlier[:, :], compare_op=ALU.is_gt, fill=0.0, base=0,
                               pattern=[[1, P]], channel_multiplier=-1).then_inc(tables, 1)

        @block.tensor
        def _(pe):
            pe.wait_ge(tables, 3)
            pe.wait_ge(summed, 1)
            pe.matmul(before[:, :, :], lhsT=earlier[:, :], rhs=chosen[:, :, :], start=True, stop=True)
            pe.matmul(total[:, :, :], lhsT=ones[:, :], rhs=chosen[:, :, :], start=True, stop=True).then_inc(counted, 1)

        @block.vector
        def _(dve):
            link = Chain(dve, steps)
            dve.tensor_tensor(chosen[:, :, :], picks[0][:, :, :], picks[1][:, :, :], ALU.add).then_inc(summed, 1)
            dve.wait_ge(tables, 3)
            link(dve.tensor_copy(full[:, :], full_i[:, :]))
            link(dve.tensor_copy(tile[:, :], tile_i[:, :]))
            link(dve.memset(carry[:, 0:1, :], 0.0))
            link(dve.memset(ends[:, 0:1], 0.0))
            dve.wait_ge(counted, 1)
            for t in range(T):
                link(dve.tensor_tensor(carry[:, t + 1:t + 2, :], carry[:, t:t + 1, :], total[:, t:t + 1, :], ALU.add))
            link(dve.tensor_tensor(over_full[:, :, :], carry[:, T, :].unsqueeze(2).to_broadcast([P, L0_E, steps_of]),
                                   full[:, :].unsqueeze(1).to_broadcast([P, L0_E, steps_of]), ALU.is_gt))
            link(dve.tensor_reduce(needed[:, :], over_full[:, :, :], AXF, ALU.add))
            for e in range(L0_E):
                link(dve.tensor_tensor(ends[:, e + 1:e + 2], ends[:, e:e + 1], needed[:, e:e + 1], ALU.add))
            spread = [1, NT, L0_E - 1]
            link(dve.tensor_tensor(behind[:, :, :], tile[:, :].unsqueeze(2).to_broadcast(spread),
                                   ends[0:1, 1:L0_E].unsqueeze(1).to_broadcast(spread), ALU.is_ge))
            link(dve.tensor_reduce(owner[:, :], behind[:, :, :], AXF, ALU.add))
            link(dve.tensor_copy(tile_expert[:, :], owner[:, :]))
            link(dve.tensor_tensor(place[:, :, :], before[:, :, :], carry[:, 0:T, :], ALU.add))
            link(dve.scalar_tensor_tensor(place[:, :, :], ends[:, 0:L0_E].unsqueeze(1).to_broadcast(shape), float(ST),
                                          place[:, :, :], ALU.mult, ALU.add))
            for k in range(L0_K):
                link(dve.tensor_tensor(part[:, :, :], picks[k][:, :, :], place[:, :, :], ALU.mult))
                link(dve.tensor_reduce(slot[:, k, :], part[:, :, :], AXF, ALU.add))
                link(dve.tensor_tensor(part[:, :, :], picks[k][:, :, :], comb[:, :, :], ALU.mult))
                link(dve.tensor_reduce(weights[:, k, :], part[:, :, :], AXF, ALU.add))
            dve.tensor_copy(slots[:, :, :], slot[:, :, :])


def l0_experts(nc, x, pair, ident, ident16, W1, b1T, W2, b2, comb, slots, tile_expert, h_slots, y_slots):
    QN, FP = ST // P, FC // 2
    with ExitStack() as ctx:
        s = Scope(nc, ctx, "e0_")
        raw1, raw2 = [s.sb(f"raw1{i}", [P, KD, L0_F]) for i in range(2)], [s.sb(f"raw2{i}", [P, FC, D]) for i in range(2)]
        w1 = [(s.sb(f"w1_hi{i}", [P, KD, L0_F], F16), s.sb(f"w1_lo{i}", [P, KD, L0_F], F16)) for i in range(2)]
        w2 = [(s.sb(f"w2_hi{i}", [P, FC, D], F16), s.sb(f"w2_lo{i}", [P, FC, D], F16)) for i in range(2)]
        b1 = [s.sb(f"b1_{i}", [P, FC]) for i in range(2)]
        rows = [s.sb(f"rows{i}", [P, QN, 2 * D], F16) for i in range(2)]
        hT = [s.sb(f"hT{i}", [P, 2 * KD, ST], F16) for i in range(2)]
        act_out = [s.sb(f"act{i}", [P, 2, ST]) for i in range(FP)]
        hid = [(s.sb(f"hid_hi{i}", [P, FC, ST], F16), s.sb(f"hid_lo{i}", [P, FC, ST], F16)) for i in range(2)]
        y = [s.sb(f"y{i}", [P, QN, D]) for i in range(2)]
        b2_sb = s.sb("b2", [L0_E, D])
        up = [s.ps(f"up{i}", [P, 2, ST]) for i in range(FP)]
        down = [s.ps(f"down{i}", [P, QN, D]) for i in range(2)]
        flipped = [s.ps(f"flipped{i}", [P, 2 * KD, ST], F16) for i in range(2)]
        scattered, turned, hT_done, up_done, act_done, hi_done, lo_done, down_done, y_done = (
            s.sem(n) for n in ("scattered", "turned", "hT", "up", "act", "hi", "lo", "down", "y"))
        w1_hi, w1_lo, w2_hi, w2_lo = (s.sem(n) for n in ("w1_hi", "w1_lo", "w2_hi", "w2_lo"))
        b2_in, comb_turned, comb_out, extra_done, extra_added = (
            s.sem(n) for n in ("b2_in", "comb_turned", "comb_out", "extra", "extra_added"))
        loaded1, loaded2, b1_in, rows_in, stored = (
            [s.sem(f"{n}{i}") for i in range(2)] for n in ("loaded1", "loaded2", "b1_in", "rows_in", "stored"))
        block = ctx.enter_context(nc.Block())

        def tiles(eng, step):
            each(eng, NT - NT % 2, 2, step)
            if NT % 2:
                step(NT - 1, 0)

        turned_comb = lambda bank, t: bank[t // 4][0:L0_E, t % 4 // 2, t % 2 * P:(t % 2 + 1) * P]
        exists = lambda i: not isinstance(i, int) or 0 <= i < NT

        @block.gpsimd
        def _(pool):
            for t in range(T):
                for k in range(L0_K):
                    pool.indirect_dma_start(h_slots[:, :], bass.IndirectOffsetOnAxis(slots[:, k, t:t + 1], 0),
                                            pair[:, t, :], None).then_inc(scattered, 16)

        @block.sync
        def _(sp):
            def load1(i, p):
                e = sp.value_load(tile_expert[0:1, ds(i, 1)], min_val=0, max_val=L0_E - 1)
                if past(i, 2):
                    sp.wait_ge(w1_lo, i - 1)
                sp.dma_start(raw1[p][:, :, :], W1[ds(e, 1)].rearrange("o (k p) f -> p (o k) f", p=P)).then_inc(loaded1[p], 16)

            def load2(i, p):
                e = sp.value_load(tile_expert[0:1, ds(i, 1)], min_val=0, max_val=L0_E - 1)
                if past(i, 2):
                    sp.wait_ge(w2_lo, i - 1)
                sp.dma_start(raw2[p][:, :, :], W2[ds(e, 1)].rearrange("o (k p) d -> p (o k) d", p=P)).then_inc(loaded2[p], 16)
                if past(i, 2):
                    sp.wait_ge(act_done, FP * (i - 1))
                sp.dma_start(b1[p][:, :], b1T[:, ds(e * FC, FC)]).then_inc(b1_in[p], 16)

            def load_rows(i, p):
                if past(i, 2):
                    sp.wait_ge(turned, i - 1)
                sp.dma_start(rows[p][:, :, :], h_slots[ds(i * ST, ST), :].rearrange("(q p) d -> p q d", p=P)).then_inc(rows_in[p], 16)

            def store(i, p):
                sp.wait_ge(y_done, i + 1)
                sp.dma_start(y_slots[ds(i * ST, ST), :].rearrange("(q p) d -> p q d", p=P), y[p][:, :, :]).then_inc(stored[p], 16)

            def step(i, p):
                if exists(i):
                    load_rows(i, p)
                    load2(i, p)
                store(i - 3, 1 - p)
                if exists(i + 1):
                    load1(i + 1, 1 - p)

            sp.dma_start(b2_sb[:, :], b2).then_inc(b2_in, 16)
            load1(0, 0)
            load2(0, 0)
            load1(1, 1)
            sp.wait_ge(scattered, 16 * T * L0_K)
            load_rows(0, 0)
            load_rows(1, 1)
            load2(1, 1)
            load1(2, 0)
            load_rows(2, 0)
            load2(2, 0)
            load1(3, 1)
            step(3, 1)
            with sp.Fori(2, NT // 2) as j:
                for p in range(2):
                    step(2 * j + p, p)
            for i in range(NT - NT % 2, NT + 3):
                step(i, i % 2)
            for b in range(2):
                sp.wait_ge(stored[b], 16 * ((NT + 1 - b) // 2))

        @block.tensor
        def _(pe):
            def turn(i, p):
                pe.wait_ge(rows_in[p], 8 * (i - p) + 16)
                if past(i, 2):
                    pe.wait_ge(hT_done, i - 1)
                for c in range(2 * KD):
                    for q in range(QN):
                        last = pe.transpose(flipped[p][:, c, q * P:(q + 1) * P], rows[p][:, q, c * P:(c + 1) * P], ident16[:, :])
                last.then_inc(turned, 1)

            def project_up(i, p):
                pe.wait_ge(w1_lo, i + 1)
                pe.wait_ge(hT_done, i + 1)
                for f in range(FC):
                    if f % 2 == 0 and past(i, 1):
                        pe.wait_ge(act_done, FP * (i - 1) + f // 2 + 1)
                    ff = slice(f * P, (f + 1) * P)
                    for k in range(KD):
                        last = matmul3(pe, up[f // 2][:, f % 2, :], w1[p][0][:, k, ff], w1[p][1][:, k, ff],
                                       hT[p][:, k, :], hT[p][:, KD + k, :], k == 0, k == KD - 1)
                    if f % 2:
                        last.then_inc(up_done, 1)

            def project_down(i, p):
                pe.wait_ge(w2_lo, i + 1)
                pe.wait_ge(lo_done, FP * (i + 1))
                if past(i, 2):
                    pe.wait_ge(y_done, i - 1)
                for q in range(QN):
                    qq = slice(q * P, (q + 1) * P)
                    for f in range(FC):
                        last = matmul3(pe, down[p][:, q, :], hid[p][0][:, f, qq], hid[p][1][:, f, qq],
                                       w2[p][0][:, f, :], w2[p][1][:, f, :], f == 0, f == FC - 1)
                last.then_inc(down_done, 1)

            def step(i, p):
                if exists(i + 1):
                    turn(i + 1, 1 - p)
                project_up(i, p)
                if past(i, 1):
                    project_down(i - 1, 1 - p)

            for t in range(T):
                last = pe.transpose(turned_comb(up, t), comb[:, t, :], ident[:, :])
            last.then_inc(comb_turned, 1)
            pe.wait_ge(comb_out, FP)
            pe.wait_ge(b2_in, 16)
            for t in range(T):
                if t >= 2:
                    pe.wait_ge(extra_added, t - 1)
                pe.matmul(down[t % 2][:, 0, :], lhsT=turned_comb(act_out, t), rhs=b2_sb[:, :], start=True, stop=True).then_inc(extra_done, 1)
            pe.wait_ge(extra_added, T)
            turn(0, 0)
            tiles(pe, step)
            project_down(NT - 1, (NT - 1) % 2)

        @block.scalar
        def _(act):
            def split1(i, p):
                act.wait_ge(loaded1[p], 8 * (i - p) + 16)
                if past(i, 2):
                    act.wait_ge(up_done, FP * (i - 1))
                act.activation(w1[p][0][:, :, :], raw1[p][:, :, :], ACT.Copy, scale=WS).then_inc(w1_hi, 1)

            def split2(i, p):
                act.wait_ge(loaded2[p], 8 * (i - p) + 16)
                if past(i, 2):
                    act.wait_ge(down_done, i - 1)
                act.activation(w2[p][0][:, :, :], raw2[p][:, :, :], ACT.Copy, scale=WS).then_inc(w2_hi, 1)

            def copy_turned(i, p):
                act.wait_ge(turned, i + 1)
                if past(i, 2):
                    act.wait_ge(up_done, FP * (i - 1))
                act.activation(hT[p][:, :, :], flipped[p][:, :, :], ACT.Copy).then_inc(hT_done, 1)

            def squash(i, p, pairs):
                for f2 in pairs:
                    n = FP * i + f2
                    act.wait_ge(up_done, n + 1)
                    if past(i, 1):
                        act.wait_ge(lo_done, n - FP + 1)
                    if f2 == 0:
                        act.wait_ge(b1_in[p], 8 * (i - p) + 16)
                    for h in range(2):
                        f = 2 * f2 + h
                        ins = act.activation(act_out[f2][:, h, :], up[f2][:, h, :], ACT.Silu, bias=b1[p][:, f:f + 1], scale=UNWS)
                    ins.then_inc(act_done, 1)

            def step(i, p):
                squash(i, p, (0,))
                if exists(i + 1):
                    copy_turned(i + 1, 1 - p)
                squash(i, p, (1,))
                split2(i, p)
                squash(i, p, (2, 3))
                if exists(i + 1):
                    split1(i + 1, 1 - p)

            split1(0, 0)
            act.wait_ge(comb_turned, 1)
            for j in range(FP):
                act.activation(act_out[j][0:L0_E, :, :], up[j][0:L0_E, :, :], ACT.Copy).then_inc(comb_out, 1)
            copy_turned(0, 0)
            tiles(act, step)

        @block.vector
        def _(dve):
            def split1(i, p):
                dve.wait_ge(w1_hi, i + 1)
                dve.scalar_tensor_tensor(w1[p][1][:, :, :], raw1[p][:, :, :], WS, w1[p][0][:, :, :], ALU.mult,
                                         ALU.subtract).then_inc(w1_lo, 1)

            def split2(i, p):
                dve.wait_ge(w2_hi, i + 1)
                dve.scalar_tensor_tensor(w2[p][1][:, :, :], raw2[p][:, :, :], WS, w2[p][0][:, :, :], ALU.mult,
                                         ALU.subtract).then_inc(w2_lo, 1)

            def hidden(i, p, pairs):
                for f2 in pairs:
                    n, ff = FP * i + f2, slice(2 * f2, 2 * f2 + 2)
                    dve.wait_ge(act_done, n + 1)
                    if f2 == 0 and past(i, 2):
                        dve.wait_ge(down_done, i - 1)
                    dve.tensor_copy(hid[p][0][:, ff, :], act_out[f2][:, :, :]).then_inc(hi_done, 1)
                    dve.wait_ge(hi_done, n + 1)
                    dve.tensor_tensor(hid[p][1][:, ff, :], act_out[f2][:, :, :], hid[p][0][:, ff, :],
                                      ALU.subtract).then_inc(lo_done, 1)

            def output(i, p):
                dve.wait_ge(down_done, i + 1)
                if past(i, 2):
                    dve.wait_ge(stored[p], 8 * (i - p))
                dve.tensor_copy(y[p][:, :, :], down[p][:, :, :]).then_inc(y_done, 1)

            def step(i, p):
                hidden(i, p, (0,))
                if past(i, 2):
                    output(i - 2, p)
                hidden(i, p, (1,))
                split2(i, p)
                hidden(i, p, (2, 3))
                if exists(i + 1):
                    split1(i + 1, 1 - p)

            split1(0, 0)
            for t in range(T):
                dve.wait_ge(extra_done, t + 1)
                dve.scalar_tensor_tensor(x[:, t, :], down[t % 2][:, 0, :], WS, x[:, t, :], ALU.mult, ALU.add).then_inc(extra_added, 1)
            tiles(dve, step)
            for i in (NT - 2, NT - 1):
                output(i, i % 2)


def l0_ffn(nc, a, x, ident, ident16, ones, slots, weights, y_slots, h_slots):
    with ExitStack() as ctx:
        s = Scope(nc, ctx, "f0_")
        pair, b1T = s.sb("pair", [P, T, 2 * D], F16), s.sb("b1T", [P, L0_E * FC])
        comb, tile_expert = s.sb("comb", [P, T, L0_E]), s.sb("tile_expert", [1, NT], I32)
        with ExitStack() as inner:
            s = Scope(nc, inner, "f0_")
            hT = s.sb("hT_hi", [P, KD, N], F16), s.sb("hT_lo", [P, KD, N], F16)
            Wg = s.sb("Wg_hi", [P, KD, L0_E], F16), s.sb("Wg_lo", [P, KD, L0_E], F16)
            picks = [s.sb(f"pick{k}", [P, T, L0_E]) for k in range(L0_K)]
            with ExitStack() as stages:
                both = Together(nc, stages)
                normalize_and_turn(nc, "f0n_", ident, x, D, "layer", *hT, tok_hi=pair[:, :, 0:D], tok_lo=pair[:, :, D:2 * D],
                                   together=both)
                load_turned_bias(nc, "f0b_", ident, a["L0_ffn_b1"].rearrange("e (f p) -> (e f) p", p=P), L0_E * FC, b1T, both)
                split_weights(nc, "f0w_", [(a["L0_ffn_Wg"].rearrange("(k p) e -> p k e", p=P), None, Wg[0][:, :, :], Wg[1][:, :, :])],
                              both)
            route(nc, "f0r_", ident, L0_E, L0_K, hT, Wg, a["L0_ffn_bg"], comb, picks)
            assign_slots(nc, "f0s_", ones, comb, picks, slots, weights, tile_expert)
        l0_experts(nc, x, pair, ident, ident16, a["L0_ffn_W1"], b1T, a["L0_ffn_W2"], a["L0_ffn_b2"], comb, slots,
                   tile_expert, h_slots, y_slots)


def keep_first_neighbors(nc, adjT, diag, upper, ones16, x, y_slots, slots, weights):
    YB = 2 * L0_K
    with ExitStack() as ctx:
        s = Scope(nc, ctx, "keep_")
        before = [s.sb(f"before{i}", [P, N], F16) for i in range(2)]
        fetched = [s.sb(f"fetched{i}", [P, D]) for i in range(YB)]
        fetch_done, added = [s.sem(f"fetch{i}") for i in range(YB)], s.sem("added")
        count = [s.ps(f"count{i}", [P, GN]) for i in range(8)]
        restored, cleared, summed, counted, kept = (s.sem(n) for n in ("restored", "cleared", "summed", "counted", "kept"))
        block = ctx.enter_context(nc.Block())

        @block.gpsimd
        def _(pool):
            for n in range(T * L0_K):
                t, k = n // L0_K, n % L0_K
                if n >= YB:
                    pool.wait_ge(added, n - YB + 1)
                pool.indirect_dma_start(fetched[n % YB][:, :], None, y_slots[:, :],
                                        bass.IndirectOffsetOnAxis(slots[:, k, t:t + 1], 0)).then_inc(fetch_done[n % YB], 16)

        @block.tensor
        def _(pe):
            def chunk(c, p):
                if not past(c, 1):
                    pe.wait_ge(restored, T)
                    pe.wait_ge(cleared, 1)
                else:
                    pe.wait_ge(summed, c)
                for g in range(G):
                    n = G * c + g
                    if past(n, 8):
                        pe.wait_ge(kept, n - 7)
                    gg = slice(g * GN, (g + 1) * GN)
                    b = G * (p % 2) + g
                    pe.matmul(count[b][:, :], lhsT=upper[:, :], rhs=adjT[:, ds(c, 1), gg], start=True, stop=False)
                    pe.matmul(count[b][:, :], lhsT=ones16[:, :], rhs=before[p % 2][:, gg], start=False, stop=True).then_inc(counted, 1)

            each(pe, T, 4, chunk)

        @block.vector
        def _(dve):
            each(dve, T, 4, lambda c, _:
                dve.tensor_copy(adjT[:, ds(c, 1), ds(c * P, P)], diag[:, ds(c, 1), :]).then_inc(restored, 1))
            dve.wait_ge(restored, T)
            dve.memset(before[0][:, :], 0.0).then_inc(cleared, 1)
            dve.wait_ge(cleared, 1)

            def chunk(c, p):
                if past(c, 1):
                    dve.wait_ge(summed, c)
                    dve.wait_ge(counted, G * c)
                dve.tensor_tensor(before[1 - p % 2][:, :].unsqueeze(1), before[p % 2][:, :].unsqueeze(1), adjT[:, ds(c, 1), :],
                                  ALU.add).then_inc(summed, 1)
                dve.wait_ge(summed, c + 1)
                for g in range(G):
                    b, gg = G * (p % 2) + g, slice(g * GN, (g + 1) * GN)
                    dve.wait_ge(counted, G * c + g + 1)
                    dve.scalar_tensor_tensor(adjT[:, ds(c, 1), gg], count[b][:, :].unsqueeze(1), float(NEIGHBORS),
                                             adjT[:, ds(c, 1), gg], ALU.is_le, ALU.mult).then_inc(kept, 1)
                for k in range(L0_K):
                    b = L0_K * (p % 2) + k
                    dve.wait_ge(fetch_done[b], 8 * (c - p % 2) + 16)
                    if k:
                        dve.wait_ge(added, L0_K * c + k)
                    dve.scalar_tensor_tensor(x[:, ds(c, 1), :], fetched[b][:, :].unsqueeze(1), weights[:, k, ds(c, 1)],
                                             x[:, ds(c, 1), :], ALU.mult, ALU.add).then_inc(added, 1)

            each(dve, T, 4, chunk)


def neighbor_mean(nc, keep, xn_hi, xn_lo, mean, has):
    NB = 4
    with ExitStack() as ctx:
        s = Scope(nc, ctx, "mean_")
        inv, cnt = [s.sb(f"inv{i}", [P, 1]) for i in range(NB)], [s.sb(f"cnt{i}", [P, 1]) for i in range(NB)]
        total = [s.ps(f"total{i}", [P, 512]) for i in range(NB)]
        summed, counted, inverted, used = (s.sem(n) for n in ("summed", "counted", "inverted", "used"))
        block = ctx.enter_context(nc.Block())

        @block.tensor
        def _(pe):
            def tile(t, p):
                if past(t, NB):
                    pe.wait_ge(used, t - NB + 1)
                for c in range(T):
                    pe.matmul(total[p][:, 0:D + 1], lhsT=keep[:, c, ds(t * P, P)], rhs=xn_hi[:, c, 0:D + 1], start=c == 0, stop=False)
                    last = pe.matmul(total[p][:, 0:D], lhsT=keep[:, c, ds(t * P, P)], rhs=xn_lo[:, c, :], start=False, stop=c == T - 1)
                last.then_inc(summed, 1)

            each(pe, T, NB, tile)

        @block.vector
        def _(dve):
            def tile(t, p):
                if past(t, NB):
                    dve.wait_ge(used, t - NB + 1)
                dve.wait_ge(summed, t + 1)
                dve.tensor_scalar(has[:, ds(t, 1)], total[p][:, D:D + 1], 0.0, None, ALU.is_gt)
                dve.tensor_scalar(cnt[p][:, :], total[p][:, D:D + 1], 1.0, None, ALU.max).then_inc(counted, 1)
                dve.wait_ge(counted, t + 1)
                dve.reciprocal(inv[p][:, :], cnt[p][:, :]).then_inc(inverted, 1)
                dve.wait_ge(inverted, t + 1)
                dve.tensor_scalar(mean[:, ds(t, 1), :], total[p][:, 0:D].unsqueeze(1), inv[p][:, :], None, ALU.mult).then_inc(used, 1)

            each(dve, T, NB, tile)


def gnn_outputs(nc, a, x, xnT, meanT, W_line, W_nb, has):
    NB = 4
    with ExitStack() as ctx:
        s = Scope(nc, ctx, "go_")
        biases = [s.sb(n, [P, D]) for n in ("b_line", "b_nb")]
        val = [[s.sb(f"val{j}{i}", [P, D]) for i in range(NB)] for j in range(2)]
        leaky = [[s.sb(f"leaky{j}{i}", [P, D]) for i in range(NB)] for j in range(2)]
        prod = [[s.ps(f"prod{j}{i}", [P, 512]) for i in range(NB)] for j in range(2)]
        loaded, made, biased, bent, added = (s.sem(n) for n in ("loaded", "made", "biased", "bent", "added"))
        block = ctx.enter_context(nc.Block())

        @block.sync
        def _(sp):
            for b, src in zip(biases, (a["L1_gnn_b_line"], a["L1_gnn_b_nb"])):
                sp.dma_start(b[:, :], src.unsqueeze(0).to_broadcast([P, D])).then_inc(loaded, 16)

        @block.tensor
        def _(pe):
            def tile(t, p):
                for j, (hT, W) in enumerate(((xnT, W_line), (meanT, W_nb))):
                    if past(t, NB):
                        pe.wait_ge(biased, 2 * (t - NB) + j + 1)
                    for k in range(KD):
                        last = matmul3(pe, prod[j][p][:, 0:D], hT[0][:, k, ds(t * P, P)], hT[1][:, k, ds(t * P, P)],
                                       W[0][:, k, :], W[1][:, k, :], k == 0, k == KD - 1)
                    last.then_inc(made, 1)

            each(pe, T, NB, tile)

        @block.vector
        def _(dve):
            dve.wait_ge(loaded, 32)

            def tile(t, p):
                for j in range(2):
                    dve.wait_ge(made, 2 * t + j + 1)
                    dve.scalar_tensor_tensor(val[j][p][:, :], prod[j][p][:, 0:D], UNWS, biases[j][:, :], ALU.mult,
                                             ALU.add).then_inc(biased, 1)
                for j in range(2):
                    dve.wait_ge(biased, 2 * t + j + 1)
                    dve.scalar_tensor_tensor(leaky[j][p][:, :], val[j][p][:, :], 0.01, val[j][p][:, :], ALU.mult,
                                             ALU.max).then_inc(bent, 1)
                xt = x[:, ds(t, 1), :]
                dve.wait_ge(bent, 2 * t + 1)
                dve.tensor_tensor(xt, leaky[0][p][:, :].unsqueeze(1), xt, ALU.add).then_inc(added, 1)
                dve.wait_ge(bent, 2 * t + 2)
                dve.wait_ge(added, 2 * t + 1)
                dve.scalar_tensor_tensor(xt, leaky[1][p][:, :].unsqueeze(1), has[:, ds(t, 1)], xt, ALU.mult, ALU.add).then_inc(added, 1)

            each(dve, T, NB, tile)


def make_triangle(nc, upper, ones16):
    with ExitStack() as ctx:
        s = Scope(nc, ctx, "tri_")
        filled = s.sem("filled")
        block = ctx.enter_context(nc.Block())

        @block.gpsimd
        def _(pool):
            pool.memset(ones16[:, :], 1.0)
            pool.memset(upper[:, :], 1.0).then_inc(filled, 1)
            pool.wait_ge(filled, 1)
            pool.affine_select(out=upper[:, :], in_=upper[:, :], compare_op=ALU.is_ge, fill=0.0, base=0,
                               pattern=[[1, P]], channel_multiplier=-1)


def l1_gnn(nc, a, x, ident, adjT, diag, slots, weights, y_slots):
    with ExitStack() as ctx:
        s = Scope(nc, ctx, "g1_")
        xnT = s.sb("xnT_hi", [P, KD, N], F16), s.sb("xnT_lo", [P, KD, N], F16)
        meanT = s.sb("meanT_hi", [P, KD, N], F16), s.sb("meanT_lo", [P, KD, N], F16)
        xn_hi, xn_lo = s.sb("xn_hi", [P, T, D + 2], F16), s.sb("xn_lo", [P, T, D], F16)
        mean, has = s.sb("mean", [P, T, D]), s.sb("has", [P, T])
        W_line = s.sb("W_line_hi", [P, KD, D], F16), s.sb("W_line_lo", [P, KD, D], F16)
        W_nb = s.sb("W_nb_hi", [P, KD, D], F16), s.sb("W_nb_lo", [P, KD, D], F16)
        upper, ones16 = s.sb("upper", [P, P], F16), s.sb("ones16", [P, P], F16)
        make_triangle(nc, upper, ones16)
        keep_first_neighbors(nc, adjT, diag, upper, ones16, x, y_slots, slots, weights)
        with ExitStack() as stages:
            both = Together(nc, stages)
            normalize_and_turn(nc, "g1n_", ident, x, D, "layer", *xnT, tok_hi=xn_hi, tok_lo=xn_lo, together=both)
            split_transposed_weights(nc, "g1w_", ident, [(a["L1_gnn_W_line"], W_line[0][:, :, :], W_line[1][:, :, :]),
                                                         (a["L1_gnn_W_nb"], W_nb[0][:, :, :], W_nb[1][:, :, :])], both)
        neighbor_mean(nc, adjT, xn_hi, xn_lo, mean, has)
        normalize_and_turn(nc, "g1m_", ident, mean, D, None, *meanT)
        gnn_outputs(nc, a, x, xnT, meanT, W_line, W_nb, has)


def latent_project(nc, a, xT, W_hi, W_lo, c_q, c_kv, k_rope, cos, sin):
    NB = 4
    with ExitStack() as ctx:
        s = Scope(nc, ctx, "lat_")
        raw_k = s.sb("raw_k", [P, T, ROPE])
        turned = s.sb("turned", [P, T, ROPE])
        prod = [s.ps(f"prod{i}", [P, 512]) for i in range(NB)]
        made, out_done, loaded, parts = (s.sem(n) for n in ("made", "out", "loaded", "parts"))
        block = ctx.enter_context(nc.Block())
        H = ROPE // 2

        @block.sync
        def _(sp):
            sp.dma_start(cos[:, :, :], a["rope_cos"].rearrange("(t p) d -> p t d", p=P)).then_inc(loaded, 16)
            sp.dma_start(sin[:, :, :], a["rope_sin"].rearrange("(t p) d -> p t d", p=P)).then_inc(loaded, 16)

        @block.tensor
        def _(pe):
            def tile(t, p):
                if past(t, NB):
                    pe.wait_ge(out_done, 3 * (t - NB) + 3)
                for k in range(KD):
                    last = matmul3(pe, prod[p][:, 0:DQ + DKV + ROPE], xT[0][:, k, ds(t * P, P)], xT[1][:, k, ds(t * P, P)],
                                   W_hi[:, k, :], W_lo[:, k, :], k == 0, k == KD - 1)
                last.then_inc(made, 1)

            each(pe, T, NB, tile)

        @block.scalar
        def _(act):
            def tile(t, p):
                act.wait_ge(made, t + 1)
                for dst, at, w in ((c_q, 0, DQ), (c_kv, DQ, DKV), (raw_k, DQ + DKV, ROPE)):
                    act.activation(dst[:, ds(t, 1), :], prod[p][:, at:at + w].unsqueeze(1), ACT.Copy, scale=UNWS).then_inc(out_done, 1)

            each(act, T, NB, tile)

        @block.vector
        def _(dve):
            dve.wait_ge(loaded, 32)
            dve.wait_ge(out_done, 3 * T)
            dve.tensor_tensor(turned[:, :, 0:H], raw_k[:, :, H:ROPE], sin[:, :, 0:H], ALU.mult).then_inc(parts, 1)
            dve.tensor_tensor(turned[:, :, H:ROPE], raw_k[:, :, 0:H], sin[:, :, H:ROPE], ALU.mult).then_inc(parts, 1)
            dve.tensor_tensor(k_rope[:, :, :], raw_k[:, :, :], cos[:, :, :], ALU.mult).then_inc(parts, 1)
            dve.wait_ge(parts, 3)
            dve.tensor_tensor(k_rope[:, :, :], k_rope[:, :, :], turned[:, :, :], ALU.add)


def queries_keys_values(nc, prefix, ident, cqT, ckvT, W_uq, W_ukv, k_rope, cos, sin, qT, kT, V, qk_dram, v_dram, first):
    H = ROPE // 2
    with ExitStack() as ctx:
        s = Scope(nc, ctx, prefix)
        tok = [[s.sb(f"tok{j}{i}", [P, HH, QK]) for i in range(2)] for j in range(2)]
        kept = [s.sb(f"kept{i}", [P, HH, ROPE]) for i in range(2)]
        swapped = [s.sb(f"swapped{i}", [P, HH, ROPE]) for i in range(2)]
        q_ps = [s.ps(f"q{i}", [P, HH, P]) for i in range(2)]
        kv_ps = [s.ps(f"kv{i}", [P, HH, 2 * UP]) for i in range(2)]
        flipped = [[s.ps(f"flipped{j}{i}", [P, HH, P]) for i in range(2)] for j in range(2)]
        q_made, kv_made, q_out, kv_out, v_lo, rot, rotated, k_ready, turned, hi_done, lo_done = (
            s.sem(n) for n in ("q_made", "kv_made", "q_out", "kv_out", "v_lo", "rot", "rotated", "k_ready",
                               "turned", "hi", "lo"))
        spilled, v_ones = s.sem("spilled"), s.sem("v_ones")
        block = ctx.enter_context(nc.Block())

        @block.sync
        def _(sp):
            heads = slice(first, first + HH)
            sp.wait_ge(v_ones, 1)
            for g in range(G):
                gg, tt = slice(g * GN, (g + 1) * GN), slice(g * TG, (g + 1) * TG)
                sp.wait_ge(v_lo, TG * (g + 1))
                for h in range(HH):
                    sp.dma_start(v_dram[first + h][:, tt, :], V[:, tt, h, :]).then_inc(spilled, 16)
                sp.wait_ge(lo_done, 2 * TG * (g + 1))
                for n, part in ((Q_HI, qT[0]), (K_HI, kT[0]), (Q_LO, qT[1]), (K_LO, kT[1])):
                    sp.dma_start(qk_dram[heads, :, n, gg].rearrange("h r s -> r h s"), part[0:QK, :, gg]).then_inc(spilled, 16)
            sp.wait_ge(spilled, 16 * G * (HH + 4))

        @block.tensor
        def _(pe):
            def turn(t, p):
                pe.wait_ge(rotated, t + 1)
                pe.wait_ge(k_ready, t + 1)
                pe.wait_ge(kv_out, t + 1)
                for j in range(2):
                    if past(t, 2):
                        pe.wait_ge(lo_done, 2 * (t - 2) + j + 1)
                    for h in range(HH):
                        last = pe.transpose(flipped[j][p][0:QK, h, :], tok[j][p][:, h, :], ident[:, :])
                    last.then_inc(turned, 1)

            def tile(t, p):
                p = p % 2
                if past(t, 2):
                    pe.wait_ge(q_out, t - 1)
                matmul3(pe, q_ps[p][:, :, :].rearrange("p h d -> p (h d)")[:, 0:HH * QK], cqT[0][:, 0, ds(t * P, P)],
                        cqT[1][:, 0, ds(t * P, P)], W_uq[0], W_uq[1], True, True).then_inc(q_made, 1)
                if past(t, 2):
                    pe.wait_ge(kv_out, t - 1)
                    pe.wait_ge(v_lo, t - 1)
                matmul3(pe, kv_ps[p][:, :, :], ckvT[0][:, 0, ds(t * P, P)], ckvT[1][:, 0, ds(t * P, P)],
                        W_ukv[0], W_ukv[1], True, True).then_inc(kv_made, 1)
                if past(t, 1):
                    turn(t - 1, 1 - p)

            each(pe, T, 4, tile)
            turn(T - 1, (T - 1) % 2)

        @block.scalar
        def _(act):
            def high(t, p):
                for j, dst in enumerate((qT, kT)):
                    act.wait_ge(turned, 2 * t + j + 1)
                    act.activation(dst[0][0:QK, :, ds(t * P, P)], flipped[j][p][0:QK, :, :], ACT.Copy).then_inc(hi_done, 1)

            def tile(t, p):
                p = p % 2
                act.wait_ge(q_made, t + 1)
                if past(t, 2):
                    act.wait_ge(turned, 2 * (t - 2) + 2)
                act.activation(tok[0][p][:, :, :].rearrange("p h d -> p (h d)"),
                               q_ps[p][:, :, :].rearrange("p h d -> p (h d)")[:, 0:HH * QK], ACT.Copy,
                               scale=UNWS * ATT_SCALE).then_inc(q_out, 1)
                act.wait_ge(kv_made, t + 1)
                act.activation(V[:, ds(t, 1), :, UP:2 * UP], kv_ps[p][:, :, UP:2 * UP].unsqueeze(1), ACT.Copy, scale=UNWS)
                act.activation(tok[1][p][:, :, 0:UP], kv_ps[p][:, :, 0:UP], ACT.Copy, scale=UNWS).then_inc(kv_out, 1)
                if past(t, 1):
                    high(t - 1, 1 - p)

            each(act, T, 4, tile)
            high(T - 1, (T - 1) % 2)

        @block.vector
        def _(dve):
            dve.memset(V[:, :, :, 2 * UP:2 * UP + 2], 1.0).then_inc(v_ones, 1)

            def low(t, p):
                for j, dst in enumerate((qT, kT)):
                    dve.wait_ge(hi_done, 2 * t + j + 1)
                    dve.tensor_tensor(dst[1][0:QK, :, ds(t * P, P)], flipped[j][p][0:QK, :, :], dst[0][0:QK, :, ds(t * P, P)],
                                      ALU.subtract).then_inc(lo_done, 1)

            def tile(t, p):
                p = p % 2
                r = tok[0][p][:, :, UP:QK]
                wide = lambda table: table.to_broadcast([P, HH, table.shape[-1]])
                if past(t, 2):
                    dve.wait_ge(turned, 2 * (t - 2) + 2)
                    dve.wait_ge(rotated, t - 1)
                dve.tensor_tensor(tok[1][p][:, :, UP:QK], wide(k_rope[:, ds(t, 1), :]), wide(k_rope[:, ds(t, 1), :]),
                                  ALU.max).then_inc(k_ready, 1)
                dve.wait_ge(q_out, t + 1)
                dve.tensor_tensor(kept[p][:, :, :], r, wide(cos[:, ds(t, 1), :]), ALU.mult).then_inc(rot, 1)
                dve.tensor_tensor(swapped[p][:, :, 0:H], r[:, :, H:ROPE], wide(sin[:, ds(t, 1), 0:H]), ALU.mult).then_inc(rot, 1)
                dve.tensor_tensor(swapped[p][:, :, H:ROPE], r[:, :, 0:H], wide(sin[:, ds(t, 1), H:ROPE]), ALU.mult).then_inc(rot, 1)
                dve.wait_ge(rot, 3 * t + 3)
                dve.tensor_tensor(r, kept[p][:, :, :], swapped[p][:, :, :], ALU.add).then_inc(rotated, 1)
                dve.wait_ge(kv_out, t + 1)
                dve.scalar_tensor_tensor(V[:, ds(t, 1), :, 0:UP], kv_ps[p][:, :, UP:2 * UP].unsqueeze(1), UNWS,
                                         V[:, ds(t, 1), :, UP:2 * UP], ALU.mult, ALU.subtract).then_inc(v_lo, 1)
                if past(t, 1):
                    low(t - 1, 1 - p)

            each(dve, T, 4, tile)
            low(T - 1, (T - 1) % 2)


def load_head(sp, h, qk, v, qk_dram, v_dram, loaded):
    sp.dma_start(qk[0:QK, :, :], qk_dram[h]).then_inc(loaded, 16)
    sp.dma_start(v[:, :, :], v_dram[h]).then_inc(loaded, 16)


def load_probe(sp, h, probe_qk, qk_dram, loaded):
    sp.dma_start(probe_qk[0:QK, :, :], qk_dram[h][:, 0:2, :]).then_inc(loaded, 16)


def first_head_maxima(nc, ident, qk, v, probe_qk, qk_dram, v_dram):
    with ExitStack() as ctx:
        s = Scope(nc, ctx, "max_")
        top, negated, rows = s.sb("top", [P, T]), s.sb("negated", [P, T]), s.sb("rows", [T, P], F16)
        scores = [s.ps(f"scores{i}", [P, N]) for i in range(2)]
        loaded, probe_loaded, made, reduced, put, turned, rounded, moved = (
            s.sem(n) for n in ("loaded", "probe_loaded", "made", "reduced", "put", "turned", "rounded", "moved"))
        block = ctx.enter_context(nc.Block())

        @block.tensor
        def _(pe):
            pe.wait_ge(loaded, 32)
            for t in range(T):
                if t >= 2:
                    pe.wait_ge(reduced, t - 1)
                for g in range(G):
                    gg = slice(g * GN, (g + 1) * GN)
                    last = pe.matmul(scores[t % 2][:, gg], lhsT=qk[0][0:QK, Q_HI, t * P:(t + 1) * P], rhs=qk[0][0:QK, K_HI, gg],
                                     start=True, stop=True)
                last.then_inc(made, 1)
            pe.wait_ge(put, 1)
            pe.transpose(scores[0][0:T, 0:P], negated[:, :], ident[:, :]).then_inc(turned, 1)

        @block.vector
        def _(dve):
            for b in range(2):
                dve.memset(qk[b][QK:QK + 1, K_HI, :], 1.0)
            for t in range(T):
                dve.wait_ge(made, t + 1)
                dve.tensor_reduce(top[:, t:t + 1], scores[t % 2][:, :], AXF, ALU.max).then_inc(reduced, 1)
            dve.wait_ge(reduced, T)
            dve.tensor_scalar(negated[:, :], top[:, :], -1.0, None, ALU.mult).then_inc(put, 1)
            dve.wait_ge(turned, 1)
            dve.tensor_copy(rows[:, :], scores[0][0:T, 0:P]).then_inc(rounded, 1)

        @block.sync
        def _(sp):
            load_head(sp, 0, qk[0], v[0], qk_dram, v_dram, loaded)
            load_probe(sp, 1, probe_qk[1], qk_dram, probe_loaded)
            sp.wait_ge(rounded, 1)
            sp.dma_start(qk[0][QK:QK + 1, Q_HI, :].rearrange("o (t j) -> o t j", j=P), rows[:, :]).then_inc(moved, 16)
            sp.wait_ge(moved, 16)
            sp.wait_ge(probe_loaded, 16)


def attention(nc, a, ident, qk, v, probe_qk, qk_dram, v_dram, heads, raw):
    NB, PB, SB, LAG, FIN, CUT = 8, 4, 3, 5, 7, 2
    HEAD, ROUND, ROUNDS = G * T, 2 * G * T, HEADS // 2
    with ExitStack() as ctx:
        s = Scope(nc, ctx, "att_")
        prob = [s.sb(f"prob{i}", [P, GN]) for i in range(PB)]
        p_hi = [s.sb(f"p_hi{i}", [P, GN], F16) for i in range(NB)]
        p_lo = [s.sb(f"p_lo{i}", [P, GN], F16) for i in range(NB)]
        v_low, total = ([s.sb(f"{n}{i}", [P, TG, UP]) for i in range(2)] for n in ("v_low", "total"))
        inv = [s.sb(f"inv{i}", [P, TG]) for i in range(2)]
        part = [s.sb(f"part{i}", [P, TG, G]) for i in range(2)]
        peak, negated, rows = s.sb("peak", [P, TG]), s.sb("negated", [P, TG]), s.sb("rows", [TG, P], F16)
        score = [s.ps(f"score{i}", [P, GN]) for i in range(SB)]
        probe = s.ps("probe", [P, GN])
        out = [s.ps(f"out{i}", [P, TG, 256]) for i in range(2)]
        scored, prob_done, hi_done, lo_done, weighed, low_out, summed, inverted, divided = (
            s.sem(n) for n in ("scored", "prob", "hi", "lo", "weighed", "low_out", "summed", "inverted", "divided"))
        probed, reduced, peaked, put, turned, rounded, moved = (
            s.sem(n) for n in ("probed", "reduced", "peaked", "put", "turned", "rounded", "moved"))
        loaded, probe_loaded = ([s.sem(f"{n}{i}") for i in range(2)] for n in ("loaded", "probe_loaded"))
        raw_loaded = s.sem("raw_loaded")
        block = ctx.enter_context(nc.Block())

        def rounds(eng, step):
            def one(j, _):
                for k in range(ROUND):
                    step(j, k)

            each(eng, ROUNDS, 1, one)

        def back(j, k, lag, do):
            if k >= lag:
                do(j, k - lag)
            elif past(j, 1):
                do(j - 1, k - lag + ROUND)

        def at_group(j, k, at, do):
            if k % T == at:
                back(j, k, T, lambda j, k: do(j, k // T))

        @block.tensor
        def _(pe):
            def scores(j, k):
                m, p, g, c, b = ROUND * j + k, k // HEAD, k // T % G, k % T, k % SB
                if k % HEAD == 0:
                    if p or past(j, 1):
                        pe.wait_ge(loaded[p], 32 * (j + p))
                    if p or past(j, 1):
                        pe.wait_ge(probe_loaded[1 - p], 16 * (j + p))
                if k % T == 0 and (p or past(j, 1)):
                    pe.wait_ge(moved, 16 * (2 * G * j + k // T - G + 1))
                if k < 2 and past(j, 1):
                    pe.wait_ge(hi_done, m - 1)
                elif past(m, SB):
                    pe.wait_ge(hi_done, m - SB + 1)
                cc, gg = slice(c * P, (c + 1) * P), slice(g * GN, (g + 1) * GN)
                pe.matmul(score[b][:, :], lhsT=qk[p][0:QK + 1, K_HI, cc], rhs=qk[p][0:QK + 1, Q_HI, gg], start=True, stop=False)
                pe.matmul(score[b][:, :], lhsT=qk[p][0:QK, K_HI, cc], rhs=qk[p][0:QK, Q_LO, gg], start=False, stop=False)
                pe.matmul(score[b][:, :], lhsT=qk[p][0:QK, K_LO, cc], rhs=qk[p][0:QK, Q_HI, gg], start=False,
                          stop=True).then_inc(scored, 1)

            def next_maxima(j, k):
                m, p, g, c = ROUND * j + k, k // HEAD, k // T % G, k % T
                if past(m, 1):
                    pe.wait_ge(reduced, m)
                if c == CUT and past(m, T):
                    n = 2 * G * j + k // T
                    pe.wait_ge(put, n)
                    pe.transpose(probe[0:TG, 0:P], negated[:, :], ident[:, :]).then_inc(turned, 1)
                    pe.wait_ge(rounded, n)
                t, gg = TG * g + c // G, slice(c % G * GN, (c % G + 1) * GN)
                pe.matmul(probe[:, :], lhsT=probe_qk[1 - p][0:QK, 0, t * P:(t + 1) * P], rhs=probe_qk[1 - p][0:QK, 1, gg],
                          start=True, stop=True).then_inc(probed, 1)

            def weigh(j, k):
                m, p, c, b = ROUND * j + k, k // HEAD, k % T, k // T % 2
                pe.wait_ge(lo_done, m + 1)
                if c == 0 and past(m, 2 * T):
                    pe.wait_ge(summed, 2 * G * j + k // T - 1)
                for q in range(TG):
                    qq = slice(q * P, (q + 1) * P)
                    pe.matmul(out[b][:, q, 0:2 * UP + 1], lhsT=p_hi[k % NB][:, qq], rhs=v[p][:, c, 0:2 * UP + 1],
                              start=c == 0 and q % 2 == 0, stop=False, skip_group_check=True)
                    last = pe.matmul(out[b][:, q, UP:2 * UP + 1], lhsT=p_lo[k % NB][:, qq], rhs=v[p][:, c, UP:2 * UP + 1],
                                     start=False, stop=c == T - 1, skip_group_check=True)
                last.then_inc(weighed, 1)

            def step(j, k):
                scores(j, k)
                next_maxima(j, k)
                back(j, k, LAG, weigh)

            rounds(pe, step)
            for k in range(ROUND - LAG, ROUND):
                weigh(ROUNDS - 1, k)

        @block.scalar
        def _(act):
            def low_sum(j, n):
                act.wait_ge(weighed, ROUND * j + T * (n + 1))
                if n >= 2 or past(j, 1):
                    act.wait_ge(summed, 2 * G * j + n - 1)
                act.activation(v_low[n % 2][:, :, :], out[n % 2][:, :, 0:UP], ACT.Copy).then_inc(low_out, 1)

            def step(j, k):
                m, b = ROUND * j + k, k % NB
                act.wait_ge(scored, m + 1)
                if past(m, PB):
                    act.wait_ge(lo_done, m - PB + 1)
                if past(m, NB):
                    act.wait_ge(weighed, m - NB + 1)
                act.activation(prob[k % PB][:, :], score[k % SB][:, :], ACT.Exp).then_inc(prob_done, 1)
                act.activation(p_hi[b][:, :], score[k % SB][:, :], ACT.Exp).then_inc(hi_done, 1)
                at_group(j, k, FIN, low_sum)

            rounds(act, step)
            low_sum(ROUNDS - 1, 2 * G - 1)

        @block.vector
        def _(dve):
            def finish(j, n):
                i, b = 2 * G * j + n, n % 2
                dve.wait_ge(low_out, i + 1)
                if n >= 2 or past(j, 1):
                    dve.wait_ge(divided, i - 1)
                dve.reciprocal(inv[b][:, :], out[b][:, :, 2 * UP]).then_inc(inverted, 1)
                dve.tensor_tensor(total[b][:, :, :], out[b][:, :, UP:2 * UP], v_low[b][:, :, :], ALU.add).then_inc(summed, 1)
                dve.wait_ge(inverted, i + 1)
                dve.wait_ge(summed, i + 1)
                g, h = n % G, 2 * j + n // G
                dve.tensor_tensor(heads[:, g * TG:(g + 1) * TG, ds(h * UP, UP)], total[b][:, :, :],
                                  inv[b][:, :].unsqueeze(2).to_broadcast([P, TG, UP]), ALU.mult).then_inc(divided, 1)

            def cut(j, n):
                i = 2 * G * j + n
                dve.wait_ge(reduced, T * (i + 1))
                dve.tensor_reduce(peak[:, :], part[n % 2][:, :, :], AXF, ALU.max).then_inc(peaked, 1)
                dve.wait_ge(peaked, i + 1)
                if n or past(j, 1):
                    dve.wait_ge(turned, i)
                dve.tensor_scalar(negated[:, :], peak[:, :], -1.0, None, ALU.mult).then_inc(put, 1)

            def round_row(j, n):
                i = 2 * G * j + n
                dve.wait_ge(turned, i + 1)
                if n or past(j, 1):
                    dve.wait_ge(moved, 16 * i)
                dve.tensor_copy(rows[:, :], probe[0:TG, 0:P]).then_inc(rounded, 1)

            def low(j, k):
                m, b = ROUND * j + k, k % NB
                dve.wait_ge(prob_done, m + 1)
                dve.wait_ge(hi_done, m + 1)
                dve.tensor_tensor(p_lo[b][:, :], prob[k % PB][:, :], p_hi[b][:, :], ALU.subtract).then_inc(lo_done, 1)

            def step(j, k):
                m, c = ROUND * j + k, k % T
                at_group(j, k, 0, cut)
                at_group(j, k, CUT, round_row)
                dve.wait_ge(probed, m + 1)
                dve.tensor_reduce(part[k // T % 2][:, c // G, c % G:c % G + 1], probe[:, :], AXF, ALU.max).then_inc(reduced, 1)
                back(j, k, 1, low)
                at_group(j, k, FIN, finish)

            rounds(dve, step)
            low(ROUNDS - 1, ROUND - 1)
            finish(ROUNDS - 1, 2 * G - 1)

        @block.sync
        def _(sp):
            for n in range(HEADS * G + 1):
                h, g = n // G, n % G
                if g == 0 and h < HEADS:
                    if h:
                        sp.wait_ge(weighed, HEAD * h)
                    if h + 1 < HEADS:
                        load_head(sp, h + 1, qk[(h + 1) % 2], v[(h + 1) % 2], qk_dram, v_dram, loaded[(h + 1) % 2])
                    if h + 2 < HEADS:
                        load_probe(sp, h + 2, probe_qk[h % 2], qk_dram, probe_loaded[h % 2])
                    elif h + 2 == HEADS:
                        sp.nop().then_inc(probe_loaded[h % 2], 16)
                if n == 0:
                    load_experts(sp, a, raw, raw_loaded)
                elif n < HEADS * G:
                    sp.wait_ge(rounded, n)
                    if n <= HEADS * G - G:
                        sp.dma_start(qk[((n - 1) // G + 1) % 2][QK:QK + 1, Q_HI, (n - 1) % G * GN:((n - 1) % G + 1) * GN]
                                     .rearrange("o (t j) -> o t j", j=P), rows[:, :]).then_inc(moved, 16)
                    else:
                        sp.nop().then_inc(moved, 16)
            sp.wait_ge(raw_loaded, 16 * RAW_LOADS)


def project_out(nc, oT, W_o, res):
    NB, K = 4, HEADS * UP // P
    with ExitStack() as ctx:
        s = Scope(nc, ctx, "wo_")
        prod = [s.ps(f"prod{i}", [P, 512]) for i in range(NB)]
        made, added = s.sem("made"), s.sem("added")
        block = ctx.enter_context(nc.Block())

        @block.tensor
        def _(pe):
            def tile(t, p):
                if past(t, NB):
                    pe.wait_ge(added, t - NB + 1)
                for k in range(K):
                    last = matmul3(pe, prod[p][:, 0:D], oT[0][:, k, ds(t * P, P)], oT[1][:, k, ds(t * P, P)],
                                   W_o[0][:, k, :], W_o[1][:, k, :], k == 0, k == K - 1)
                last.then_inc(made, 1)

            each(pe, T, NB, tile)

        @block.vector
        def _(dve):
            def tile(t, p):
                dve.wait_ge(made, t + 1)
                dve.scalar_tensor_tensor(res[:, ds(t, 1), :], prod[p][:, 0:D].unsqueeze(1), UNWS, res[:, ds(t, 1), :],
                                         ALU.mult, ALU.add).then_inc(added, 1)

            each(dve, T, NB, tile)


def l1_attention(nc, a, x, res, ident, raw, W_o, Wg):
    qk_dram = nc.dram_tensor("qk_dram", (HEADS, QK, 4, N), F16, kind="Internal").ap()
    v_dram = nc.dram_tensor("v_dram", (HEADS, P, T, 2 * UP + 2), F16, kind="Internal").ap()
    col = lambda ap: ap.rearrange("(k p) -> p k", p=P)
    rows = lambda ap: ap.rearrange("(k p) n -> p k n", p=P)
    normalize_and_turn(nc, "a1n_", ident, x, D, "layer", None, None, tok=res)
    with ExitStack() as ctx:
        s = Scope(nc, ctx, "a1_")
        cqT = s.sb("cqT_hi", [P, 1, N], F16), s.sb("cqT_lo", [P, 1, N], F16)
        ckvT = s.sb("ckvT_hi", [P, 1, N], F16), s.sb("ckvT_lo", [P, 1, N], F16)
        cos, sin, k_rope = (s.sb(n, [P, T, ROPE]) for n in ("cos", "sin", "k_rope"))
        W_uq = s.sb("uq_hi", [P, 1, HEADS * QK], F16), s.sb("uq_lo", [P, 1, HEADS * QK], F16)
        W_ukv = s.sb("ukv_hi", [P, 1, HEADS * 2 * UP], F16), s.sb("ukv_lo", [P, 1, HEADS * 2 * UP], F16)
        with ExitStack() as early:
            s = Scope(nc, early, "a1e_")
            xT = s.sb("xT_hi", [P, KD, N], F16), s.sb("xT_lo", [P, KD, N], F16)
            c_q, c_kv = s.sb("c_q", [P, T, DQ]), s.sb("c_kv", [P, T, DKV])
            W = s.sb("W_hi", [P, KD, DQ + DKV + ROPE], F16), s.sb("W_lo", [P, KD, DQ + DKV + ROPE], F16)
            dq, dkv = slice(0, DQ), slice(DQ, DQ + DKV + ROPE)
            with ExitStack() as stages:
                both = Together(nc, stages)
                normalize_and_turn(nc, "a1r_", ident, res, D, "rms", *xT, together=both)
                split_weights(nc, "a1w_", [
                    (rows(a["L1_ffn_w_dq"]), col(a["L1_ffn_w_in_norm"]), W[0][:, :, dq], W[1][:, :, dq]),
                    (rows(a["L1_ffn_w_dkv"]), col(a["L1_ffn_w_in_norm"]), W[0][:, :, dkv], W[1][:, :, dkv]),
                    (rows(a["L1_ffn_w_uq"]), col(a["L1_ffn_w_qnorm"]), W_uq[0][:, :, :], W_uq[1][:, :, :]),
                    (rows(a["L1_ffn_w_ukv"]), col(a["L1_ffn_w_kvnorm"]), W_ukv[0][:, :, :], W_ukv[1][:, :, :]),
                    (rows(a["L1_ffn_w_o"]), None, W_o[0][:, :, :], W_o[1][:, :, :]),
                    (rows(a["L1_ffn_w_gate"]), col(a["L1_ffn_w_post_norm"]), Wg[0][:, :, :], Wg[1][:, :, :])], both)
            latent_project(nc, a, xT, W[0], W[1], c_q, c_kv, k_rope, cos, sin)
            with ExitStack() as stages:
                both = Together(nc, stages)
                normalize_and_turn(nc, "a1q_", ident, c_q, DQ, "rms", *cqT, together=both)
                normalize_and_turn(nc, "a1k_", ident, c_kv, DKV, "rms", *ckvT, together=both)
        s = Scope(nc, ctx, "a1h_")
        qT = s.sb("qT_hi", [P, HH, N], F16), s.sb("qT_lo", [P, HH, N], F16)
        kT = s.sb("kT_hi", [P, HH, N], F16), s.sb("kT_lo", [P, HH, N], F16)
        V = s.sb("V", [P, T, HH, 2 * UP + 2], F16)
        for n, first in enumerate(range(0, HEADS, HH)):
            uq, ukv = slice(first * QK, (first + HH) * QK), slice(first * 2 * UP, (first + HH) * 2 * UP)
            queries_keys_values(nc, f"qkv{n}_", ident, cqT, ckvT, [w[:, 0, uq] for w in W_uq], [w[:, 0, ukv] for w in W_ukv],
                                k_rope, cos, sin, qT, kT, V, qk_dram, v_dram, first)
    with ExitStack() as ctx:
        heads = Scope(nc, ctx, "a1_").sb("heads", [P, T, HEADS * UP])
        with ExitStack() as inner:
            s = Scope(nc, inner, "a1m_")
            qk = [s.sb(f"qk{i}", [P, 4, N], F16) for i in range(2)]
            probe_qk = [s.sb(f"probe_qk{i}", [P, 2, N], F16) for i in range(2)]
            v = [s.sb(f"v{i}", [P, T, 2 * UP + 2], F16) for i in range(2)]
            first_head_maxima(nc, ident, qk, v, probe_qk, qk_dram, v_dram)
            nc.disable_value_cache = True
            attention(nc, a, ident, qk, v, probe_qk, qk_dram, v_dram, heads, raw)
            nc.disable_value_cache = False
        s = Scope(nc, ctx, "a1o_")
        oT = s.sb("oT_hi", [P, HEADS * UP // P, N], F16), s.sb("oT_lo", [P, HEADS * UP // P, N], F16)
        normalize_and_turn(nc, "a1t_", ident, heads, HEADS * UP, None, *oT)
        project_out(nc, oT, W_o, res)


RAW_LOADS = 12


def load_experts(sp, a, raw, loaded):
    for j, (routed, shared) in enumerate((("r_wg", "sh_wg"), ("r_wu", "sh_wu"))):
        for k in range(KD):
            kk = slice(k * P, (k + 1) * P)
            sp.dma_start(raw[:, 2 * j + k, 0:L1_E, :], a["L1_ffn_" + routed][:, kk, :].rearrange("e p i -> p e i")).then_inc(loaded, 16)
            sp.dma_start(raw[:, 2 * j + k, L1_E, :], a["L1_ffn_" + shared][kk, :]).then_inc(loaded, 16)
    for k in range(KD):
        kk = slice(k * P, (k + 1) * P)
        sp.dma_start(raw[:, 4 + k, 0:L1_E, :], a["L1_ffn_r_wd"][:, :, kk].rearrange("e p i -> p e i")).then_inc(loaded, 16)
        sp.dma_start(raw[:, 4 + k, L1_E, :], a["L1_ffn_sh_wd"][:, kk]).then_inc(loaded, 16)


def l1_experts(nc, x, res, hT, raw, scale, w_hi, w_lo, comb):
    E = L1_E + 1
    LAG = 2
    with ExitStack() as ctx:
        s = Scope(nc, ctx, "e1_")
        gate_out = [s.sb(f"gate{i}", [P, GN]) for i in range(2)]
        mixed = [s.sb(f"mixed{i}", [P, GN]) for i in range(2)]
        hid = [(s.sb(f"hid_hi{i}", [P, GN], F16), s.sb(f"hid_lo{i}", [P, GN], F16)) for i in range(4)]
        up = [[s.ps(f"up{j}{i}", [P, GN]) for i in range(2)] for j in range(2)]
        down = [s.ps(f"down{i}", [P, 512]) for i in range(TG)]
        w_high, w_low, up_done, gated, mixed_done, hi_done, lo_done, down_done, added = (
            s.sem(n) for n in ("w_high", "w_low", "up", "gated", "mixed", "hi", "lo", "down", "added"))
        block = ctx.enter_context(nc.Block())
        WROWS = 6
        AHEAD = 2

        def all_experts(eng, expert, prepare):
            for e in range(AHEAD):
                prepare(e)

            def body(e, _):
                prepare(e + AHEAD)
                expert(e)

            each(eng, E - AHEAD, 1, body)
            for e in range(E - AHEAD, E):
                expert(e)

        def lagged(e, g, do):
            if g >= LAG:
                do(e, g - LAG)
            elif past(e, 1):
                do(e - 1, G + g - LAG)

        @block.tensor
        def _(pe):
            def project_down(e, g):
                u = G * e + g
                pe.wait_ge(lo_done, u + 1)
                for q in range(TG):
                    if past(u, 1):
                        pe.wait_ge(added, TG * (u - 1) + q + 1)
                    qq = slice(q * P, (q + 1) * P)
                    last = matmul3(pe, down[q][:, 0:D], hid[g][0][:, qq], hid[g][1][:, qq],
                                   w_hi[:, 4:6, ds(e, 1), :], w_lo[:, 4:6, ds(e, 1), :], True, True)
                    last.then_inc(down_done, 1)

            def expert(e):
                pe.wait_ge(w_low, WROWS * e + WROWS)
                for g in range(G):
                    u, gg = G * e + g, slice(g * GN, (g + 1) * GN)
                    if past(u, 2):
                        pe.wait_ge(mixed_done, u - 1)
                    for j in range(2):
                        for k in range(KD):
                            last = matmul3(pe, up[j][g % 2][:, :], w_hi[:, 2 * j + k, ds(e, 1), :], w_lo[:, 2 * j + k, ds(e, 1), :],
                                           hT[0][:, k, gg], hT[1][:, k, gg], k == 0, k == KD - 1)
                        last.then_inc(up_done, 1)
                    lagged(e, g, project_down)

            all_experts(pe, expert, lambda e: None)
            for g in range(G - LAG, G):
                project_down(E - 1, g)

        @block.scalar
        def _(act):
            def prepare(e):
                for r in range(WROWS):
                    act.activation(w_hi[:, r, ds(e, 1), :], raw[:, r, ds(e, 1), :], ACT.Copy,
                                   scale=scale[:, r % 2:r % 2 + 1] if r < 4 else WS).then_inc(w_high, 1)

            def expert(e):
                for g in range(G):
                    u, b = G * e + g, g % 2
                    act.wait_ge(up_done, 2 * u + 1)
                    if past(u, 2):
                        act.wait_ge(mixed_done, u - 1)
                    act.activation(gate_out[b][:, :], up[0][b][:, :], ACT.Silu, scale=UNWS).then_inc(gated, 1)
                    act.wait_ge(mixed_done, u + 1)
                    if past(u, 4):
                        act.wait_ge(down_done, TG * (u - 3))
                    act.activation(hid[g][0][:, :], mixed[b][:, :], ACT.Copy).then_inc(hi_done, 1)

            all_experts(act, expert, prepare)

        @block.vector
        def _(dve):
            def prepare(e):
                for r in range(WROWS):
                    dve.wait_ge(w_high, WROWS * e + r + 1)
                    dve.scalar_tensor_tensor(w_lo[:, r, ds(e, 1), :], raw[:, r, ds(e, 1), :],
                                             scale[:, r % 2:r % 2 + 1] if r < 4 else WS, w_hi[:, r, ds(e, 1), :],
                                             ALU.mult, ALU.subtract).then_inc(w_low, 1)

            def add(e, g):
                u = G * e + g
                for q in range(TG):
                    n = TG * u + q
                    dve.wait_ge(down_done, n + 1)
                    if past(u, 1):
                        dve.wait_ge(added, n - TG + 1)
                    dve.scalar_tensor_tensor(res[:, TG * g + q, :], down[q][:, 0:D], comb[:, TG * g + q, ds(e, 1)],
                                             res[:, TG * g + q, :], ALU.mult, ALU.add).then_inc(added, 1)

            def expert(e):
                for g in range(G):
                    u, b = G * e + g, g % 2
                    dve.wait_ge(gated, u + 1)
                    dve.wait_ge(up_done, 2 * u + 2)
                    if past(u, 2):
                        dve.wait_ge(hi_done, u - 1)
                        dve.wait_ge(lo_done, u - 1)
                    dve.scalar_tensor_tensor(mixed[b][:, :], up[1][b][:, :], UNWS, gate_out[b][:, :], ALU.mult,
                                             ALU.mult).then_inc(mixed_done, 1)
                    dve.wait_ge(hi_done, u + 1)
                    dve.tensor_tensor(hid[g][1][:, :], mixed[b][:, :], hid[g][0][:, :], ALU.subtract).then_inc(lo_done, 1)
                    lagged(e, g, add)

            all_experts(dve, expert, prepare)
            for g in range(G - LAG, G):
                add(E - 1, g)
            for t in range(T):
                dve.wait_ge(added, TG * (G * (E - 1)) + t + 1)
                dve.tensor_tensor(x[:, t, :], x[:, t, :], res[:, t, :], ALU.add)


def prepare_scale(nc, src, scale, shared, together):
    s = Scope(nc, together.ctx, "sc_")
    loaded, steps = s.sem("loaded"), s.sem("steps")
    block = together.block

    @block.sync
    def _(sp):
        with nc.allow_non_contiguous_dma(reason="a short column of norm weights"):
            sp.dma_start(scale[:, :], src).then_inc(loaded, 16)

    @block.vector
    def _(dve):
        dve.memset(shared, UNWS)
        dve.wait_ge(loaded, 16)
        dve.tensor_scalar(scale[:, :], scale[:, :], WS, None, ALU.mult)


def l1_moe(nc, a, x, res, ident, raw, Wg):
    with ExitStack() as ctx:
        s = Scope(nc, ctx, "m1_")
        w_hi, w_lo = s.sb("w_hi", [P, 6, L1_E + 1, P], F16), s.sb("w_lo", [P, 6, L1_E + 1, P], F16)
        hT = s.sb("hT_hi", [P, KD, N], F16), s.sb("hT_lo", [P, KD, N], F16)
        scale = s.sb("scale", [P, KD])
        comb = s.sb("comb", [P, T, L1_E + 1])
        norm = a["L1_ffn_w_post_norm"].rearrange("(k p) -> p k", p=P)
        with ExitStack() as stages:
            both = Together(nc, stages)
            normalize_and_turn(nc, "m1n_", ident, res, D, "rms", *hT, together=both)
            prepare_scale(nc, norm, scale, comb[:, :, L1_E:L1_E + 1], both)
        route(nc, "m1r_", ident, L1_E, L1_K, hT, Wg, None, comb[:, :, 0:L1_E])
        l1_experts(nc, x, res, hT, raw, scale, w_hi, w_lo, comb)


def l1_ffn(nc, a, x, ident):
    with ExitStack() as ctx:
        s = Scope(nc, ctx, "l1_")
        res = s.sb("res", [P, T, D])
        W_o = s.sb("W_o_hi", [P, HEADS * UP // P, D], F16), s.sb("W_o_lo", [P, HEADS * UP // P, D], F16)
        Wg = s.sb("Wg_hi", [P, KD, L1_E], F16), s.sb("Wg_lo", [P, KD, L1_E], F16)
        raw = s.sb("raw", [P, 6, L1_E + 1, P])
        l1_attention(nc, a, x, res, ident, raw, W_o, Wg)
        recycle_semaphores(nc)
        l1_moe(nc, a, x, res, ident, raw, Wg)


def load_or_store(nc, prefix, out, in_):
    with ExitStack() as ctx:
        done = Scope(nc, ctx, prefix).sem("done")
        block = ctx.enter_context(nc.Block())

        @block.sync
        def _(sp):
            sp.dma_start(out, in_).then_inc(done, 16)
            sp.wait_ge(done, 16)


def build(nc, a, out):
    Scope.used.clear()
    with ExitStack() as ctx:
        s = Scope(nc, ctx, "")
        ident, ident16, ones = s.sb("ident", [P, P]), s.sb("ident16", [P, P], F16), s.sb("ones", [P, P])
        x = s.sb("x", [P, T, D])
        h_slots = nc.dram_tensor("h_slots", (NT * ST, 2 * D), F16, kind="Internal").ap()
        y_slots = nc.dram_tensor("y_slots", (NT * ST, D), F32, kind="Internal").ap()
        tiles = lambda ap: ap.rearrange("(t p) d -> p t d", p=P)
        make_identities(nc, ident, ident16, ones)
        with ExitStack() as adj_ctx:
            s2 = Scope(nc, adj_ctx, "")
            slots, weights = s2.sb("slots", [P, L0_K, T], I32), s2.sb("weights", [P, L0_K, T])
            adjT, diag = s2.sb("adjT", [P, T, N], F16), s2.sb("diag", [P, T, P], F16)
            transpose_adjacency(nc, a["adj"], ident16, adjT, diag, x[:, :, :], tiles(a["x"]))
            l0_gnn(nc, a, x, ident, ident16, ones, adjT, h_slots)
            recycle_semaphores(nc)
            l0_ffn(nc, a, x, ident, ident16, ones, slots, weights, y_slots, h_slots); recycle_semaphores(nc); l1_gnn(nc, a, x, ident, adjT, diag, slots, weights, y_slots)
            recycle_semaphores(nc)
        l1_ffn(nc, a, x, ident)
        load_or_store(nc, "out_", tiles(out), x[:, :, :])


INPUTS = ["x", "adj", "L0_gnn_W", "L0_ffn_Wg", "L0_ffn_bg", "L0_ffn_W1", "L0_ffn_b1", "L0_ffn_W2", "L0_ffn_b2",
          "L1_gnn_W_nb", "L1_gnn_b_nb", "L1_gnn_W_line", "L1_gnn_b_line", "L1_ffn_w_in_norm", "L1_ffn_w_dq",
          "L1_ffn_w_qnorm", "L1_ffn_w_uq", "L1_ffn_w_dkv", "L1_ffn_w_kvnorm", "L1_ffn_w_ukv", "L1_ffn_w_o",
          "L1_ffn_w_post_norm", "L1_ffn_w_gate", "L1_ffn_sh_wg", "L1_ffn_sh_wu", "L1_ffn_sh_wd", "L1_ffn_r_wg",
          "L1_ffn_r_wu", "L1_ffn_r_wd"]


def kernel(**inputs):
    import numpy as np
    import concourse.bacc as bacc
    from concourse.bass_utils import run_bass_kernel_spmd

    nc = bacc.Bacc("TRN2", target_bir_lowering=False, num_devices=1)
    arrays = {name: np.ascontiguousarray(inputs[name]) for name in INPUTS}
    freq = (np.float32(1.0) / np.float32(10000.0) ** (np.arange(0, ROPE, 2, dtype=np.float32) / np.float32(ROPE))).astype(np.float32)
    angle = np.outer(np.arange(N, dtype=np.float32), freq).astype(np.float32)
    arrays["rope_cos"] = np.concatenate([np.cos(angle), np.cos(angle)], axis=-1).astype(np.float32)
    arrays["rope_sin"] = np.concatenate([-np.sin(angle), np.sin(angle)], axis=-1).astype(np.float32)
    args = {name: nc.dram_tensor("in_" + name, v.shape, mybir.dt.from_np(v.dtype), kind="ExternalInput").ap()
            for name, v in arrays.items()}
    out = nc.dram_tensor("out_0", (N, D), F32, kind="ExternalOutput").ap()
    build(nc, args, out)
    r = run_bass_kernel_spmd(nc, [{"in_" + name: v for name, v in arrays.items()}], core_ids=[0])
    return r.results[0]["out_0"]
```
